# Optimizing a Trainium2 kernel written in Bass

```python
import numpy as np
import jax
import jax.numpy as jnp

def _softmax(x, axis=-1):
    return jax.nn.softmax(x, axis=axis)

def _gelu(x):
    return jax.nn.gelu(x, approximate=True)

def _silu(x):
    return jax.nn.silu(x)

def _sigmoid(x):
    return jax.nn.sigmoid(x)

def _layernorm(x, axis=-1, eps=1e-05):
    m = jnp.mean(x, axis=axis, keepdims=True)
    v = jnp.var(x, axis=axis, keepdims=True)
    return (x - m) / jnp.sqrt(v + eps)

def _scatter_add(tgt, idx, src, axis=0):
    return tgt.at[idx].add(src)

def _segment_sum(src, seg, n):
    return jax.ops.segment_sum(src, seg, n)
kernel_name = 'mk_rec_standalone_d1_rec_r8_442ca6'

def setup_inputs(seed: int=0):
    np.random.seed(seed)
    _w = jnp.asarray

    def _rec_inputs():
        import jax
        import jax.numpy as jnp
        _rk = jax.random.key(seed)
        r_input_ids = jnp.stack([jax.random.randint(jax.random.fold_in(jax.random.fold_in(_rk, 1), 0), (2048,), 87, 199707, jnp.int32), jax.random.randint(jax.random.fold_in(jax.random.fold_in(_rk, 1), 1), (2048,), 919, 199903, jnp.int32), jax.random.randint(jax.random.fold_in(jax.random.fold_in(_rk, 1), 2), (2048,), 158, 199806, jnp.int32), jax.random.randint(jax.random.fold_in(jax.random.fold_in(_rk, 1), 3), (2048,), 1, 199971, jnp.int32), jax.random.randint(jax.random.fold_in(jax.random.fold_in(_rk, 1), 4), (2048,), 539, 199213, jnp.int32), jax.random.randint(jax.random.fold_in(jax.random.fold_in(_rk, 1), 5), (2048,), 131, 199420, jnp.int32), jax.random.randint(jax.random.fold_in(jax.random.fold_in(_rk, 1), 6), (2048,), 81, 199970, jnp.int32), jax.random.randint(jax.random.fold_in(jax.random.fold_in(_rk, 1), 7), (2048,), 45, 199853, jnp.int32), jax.random.randint(jax.random.fold_in(jax.random.fold_in(_rk, 1), 8), (2048,), 77, 199756, jnp.int32), jax.random.randint(jax.random.fold_in(jax.random.fold_in(_rk, 1), 9), (2048,), 126, 24976, jnp.int32), jax.random.randint(jax.random.fold_in(jax.random.fold_in(_rk, 1), 10), (2048,), 149, 24964, jnp.int32), jax.random.randint(jax.random.fold_in(jax.random.fold_in(_rk, 1), 11), (2048,), 51, 198661, jnp.int32), jax.random.randint(jax.random.fold_in(jax.random.fold_in(_rk, 1), 12), (2048,), 430, 198581, jnp.int32), jax.random.randint(jax.random.fold_in(jax.random.fold_in(_rk, 1), 13), (2048,), 47, 199740, jnp.int32), jax.random.randint(jax.random.fold_in(jax.random.fold_in(_rk, 1), 14), (2048,), 244, 199922, jnp.int32), jax.random.randint(jax.random.fold_in(jax.random.fold_in(_rk, 1), 15), (2048,), 633, 199689, jnp.int32), jax.random.randint(jax.random.fold_in(jax.random.fold_in(_rk, 1), 16), (2048,), 165, 199301, jnp.int32), jax.random.randint(jax.random.fold_in(jax.random.fold_in(_rk, 1), 17), (2048,), 750, 199817, jnp.int32), jax.random.randint(jax.random.fold_in(jax.random.fold_in(_rk, 1), 18), (2048,), 76, 199922, jnp.int32), jax.random.randint(jax.random.fold_in(jax.random.fold_in(_rk, 1), 19), (2048,), 98, 199990, jnp.int32), jax.random.randint(jax.random.fold_in(jax.random.fold_in(_rk, 1), 20), (2048,), 815, 199893, jnp.int32), jax.random.randint(jax.random.fold_in(jax.random.fold_in(_rk, 1), 21), (2048,), 764, 199263, jnp.int32), jax.random.randint(jax.random.fold_in(jax.random.fold_in(_rk, 1), 22), (2048,), 180, 198859, jnp.int32), jax.random.randint(jax.random.fold_in(jax.random.fold_in(_rk, 1), 23), (2048,), 509, 199510, jnp.int32), jax.random.randint(jax.random.fold_in(jax.random.fold_in(_rk, 1), 24), (2048,), 799, 199907, jnp.int32), jax.random.randint(jax.random.fold_in(jax.random.fold_in(_rk, 1), 25), (2048,), 332, 199638, jnp.int32), jax.random.randint(jax.random.fold_in(jax.random.fold_in(_rk, 1), 26), (2048,), 13, 199633, jnp.int32), jax.random.randint(jax.random.fold_in(jax.random.fold_in(_rk, 1), 27), (2048,), 1124, 199709, jnp.int32), jax.random.randint(jax.random.fold_in(jax.random.fold_in(_rk, 1), 28), (2048,), 352, 24992, jnp.int32), jax.random.randint(jax.random.fold_in(jax.random.fold_in(_rk, 1), 29), (2048,), 1229, 199547, jnp.int32), jax.random.randint(jax.random.fold_in(jax.random.fold_in(_rk, 1), 30), (2048,), 62, 199806, jnp.int32), jax.random.randint(jax.random.fold_in(jax.random.fold_in(_rk, 1), 31), (2048,), 370, 199625, jnp.int32), jax.random.randint(jax.random.fold_in(jax.random.fold_in(_rk, 1), 32), (2048,), 413, 199070, jnp.int32), jax.random.randint(jax.random.fold_in(jax.random.fold_in(_rk, 1), 33), (2048,), 451, 199750, jnp.int32), jax.random.randint(jax.random.fold_in(jax.random.fold_in(_rk, 1), 34), (2048,), 145, 199693, jnp.int32), jax.random.randint(jax.random.fold_in(jax.random.fold_in(_rk, 1), 35), (2048,), 60, 199284, jnp.int32), jax.random.randint(jax.random.fold_in(jax.random.fold_in(_rk, 1), 36), (2048,), 177, 199809, jnp.int32), jax.random.randint(jax.random.fold_in(jax.random.fold_in(_rk, 1), 37), (2048,), 944, 199566, jnp.int32), jax.random.randint(jax.random.fold_in(jax.random.fold_in(_rk, 1), 38), (2048,), 233, 24898, jnp.int32), jax.random.randint(jax.random.fold_in(jax.random.fold_in(_rk, 1), 39), (2048,), 361, 199887, jnp.int32), jax.random.randint(jax.random.fold_in(jax.random.fold_in(_rk, 1), 40), (2048,), 355, 199964, jnp.int32), jax.random.randint(jax.random.fold_in(jax.random.fold_in(_rk, 1), 41), (2048,), 301, 199862, jnp.int32), jax.random.randint(jax.random.fold_in(jax.random.fold_in(_rk, 1), 42), (2048,), 33, 24998, jnp.int32), jax.random.randint(jax.random.fold_in(jax.random.fold_in(_rk, 1), 43), (2048,), 42, 199836, jnp.int32), jax.random.randint(jax.random.fold_in(jax.random.fold_in(_rk, 1), 44), (2048,), 151, 24933, jnp.int32), jax.random.randint(jax.random.fold_in(jax.random.fold_in(_rk, 1), 45), (2048,), 116, 199163, jnp.int32), jax.random.randint(jax.random.fold_in(jax.random.fold_in(_rk, 1), 46), (2048,), 448, 199962, jnp.int32), jax.random.randint(jax.random.fold_in(jax.random.fold_in(_rk, 1), 47), (2048,), 72, 199690, jnp.int32), jax.random.randint(jax.random.fold_in(jax.random.fold_in(_rk, 1), 48), (2048,), 475, 199514, jnp.int32), jax.random.randint(jax.random.fold_in(jax.random.fold_in(_rk, 1), 49), (2048,), 72, 199500, jnp.int32), jax.random.randint(jax.random.fold_in(jax.random.fold_in(_rk, 1), 50), (2048,), 8, 199990, jnp.int32), jax.random.randint(jax.random.fold_in(jax.random.fold_in(_rk, 1), 51), (2048,), 483, 199844, jnp.int32), jax.random.randint(jax.random.fold_in(jax.random.fold_in(_rk, 1), 52), (2048,), 16, 24997, jnp.int32), jax.random.randint(jax.random.fold_in(jax.random.fold_in(_rk, 1), 53), (2048,), 695, 24942, jnp.int32), jax.random.randint(jax.random.fold_in(jax.random.fold_in(_rk, 1), 54), (2048,), 441, 199915, jnp.int32), jax.random.randint(jax.random.fold_in(jax.random.fold_in(_rk, 1), 55), (2048,), 1838, 199987, jnp.int32), jax.random.randint(jax.random.fold_in(jax.random.fold_in(_rk, 1), 56), (2048,), 787, 199580, jnp.int32), jax.random.randint(jax.random.fold_in(jax.random.fold_in(_rk, 1), 57), (2048,), 149, 199670, jnp.int32), jax.random.randint(jax.random.fold_in(jax.random.fold_in(_rk, 1), 58), (2048,), 336, 198646, jnp.int32), jax.random.randint(jax.random.fold_in(jax.random.fold_in(_rk, 1), 59), (2048,), 94, 199887, jnp.int32), jax.random.randint(jax.random.fold_in(jax.random.fold_in(_rk, 1), 60), (2048,), 30, 199209, jnp.int32), jax.random.randint(jax.random.fold_in(jax.random.fold_in(_rk, 1), 61), (2048,), 69, 199815, jnp.int32), jax.random.randint(jax.random.fold_in(jax.random.fold_in(_rk, 1), 62), (2048,), 681, 199279, jnp.int32), jax.random.randint(jax.random.fold_in(jax.random.fold_in(_rk, 1), 63), (2048,), 320, 199181, jnp.int32)], axis=1)
        return r_input_ids
    r_input_ids = _rec_inputs()

    def _L0_rec_setup():
        import jax, jax.numpy as jnp
        import numpy as np
        NUM_ITEMS = 25000
        B = 512
        S = 64
        D = 64
        H = 1
        NBLOCKS = 2
        EPS = 0.001
        NEG = -2.0 ** 32 + 1.0

        def _layernorm(x, g, b):
            mu = jnp.mean(x, -1, keepdims=True)
            var = jnp.var(x, -1, keepdims=True)
            return (x - mu) * jax.lax.rsqrt(var + EPS) * g + b

        def _mha(queries, keys, Wq, bq, Wk, bk, Wv, bv):
            Bq, Sq, Dm = queries.shape
            dh = Dm // H

            def split(x):
                return x.reshape(Bq, Sq, H, dh).transpose(0, 2, 1, 3)
            Q = split(queries @ Wq + bq)
            K = split(keys @ Wk + bk)
            V = split(keys @ Wv + bv)
            scores = jnp.einsum('bhqd,bhkd->bhqk', Q, K) / jnp.sqrt(jnp.float32(dh))
            key_mask = jnp.sign(jnp.abs(jnp.sum(keys, -1)))
            scores = jnp.where(key_mask[:, None, None, :] == 0, NEG, scores)
            causal = jnp.tril(jnp.ones((Sq, Sq), jnp.float32))
            scores = jnp.where(causal[None, None] == 0, NEG, scores)
            attn = jax.nn.softmax(scores, axis=-1)
            query_mask = jnp.sign(jnp.abs(jnp.sum(queries, -1)))
            attn = attn * query_mask[:, None, :, None]
            out = jnp.einsum('bhqk,bhkd->bhqd', attn, V)
            return out.transpose(0, 2, 1, 3).reshape(Bq, Sq, Dm)
        key = jax.random.key(seed)
        ks = jax.random.split(key, 12)

        def nrm(k, shape, s=0.02):
            return jax.random.normal(k, shape, dtype=jnp.float32) * s
        return {'input_ids': jax.random.randint(ks[0], (B, S), 0, NUM_ITEMS + 1), 'item_emb': nrm(ks[1], (NUM_ITEMS + 1, D)), 'pos_emb': nrm(ks[2], (S, D)), 'ln1_g': jnp.ones((NBLOCKS, D), jnp.float32), 'ln1_b': jnp.zeros((NBLOCKS, D), jnp.float32), 'Wq': nrm(ks[3], (NBLOCKS, D, D)), 'bq': jnp.zeros((NBLOCKS, D), jnp.float32), 'Wk': nrm(ks[4], (NBLOCKS, D, D)), 'bk': jnp.zeros((NBLOCKS, D), jnp.float32), 'Wv': nrm(ks[5], (NBLOCKS, D, D)), 'bv': jnp.zeros((NBLOCKS, D), jnp.float32), 'ln2_g': jnp.ones((NBLOCKS, D), jnp.float32), 'ln2_b': jnp.zeros((NBLOCKS, D), jnp.float32), 'W1': nrm(ks[6], (NBLOCKS, D, D)), 'b1': jnp.zeros((NBLOCKS, D), jnp.float32), 'W2': nrm(ks[7], (NBLOCKS, D, D)), 'b2': jnp.zeros((NBLOCKS, D), jnp.float32), 'lnf_g': jnp.ones((D,), jnp.float32), 'lnf_b': jnp.zeros((D,), jnp.float32), 'out_item_emb': nrm(ks[8], (NUM_ITEMS, D))}
    _L0_rec_all = _L0_rec_setup()
    _L0_rec_in = {k: v for k, v in _L0_rec_all.items() if k in ('item_emb', 'pos_emb', 'ln1_g', 'ln1_b', 'Wq', 'bq', 'Wk', 'bk', 'Wv', 'bv', 'ln2_g', 'ln2_b', 'W1', 'b1', 'W2', 'b2', 'lnf_g', 'lnf_b', 'out_item_emb')}
    del _L0_rec_all
    return {'r_input_ids': r_input_ids, 'L0_rec_item_emb': _L0_rec_in['item_emb'], 'L0_rec_pos_emb': _L0_rec_in['pos_emb'], 'L0_rec_ln1_g': _L0_rec_in['ln1_g'], 'L0_rec_ln1_b': _L0_rec_in['ln1_b'], 'L0_rec_Wq': _L0_rec_in['Wq'], 'L0_rec_bq': _L0_rec_in['bq'], 'L0_rec_Wk': _L0_rec_in['Wk'], 'L0_rec_bk': _L0_rec_in['bk'], 'L0_rec_Wv': _L0_rec_in['Wv'], 'L0_rec_bv': _L0_rec_in['bv'], 'L0_rec_ln2_g': _L0_rec_in['ln2_g'], 'L0_rec_ln2_b': _L0_rec_in['ln2_b'], 'L0_rec_W1': _L0_rec_in['W1'], 'L0_rec_b1': _L0_rec_in['b1'], 'L0_rec_W2': _L0_rec_in['W2'], 'L0_rec_b2': _L0_rec_in['b2'], 'L0_rec_lnf_g': _L0_rec_in['lnf_g'], 'L0_rec_lnf_b': _L0_rec_in['lnf_b'], 'L0_rec_out_item_emb': _L0_rec_in['out_item_emb']}

def reference(r_input_ids, L0_rec_item_emb, L0_rec_pos_emb, L0_rec_ln1_g, L0_rec_ln1_b, L0_rec_Wq, L0_rec_bq, L0_rec_Wk, L0_rec_bk, L0_rec_Wv, L0_rec_bv, L0_rec_ln2_g, L0_rec_ln2_b, L0_rec_W1, L0_rec_b1, L0_rec_W2, L0_rec_b2, L0_rec_lnf_g, L0_rec_lnf_b, L0_rec_out_item_emb):
    import jax
    import jax.numpy as jnp

    def _L0_rec_ref(input_ids, item_emb, pos_emb, ln1_g, ln1_b, Wq, bq, Wk, bk, Wv, bv, ln2_g, ln2_b, W1, b1, W2, b2, lnf_g, lnf_b, out_item_emb):
        import jax, jax.numpy as jnp
        import numpy as np
        NUM_ITEMS = 25000
        B = 512
        S = 64
        D = 64
        H = 1
        NBLOCKS = 2
        EPS = 0.001
        NEG = -2.0 ** 32 + 1.0

        def _layernorm(x, g, b):
            mu = jnp.mean(x, -1, keepdims=True)
            var = jnp.var(x, -1, keepdims=True)
            return (x - mu) * jax.lax.rsqrt(var + EPS) * g + b

        def _mha(queries, keys, Wq, bq, Wk, bk, Wv, bv):
            Bq, Sq, Dm = queries.shape
            dh = Dm // H

            def split(x):
                return x.reshape(Bq, Sq, H, dh).transpose(0, 2, 1, 3)
            Q = split(queries @ Wq + bq)
            K = split(keys @ Wk + bk)
            V = split(keys @ Wv + bv)
            scores = jnp.einsum('bhqd,bhkd->bhqk', Q, K) / jnp.sqrt(jnp.float32(dh))
            key_mask = jnp.sign(jnp.abs(jnp.sum(keys, -1)))
            scores = jnp.where(key_mask[:, None, None, :] == 0, NEG, scores)
            causal = jnp.tril(jnp.ones((Sq, Sq), jnp.float32))
            scores = jnp.where(causal[None, None] == 0, NEG, scores)
            attn = jax.nn.softmax(scores, axis=-1)
            query_mask = jnp.sign(jnp.abs(jnp.sum(queries, -1)))
            attn = attn * query_mask[:, None, :, None]
            out = jnp.einsum('bhqk,bhkd->bhqd', attn, V)
            return out.transpose(0, 2, 1, 3).reshape(Bq, Sq, Dm)
        mask = (input_ids != NUM_ITEMS).astype(jnp.float32)[..., None]
        seq = item_emb[input_ids] + pos_emb[None]
        seq = seq * mask
        for i in range(NBLOCKS):
            x = _layernorm(seq, ln1_g[i], ln1_b[i])
            q = x
            x = _mha(q, seq, Wq[i], bq[i], Wk[i], bk[i], Wv[i], bv[i])
            x = x + q
            x = _layernorm(x, ln2_g[i], ln2_b[i])
            res = x
            x = jax.nn.relu(x @ W1[i] + b1[i]) @ W2[i] + b2[i]
            x = x + res
            seq = x * mask
        seq_emb = _layernorm(seq, lnf_g, lnf_b)[:, -1, :]
        return seq_emb @ out_item_emb.T
    y = _L0_rec_ref(r_input_ids, L0_rec_item_emb, L0_rec_pos_emb, L0_rec_ln1_g, L0_rec_ln1_b, L0_rec_Wq, L0_rec_bq, L0_rec_Wk, L0_rec_bk, L0_rec_Wv, L0_rec_bv, L0_rec_ln2_g, L0_rec_ln2_b, L0_rec_W1, L0_rec_b1, L0_rec_W2, L0_rec_b2, L0_rec_lnf_g, L0_rec_lnf_b, L0_rec_out_item_emb)
    return y

_drawn_inputs = setup_inputs


def setup_inputs(seed=0):
    import zlib

    import numpy as np

    out = dict(_drawn_inputs(seed))
    spreads = {'L0_rec_ln1_g': (1.0, 0.2),
     'L0_rec_ln1_b': (0.0, 0.1),
     'L0_rec_bq': (0.0, 2.0),
     'L0_rec_bk': (0.0, 2.0),
     'L0_rec_bv': (0.0, 0.1),
     'L0_rec_ln2_g': (1.0, 0.2),
     'L0_rec_ln2_b': (0.0, 0.1),
     'L0_rec_b1': (0.0, 0.607),
     'L0_rec_b2': (0.0, 0.1),
     'L0_rec_lnf_g': (1.0, 0.2),
     'L0_rec_lnf_b': (0.0, 0.1)}
    factors = {'L0_rec_Wq': 8.0, 'L0_rec_Wk': 8.0, 'L0_rec_W1': 2.684}
    for name, (base, spread) in spreads.items():
        noise = np.random.default_rng([zlib.crc32(name.encode()), seed]).standard_normal(out[name].shape)
        drawn = base * np.exp(spread * noise) if base else spread * noise
        out[name] = jnp.asarray(drawn.astype(out[name].dtype))
    for name, factor in factors.items():
        out[name] = (out[name] * factor).astype(out[name].dtype)
    return out
```

```python
from contextlib import ExitStack

import concourse.bass as bass
from concourse import mybir

F32 = mybir.dt.float32
F32R = mybir.dt.float32r
BF16 = mybir.dt.bfloat16
I32 = mybir.dt.int32
ALU = mybir.AluOpType
ACT = mybir.ActivationFunctionType
AX = mybir.AxisListType.X

P = 128
LANES = 4
TILES = 8
PAIRS = TILES // 2
EPS = 1e-3
MASKED = -(2.0 ** 100)


class Steps:

    def __init__(self, sem, names):
        self.sem = sem
        self.per_pass = len(names)
        self.index = {name: i + 1 for i, name in enumerate(names)}
        assert len(self.index) == len(names)

    def at(self, n, *name):
        return n * self.per_pass + self.index[name]

    def start(self, n):
        return n * self.per_pass


def each(*names):
    return [(name, u) for name in names for u in range(LANES)]


def stats(k):
    return [(k + x,) for x in ("sum", "diff", "m2", "spread", "var64", "var")]


def newton(k):
    return [(k + x,) for x in ("nsq", "nhalf", "rstd")]


def row_norm(k):
    return [(k + "bn",)] + stats(k) + [(k + "mean",)] + newton(k) + [(k + "hat",), (k + "gain",), (k + "out",)]


def recommender(nc, ids, item_emb, pos_emb, wqT, wkT, wv, w1, w2, cols, rows, out_emb, const, out):
    B, S = ids.shape
    NI, D = item_emb.shape
    NO = out_emb.shape[0]
    MASK_ID = NI - 1
    assert S == 64 and D == 64 and B % P == 0
    BATCH = 16 * LANES
    PASSES = B // BATCH
    T = B * S // P
    GROUPS = B // P
    TQ = T // P if T >= P else 1
    TR = min(T, P)
    NSL = 500
    DSL = 5
    STORES = NO // (NSL * DSL)
    ER = 125
    EL = 4
    ELOADS = NO // (ER * EL)
    assert NO % (NSL * DSL) == 0 and NO % (ER * EL) == 0

    ctx = ExitStack()
    with ctx:
        def sem(name):
            return ctx.enter_context(nc.semaphore(name))

        hid_hi = ctx.enter_context(nc.sbuf_tensor("s_hid_hi", [P, B], F32R))
        hid_lo = ctx.enter_context(nc.sbuf_tensor("s_hid_lo", [P, B], F32R))
        ph1 = ctx.enter_context(ExitStack())

        def sb(name, shape, dt=F32):
            return ph1.enter_context(nc.sbuf_tensor("s_" + name, shape, dt))

        ident = sb("ident", [P, P])
        maskid = sb("maskid", [P, P], BF16)
        ones_b = sb("ones_b", [P, P], BF16)
        later = sb("later", [P, 512], BF16)
        ksel = sb("ksel", [P, 512], BF16)
        rsel = sb("rsel", [P, P], BF16)
        other = sb("other", [P, 512], BF16)
        abrow = sb("abrow", [P, P])
        ab01 = sb("ab01", [P, 2])
        cstage = sb("cstage", [P, 512])
        bd = {k: sb("bd_" + k, [P, P]) for k in ("m", "v", "w1", "w2")}
        gpair = sb("gpair", [P, 2])
        col = sb("col", [P, cols.shape[1]])
        row = sb("row", [P, rows.shape[0], D])
        wq_s = sb("wq_s", [D, 2, D])
        wk_s = sb("wk_s", [D, 2, 2 * D])
        wq_d = sb("wq_d", [D, 2, 2 * D])
        m2dup = sb("m2dup", [D, P])
        cbias = sb("cbias", [P, 2])
        small = sb("small", [D, 4, D])
        bv3 = sb("bv3", [P, 512], BF16)
        bvt = sb("bvt", [P, 4, D])
        bvb = sb("bvb", [P, 3, D], BF16)
        gsum = sb("gsum", [P, 2])
        eps = sb("eps", [P, 1])

        idx_all = sb("idx_all", [P, T], I32)
        kept_all = sb("kept_all", [P, T])
        last_i = sb("last_i", [P, PASSES], I32)
        last_all = sb("last_all", [P, PASSES])

        LN = range(LANES)
        X = [sb(f"XIN{u}", [P, TILES, D]) for u in LN]
        SEQ = [sb(f"SEQ{u}", [P, TILES, D]) for u in LN]
        XN = [sb(f"XN{u}", [P, TILES, D]) for u in LN]
        KT = [sb(f"KT{u}", [P, 512]) for u in LN]
        QT = [sb(f"QT{u}", [P, 512]) for u in LN]
        BLK = [sb(f"BLK{u}", [P, TILES, P]) for u in LN]
        V = [sb(f"V{u}", [P, TILES, D]) for u in LN]
        S2T = [sb(f"S2T{u}", [P, 512]) for u in LN]
        S2N = [sb(f"S2N{u}", [P, TILES, D]) for u in LN]
        idx_now = [sb(f"idx_now{u}", [P, TILES], I32) for u in LN]
        bn = sb("bn", [P, LANES, TILES, 6])
        st = {k: sb("st_" + k, [P, LANES, TILES]) for k in
              ("sum", "diff", "m2", "spread", "var64", "var", "ln", "r0", "nsq", "nhalf", "rstd",
               "max", "den", "rden", "rq", "qs", "qsr", "qtok", "qrow")}
        kflag = sb("kflag", [P, LANES, 32])
        kflagT = sb("kflagT", [P, P], BF16)

        XL = sb("XL", [P, D])
        XLM = sb("XLM", [P, D])
        last_now = sb("last_now", [P, 1])
        kept_now = sb("kept_now", [P, LANES * TILES])
        rbn = sb("rbn", [P, 6])
        rs = {k: sb("rs_" + k, [P, 1]) for k in
              ("sum", "diff", "m2", "spread", "var64", "var", "ln", "r0", "nsq", "nhalf", "rstd", "mean",
               "qsum", "qm", "max", "den", "rden", "ra", "rb")}
        rhat = sb("rhat", [P, D])
        rgain = sb("rgain", [P, D])
        Q2w = sb("Q2w", [P, P])
        Q2 = Q2w[:, 0:D]
        rT = sb("rT", [D, P])
        G2B = sb("G2B", [P, LANES, 32])
        idrow = sb("idrow", [P, 512], I32)
        idflag = sb("idflag", [P, 512])
        flag2 = sb("flag2", [P, 512], BF16)
        P2 = sb("P2", [P, 512])
        P2T = sb("P2T", [P, PAIRS, P])
        A2w = sb("A2w", [P, P])
        A2 = A2w[:, 0:D]
        X2a = sb("X2a", [P, D])
        X2 = sb("X2", [P, D])
        Y2w = sb("Y2w", [P, P])
        Y2 = Y2w[:, 0:D]
        Z2a = sb("Z2a", [P, D])
        Z2 = sb("Z2", [P, D])
        Z2m = sb("Z2m", [P, D])
        hfin = sb("hfin", [P, 2, D])

        pl = [ph1.enter_context(nc.psum_tensor(f"pl{u}", [P, 512], F32)) for u in LN]
        pr = ph1.enter_context(nc.psum_tensor("pr", [P, 512], F32))
        pr2 = ph1.enter_context(nc.psum_tensor("pr2", [P, 512], F32))
        pm = ph1.enter_context(nc.psum_tensor("pm", [P, 512], F32))
        pg = ph1.enter_context(nc.psum_tensor("pg", [P, 512], F32))

        loaded = sem("loaded")
        stage_in = sem("stage_in")
        set_dve = sem("set_dve")
        set_pe = sem("set_pe")
        set_act = sem("set_act")
        ready = sem("ready")
        prefilled = [sem(f"prefilled{u}") for u in LN]
        cleared = sem("cleared")
        idx_copied = sem("idx_copied")
        gathered = [sem(f"gathered{u}") for u in LN]
        rows_in = sem("rows_in")
        dve_lane = sem("dve_lane")
        act_lane = sem("act_lane")
        pe_lane = sem("pe_lane")
        dve_row = sem("dve_row")
        act_row = sem("act_row")
        pe_row = sem("pe_row")

        DL = Steps(dve_lane, each("seq", "bn1") + stats("1") + [("kflag",)] + each("cen1") + newton("1")
                   + each("hat1") + [("qs",), ("qsr",), ("qtok",)] + [("qrow", k) for k in range(4)]
                   + each("max", "shift", "den") + [("rden",), ("rq",)] + each("prob", "res1", "bn2")
                   + stats("2") + each("cen2") + newton("2") + each("hat2", "seq2"))
        AL = Steps(act_lane, each("keyT") + [("1ln",), ("1r0",), ("kflagT",)] + each("v", "qT", "gA", "gB", "exp", "pA", "pB")
                   + [("2ln",), ("2r0",)] + each("yT", "hT", "s2N"))
        PL = Steps(pe_lane, each("keyT") + [("kflagT",)] + each("v", "hatT", "g", "s", "pT", "pv", "xtok", "yT", "h", "o", "s2N"))
        DR = Steps(dve_row, [("now",), ("kept",), ("xlm",)] + row_norm("a") + [("qsum",), ("qm",), ("g2",), ("idflag",), ("flag2",), ("max",), ("shift",),
                   ("valid",), ("den",), ("rden",), ("ra",), ("rb",)] + [("p2T", k) for k in range(PAIRS)]
                   + [("a2a",), ("a2",), ("x2a",), ("x2",)] + row_norm("b") + [("z2a",), ("z2",), ("z2m",)]
                   + row_norm("c") + [("hi",), ("lo",)])
        AR = Steps(act_row, [("aln",), ("ar0",), ("qT",), ("exp",), ("a2T",), ("bln",), ("br0",), ("yT",), ("hT",), ("cln",), ("cr0",)])
        PR = Steps(pe_row, [("qT",), ("g2",), ("s2",), ("flag",), ("p2T",), ("a2",), ("a2T",), ("o2",), ("yT",), ("h",), ("z",), ("fT",)])
        ROWS_DMA = 16 * (2 * LANES + LANES)

        ids_tiles = ids.rearrange("b s -> (b s)").rearrange("(q r p) -> r q p", r=TR, p=P)
        ids_rows = ids.rearrange("b s -> (b s)").rearrange("(c x a p) -> c a x p", x=PAIRS, a=2, p=P)
        ids_last = ids.rearrange("(n u t s) j -> u s t n j", u=LANES, t=TILES, s=2)

        def bc(ap, w=D):
            return ap.unsqueeze(2).broadcast_to([ap.shape[0], ap.shape[1], w])

        negpos = sb("negpos", [P, TILES, D])
        with ExitStack() as setup:
            ids_in = setup.enter_context(nc.sbuf_tensor("s_ids_in", [P, TQ, P], I32))
            idf = setup.enter_context(nc.sbuf_tensor("s_idf", [P, TQ, P], F32))
            idn = setup.enter_context(nc.sbuf_tensor("s_idn", [P, TQ, P], F32))
            CW = [("ident", P), ("maskid", P), ("later", 512), ("ksel", 512), ("rsel", P), ("other", 512), ("abrow", P), ("ab01", 2)]
            with nc.Block() as block:
                @block.sync
                def _(sp):
                    off = 0
                    for k, (name, w) in enumerate(CW):
                        if k:
                            sp.wait_ge(set_act, k)
                        sp.dma_start(cstage[:, 0:w], const[:, off:off + w]).then_inc(stage_in, 16)
                        off += w

                @block.scalar
                def _(act):
                    tiles = {"ident": ident, "maskid": maskid, "later": later, "ksel": ksel, "rsel": rsel,
                             "other": other, "abrow": abrow, "ab01": ab01}
                    for k, (name, w) in enumerate(CW):
                        act.wait_ge(stage_in, 16 * (k + 1))
                        nc.scalar.activation(tiles[name][:], cstage[:, 0:w], ACT.Copy).then_inc(set_act, 1)
                    N0 = len(CW)
                    act.wait_ge(set_pe, 4)
                    nc.scalar.activation(bd["m"][0:D, 0:D], pm[0:D, 0:D], ACT.Copy, scale=0.125).then_inc(set_act, 1)
                    nc.scalar.activation(bd["m"][D:P, D:P], pm[D:P, 0:D], ACT.Copy, scale=0.125).then_inc(set_act, 1)
                    nc.scalar.activation(m2dup[:, 0:D], pm[0:D, 64:128], ACT.Copy, scale=0.125).then_inc(set_act, 1)
                    nc.scalar.activation(m2dup[:, D:P], pm[0:D, 64:128], ACT.Copy, scale=0.125).then_inc(set_act, 1)
                    nc.scalar.activation(cbias[:, :], pm[:, 128:130], ACT.Copy, scale=0.125).then_inc(set_act, 1)
                    act.wait_ge(set_act, N0 + 5)

                @block.gpsimd
                def _(pool):
                    for t in (bd["m"], bd["v"], bd["w1"], bd["w2"], gpair, G2B, idrow, bv3, last_i, P2T, kflag, XL, Q2w, A2w, Y2w):
                        nc.gpsimd.memset(t[:], 0).then_inc(cleared, 1)
                    nc.gpsimd.memset(ones_b[:], 1.0).then_inc(cleared, 1)
                    nc.gpsimd.memset(eps[:], EPS).then_inc(cleared, 1)
                    for u in LN:
                        nc.gpsimd.memset(BLK[u][:], 0).then_inc(cleared, 1)
                    pool.wait_ge(cleared, 17 + LANES)
                    for ab in range(2):
                        for u in LN:
                            nc.gpsimd.memset(G2B[ab * D:ab * D + D, u, 16 + ab:17 + ab], 1.0).then_inc(cleared, 1)
                    pool.wait_ge(cleared, 17 + 3 * LANES)
                    h = slice
                    dma = [(bd["v"][0:D, 0:D], wv[0]), (bd["v"][D:P, D:P], wv[0]),
                           (bd["w1"][0:D, 0:D], w1[0]), (bd["w1"][D:P, D:P], w1[0]),
                           (bd["w2"][0:D, 0:D], w2[0]), (bd["w2"][D:P, D:P], w2[0]),
                           (small[:, 0, :], wv[1]), (small[:, 1, :], w1[1]), (small[:, 2, :], w1[1]), (small[:, 3, :], w2[1]),
                           (col[:], cols), (gpair[0:D, 0:1], cols[0:D, 0:1]), (gpair[D:P, 1:2], cols[D:P, 0:1]),
                           (wq_d[:, :, 0:D], wqT.rearrange("l d f -> d l f")), (wq_d[:, :, D:P], wqT.rearrange("l d f -> d l f")),
                           (wk_s[:, :, 0:D], wkT.rearrange("l d f -> d l f")), (wk_s[:, :, D:P], wkT.rearrange("l d f -> d l f")),
                           (row[:], rows.unsqueeze(0).broadcast_to([P, rows.shape[0], D])),
                           (SEQ[0][0:S, 0, :], pos_emb), (SEQ[0][S:P, 0, :], pos_emb),
                           (ids_in[0:TR], ids_tiles)]
                    for dst, src in dma:
                        pool.dma_start(dst, src, allow_slow_non_contiguous=True).then_inc(loaded, 16)
                    for u in LN:
                        for s in range(2):
                            pool.dma_start(last_i[32 * u + 8 * s:32 * u + 8 * s + 8, :].unsqueeze(2), ids_last[u, s][:, :, S - 1:S],
                                           allow_slow_non_contiguous=True).then_inc(loaded, 16)
                    pool.wait_ge(loaded, 16 * (len(dma) + 2 * LANES))

                @block.tensor
                def _(pe):
                    pe.wait_ge(loaded, 16 * (21 + 2 * LANES))
                    nc.tensor.matmul(pm[:, 0:D], wq_d[:, 0, :], wk_s[:, 0, 0:D], start=True, stop=True).then_inc(set_pe, 1)
                    nc.tensor.matmul(pm[0:D, D:P], wq_d[:, 1, 0:D], wk_s[:, 1, 0:D], start=True, stop=True).then_inc(set_pe, 1)
                    for l in range(2):
                        nc.tensor.matmul(pm[:, P + l:P + l + 1], wk_s[:, l, :], col[0:D, 5 + l:6 + l], start=True, stop=True).then_inc(set_pe, 1)
                    pe.wait_ge(set_dve, 12)
                    pe.wait_ge(set_act, 1)
                    for q in range(TQ):
                        if q:
                            pe.wait_ge(set_dve, 12 + 2 * q)
                        nc.tensor.transpose(pl[0][:, 0:TR], idf[0:TR, q, :], ident[0:TR, 0:TR]).then_inc(set_pe, 1)
                        nc.tensor.transpose(pl[1][:, 0:TR], idn[0:TR, q, :], ident[0:TR, 0:TR]).then_inc(set_pe, 1)

                @block.vector
                def _(dve):
                    dve.wait_ge(loaded, 16 * (21 + 2 * LANES))
                    k = [0]

                    def done(ins):
                        ins.then_inc(set_dve, 1)
                        k[0] += 1
                        dve.wait_ge(set_dve, k[0])

                    done(nc.vector.tensor_copy(idf[0:TR], ids_in[0:TR]))
                    done(nc.vector.tensor_scalar(idn[0:TR], idf[0:TR], 0.0, float(NI), ALU.is_lt, ALU.mult))
                    done(nc.vector.tensor_tensor(idn[0:TR], idn[0:TR], idf[0:TR], ALU.add))
                    done(nc.vector.tensor_scalar(idn[0:TR], idn[0:TR], 0.0, float(NI - 1), ALU.max, ALU.min))
                    done(nc.vector.scalar_tensor_tensor(out=idf[0:TR], in0=idf[0:TR], scalar=float(MASK_ID), in1=idn[0:TR],
                                                        op0=ALU.is_equal, op1=ALU.add))
                    done(nc.vector.tensor_copy(idn[0:TR], ids_in[0:TR]))
                    done(nc.vector.tensor_scalar(idn[0:TR], idn[0:TR], float(MASK_ID), None, ALU.not_equal))
                    done(nc.vector.tensor_copy(last_all[:], last_i[:]))
                    done(nc.vector.tensor_scalar(last_all[:], last_all[:], float(MASK_ID), None, ALU.not_equal))
                    done(nc.vector.tensor_scalar(negpos[:, :, :], SEQ[0][:, 0, :].unsqueeze(1).broadcast_to([P, TILES, D]),
                                                 -1.0, None, ALU.mult))
                    done(nc.vector.tensor_reduce(gsum[:, 0:1], row[:, 0, :], AX, ALU.add))
                    done(nc.vector.tensor_reduce(gsum[:, 1:2], row[:, 1, :], AX, ALU.add))
                    assert k[0] == 12
                    for q in range(TQ):
                        dve.wait_ge(set_pe, 4 + 2 * q + 2)
                        done(nc.vector.tensor_copy(idx_all[:, q * TR:q * TR + TR], pl[0][:, 0:TR]))
                        done(nc.vector.tensor_copy(kept_all[:, q * TR:q * TR + TR], pl[1][:, 0:TR]))
                    done(nc.vector.tensor_scalar(gsum[:, 0:1], gsum[:, 0:1], -0.5, None, ALU.mult))
                    bv = row[:, 2, :]
                    done(nc.vector.tensor_copy(bvb[:, 0, :], bv))
                    done(nc.vector.tensor_copy(bvt[:, 0, :], bvb[:, 0, :]))
                    done(nc.vector.tensor_tensor(bvt[:, 1, :], bv, bvt[:, 0, :], ALU.subtract))
                    done(nc.vector.tensor_copy(bvb[:, 1, :], bvt[:, 1, :]))
                    done(nc.vector.tensor_copy(bvt[:, 2, :], bvb[:, 1, :]))
                    done(nc.vector.tensor_tensor(bvt[:, 3, :], bvt[:, 1, :], bvt[:, 2, :], ALU.subtract))
                    done(nc.vector.tensor_copy(bvb[:, 2, :], bvt[:, 3, :]))
                    for r in range(3):
                        done(nc.vector.tensor_copy(bv3[32 * r:32 * r + 1, :].rearrange("p (t f) -> p t f", f=D),
                                                   bvb[32 * r:32 * r + 1, r, :].unsqueeze(1).broadcast_to([1, TILES, D])))

        def rows_act(act, n):
            def rstd0(k):
                act.wait_ge(dve_row, DR.at(n, k + "var64"))
                nc.scalar.activation(rs["ln"][:], rs["var64"][:], ACT.Ln, scale=1.0 / 64, bias=eps[:, 0:1]).then_inc(act_row, 1)
                act.wait_ge(act_row, AR.at(n, k + "ln"))
                nc.scalar.activation(rs["r0"][:], rs["ln"][:], ACT.Exp, scale=-0.5).then_inc(act_row, 1)
            rstd0("a")
            act.wait_ge(pe_row, PR.at(n, "qT"))
            nc.scalar.activation(rT[:], pr2[0:D, 0:P], ACT.Copy).then_inc(act_row, 1)
            act.wait_ge(dve_row, DR.at(n, "shift"))
            nc.scalar.activation(P2[:], P2[:], ACT.Exp).then_inc(act_row, 1)
            act.wait_ge(pe_row, PR.at(n, "a2T"))
            nc.scalar.activation(rT[:], pr2[0:D, 0:P], ACT.Copy).then_inc(act_row, 1)
            rstd0("b")
            act.wait_ge(pe_row, PR.at(n, "yT"))
            nc.scalar.activation(rT[:], pr2[0:D, 0:P], ACT.Copy).then_inc(act_row, 1)
            act.wait_ge(pe_row, PR.at(n, "h"))
            nc.scalar.activation(rT[:], pr2[0:D, 0:P], ACT.Relu, bias=col[0:D, 7:8]).then_inc(act_row, 1)
            rstd0("c")

        def rows_pe(pe, n):
            pe.wait_ge(dve_row, DR.at(n, "aout"))
            nc.tensor.transpose(pr2[:, 0:P], Q2w[:], ident[:]).then_inc(pe_row, 1)
            pe.wait_ge(act_row, AR.at(n, "qT"))
            nc.tensor.matmul(pr2[:, P:2 * P], m2dup[:], rT[:], start=True, stop=True).then_inc(pe_row, 1)
            pe.wait_ge(dve_row, DR.at(n, "g2"))
            for u in LN:
                m = nc.tensor.matmul(pr[32 * u:32 * u + 32, :], G2B[:, u, :], S2T[u][:], start=True, stop=False, skip_group_check=True)
            m.then_inc(pe_row, 1)
            pe.wait_ge(dve_row, DR.at(n, "flag2"))
            nc.tensor.matmul(pr[:], rsel[:], flag2[:], start=False, stop=False, skip_group_check=True)
            nc.tensor.matmul(pr[:], maskid[:], other[:], start=False, stop=True, skip_group_check=True).then_inc(pe_row, 1)
            pe.wait_ge(dve_row, DR.at(n, "valid"))
            for x in range(PAIRS):
                m = nc.tensor.transpose(pr[:, x * P:(x + 1) * P], P2[:, x * P:(x + 1) * P], ident[:])
            m.then_inc(pe_row, 1)
            pe.wait_ge(dve_row, DR.at(n, "p2T", PAIRS - 1))
            for u in LN:
                pe.wait_ge(act_lane, AL.at(n, "s2N", u))
                for x in range(PAIRS):
                    m = nc.tensor.matmul(pr2[32 * u:32 * u + 32, 0:P], P2T[:, x, 32 * u:32 * u + 32],
                                         S2N[u][:, 2 * x:2 * x + 2, :].rearrange("p t f -> p (t f)"),
                                         start=(x == 0), stop=(x == PAIRS - 1), skip_group_check=True)
            m.then_inc(pe_row, 1)
            pe.wait_ge(dve_row, DR.at(n, "a2"))
            nc.tensor.transpose(pr2[:, 0:P], A2w[:], ident[:]).then_inc(pe_row, 1)
            pe.wait_ge(act_row, AR.at(n, "a2T"))
            nc.tensor.matmul(pr2[:, P:P + D], rT[:], small[:, 0, :], start=True, stop=True).then_inc(pe_row, 1)
            pe.wait_ge(dve_row, DR.at(n, "bout"))
            nc.tensor.transpose(pr2[:, 0:P], Y2w[:], ident[:]).then_inc(pe_row, 1)
            pe.wait_ge(act_row, AR.at(n, "yT"))
            nc.tensor.matmul(pr2[:, 0:P], small[:, 1:3, :].rearrange("p k f -> p (k f)"), rT[:], start=True, stop=True).then_inc(pe_row, 1)
            pe.wait_ge(act_row, AR.at(n, "hT"))
            nc.tensor.matmul(pr2[:, P:P + D], rT[:], small[:, 3, :], start=True, stop=True).then_inc(pe_row, 1)
            pe.wait_ge(dve_row, DR.at(n, "cout"))
            nc.tensor.transpose(pr2[:, 0:P], hfin[:].rearrange("p k f -> p (k f)"), ident[:]).then_inc(pe_row, 1)

        def rows_dve(dve, n):
            def seen(*name):
                return DR.at(n, *name)

            def norm(k, src, gain, bias, dst, need):
                dve.wait_ge(dve_row, need)
                nc.vector.bn_stats(rbn[:], src).then_inc(dve_row, 1)
                dve.wait_ge(dve_row, seen(k + "bn"))
                nc.vector.tensor_tensor(rs["sum"][:], rbn[:, 1:2], rbn[:, 4:5], ALU.add).then_inc(dve_row, 1)
                nc.vector.tensor_tensor(rs["diff"][:], rbn[:, 1:2], rbn[:, 4:5], ALU.subtract).then_inc(dve_row, 1)
                nc.vector.tensor_tensor(rs["m2"][:], rbn[:, 2:3], rbn[:, 5:6], ALU.add).then_inc(dve_row, 1)
                dve.wait_ge(dve_row, seen(k + "diff"))
                nc.vector.scalar_tensor_tensor(out=rs["spread"][:], in0=rs["diff"][:], scalar=16.0, in1=rs["diff"][:],
                                               op0=ALU.mult, op1=ALU.mult).then_inc(dve_row, 1)
                dve.wait_ge(dve_row, seen(k + "spread"))
                nc.vector.tensor_tensor(rs["var64"][:], rs["m2"][:], rs["spread"][:], ALU.add).then_inc(dve_row, 1)
                dve.wait_ge(dve_row, seen(k + "var64"))
                nc.vector.tensor_scalar(rs["var"][:], rs["var64"][:], 1.0 / 64, EPS, ALU.mult, ALU.add).then_inc(dve_row, 1)
                nc.vector.tensor_scalar(rs["mean"][:], rs["sum"][:], 0.5, None, ALU.mult).then_inc(dve_row, 1)
                dve.wait_ge(act_row, AR.at(n, k + "r0"))
                nc.vector.tensor_tensor(rs["nsq"][:], rs["r0"][:], rs["r0"][:], ALU.mult).then_inc(dve_row, 1)
                dve.wait_ge(dve_row, seen(k + "nsq"))
                nc.vector.scalar_tensor_tensor(out=rs["nhalf"][:], in0=rs["nsq"][:], scalar=-0.5, in1=rs["var"][:],
                                               op0=ALU.mult, op1=ALU.mult).then_inc(dve_row, 1)
                dve.wait_ge(dve_row, seen(k + "nhalf"))
                nc.vector.scalar_tensor_tensor(out=rs["rstd"][:], in0=rs["nhalf"][:], scalar=1.5, in1=rs["r0"][:],
                                               op0=ALU.add, op1=ALU.mult).then_inc(dve_row, 1)
                dve.wait_ge(dve_row, seen(k + "rstd"))
                nc.vector.tensor_scalar(rhat[:], src, rs["mean"][:, 0:1], rs["rstd"][:, 0:1], ALU.subtract, ALU.mult).then_inc(dve_row, 1)
                dve.wait_ge(dve_row, seen(k + "hat"))
                nc.vector.tensor_tensor(rgain[:], rhat[:], gain, ALU.mult).then_inc(dve_row, 1)
                dve.wait_ge(dve_row, seen(k + "gain"))
                if dst is hfin:
                    nc.vector.tensor_tensor(hfin[:], rgain[:].unsqueeze(1).broadcast_to([P, 2, D]),
                                            bias.unsqueeze(1).broadcast_to([P, 2, D]), ALU.add).then_inc(dve_row, 1)
                else:
                    nc.vector.tensor_tensor(dst[:], rgain[:], bias, ALU.add).then_inc(dve_row, 1)

            nc.vector.tensor_copy(last_now[:], last_all[:, bass.ds(n, 1)]).then_inc(dve_row, 1)
            nc.vector.tensor_copy(kept_now[:], kept_all[:, bass.ds(n * (LANES * TILES), LANES * TILES)]).then_inc(dve_row, 1)
            dve.wait_ge(rows_in, n * ROWS_DMA + ROWS_DMA)
            dve.wait_ge(dve_row, seen("now"))
            nc.vector.tensor_scalar(XLM[:], XL[:], last_now[:, 0:1], None, ALU.mult).then_inc(dve_row, 1)
            norm("a", XLM[:], row[:, 3, :], row[:, 4, :], Q2, seen("xlm"))
            dve.wait_ge(dve_row, seen("aout"))
            nc.vector.tensor_reduce(rs["qsum"][:], Q2[:], AX, ALU.add).then_inc(dve_row, 1)
            dve.wait_ge(dve_row, seen("qsum"))
            nc.vector.tensor_scalar(rs["qm"][:], rs["qsum"][:], 0.0, None, ALU.not_equal).then_inc(dve_row, 1)
            dve.wait_ge(pe_row, PR.at(n, "g2"))
            nc.vector.scalar_tensor_tensor(out=G2B[:, :, 0:16], in0=pr2[:, P:2 * P].rearrange("p (u r) -> p u r", r=32)[:, :, 0:16],
                                           scalar=cbias[:, 1:2], in1=abrow[:].rearrange("p (u r) -> p u r", r=32)[:, :, 0:16],
                                           op0=ALU.add, op1=ALU.mult).then_inc(dve_row, 1)
            nc.vector.tensor_scalar(idflag[:], idrow[:], float(MASK_ID), None, ALU.is_equal).then_inc(dve_row, 1)
            dve.wait_ge(dve_row, seen("idflag"))
            dve.wait_ge(pe_row, PR.at(n, "s2"))
            nc.vector.scalar_tensor_tensor(out=flag2[:], in0=pr[:], scalar=0.0, in1=idflag[:],
                                           op0=ALU.is_equal, op1=ALU.max).then_inc(dve_row, 1)
            dve.wait_ge(pe_row, PR.at(n, "flag"))
            nc.vector.tensor_reduce(rs["max"][:], pr[:], AX, ALU.max).then_inc(dve_row, 1)
            dve.wait_ge(dve_row, seen("max"))
            nc.vector.tensor_scalar(P2[:], pr[:], MASKED, rs["max"][:, 0:1], ALU.max, ALU.subtract).then_inc(dve_row, 1)
            dve.wait_ge(act_row, AR.at(n, "exp"))
            nc.vector.scalar_tensor_tensor(out=P2[:], in0=other[:], scalar=0.0, in1=P2[:],
                                           op0=ALU.is_equal, op1=ALU.mult).then_inc(dve_row, 1)
            dve.wait_ge(dve_row, seen("valid"))
            nc.vector.tensor_reduce(rs["den"][:], P2[:], AX, ALU.add).then_inc(dve_row, 1)
            dve.wait_ge(dve_row, seen("den"))
            nc.vector.reciprocal(rs["rden"][:], rs["den"][:]).then_inc(dve_row, 1)
            dve.wait_ge(dve_row, seen("rden"))
            nc.vector.tensor_tensor(rs["ra"][:], rs["rden"][:], ab01[:, 0:1], ALU.mult).then_inc(dve_row, 1)
            nc.vector.tensor_tensor(rs["rb"][:], rs["rden"][:], ab01[:, 1:2], ALU.mult).then_inc(dve_row, 1)
            dve.wait_ge(pe_row, PR.at(n, "p2T"))
            kn = kept_now[:].rearrange("p (u t) -> p u t", u=LANES).unsqueeze(2).broadcast_to([P, LANES, 2, TILES])
            for x in range(PAIRS):
                nc.vector.tensor_tensor(P2T[:, x, :].rearrange("p (u s t) -> p u s t", u=LANES, t=TILES)[:, :, 0:2, :],
                                        pr[:, x * P:(x + 1) * P].rearrange("p (u s t) -> p u s t", u=LANES, t=TILES)[:, :, 0:2, :],
                                        kn, ALU.mult).then_inc(dve_row, 1)
            dve.wait_ge(pe_row, PR.at(n, "a2"))
            dve.wait_ge(dve_row, seen("rb"))
            nc.vector.tensor_scalar(A2[:], pr2[:, 0:D], rs["ra"][:, 0:1], None, ALU.mult).then_inc(dve_row, 1)
            dve.wait_ge(dve_row, seen("a2a"))
            nc.vector.scalar_tensor_tensor(out=A2[:], in0=pr2[:, D:P], scalar=rs["rb"][:, 0:1], in1=A2[:],
                                           op0=ALU.mult, op1=ALU.add).then_inc(dve_row, 1)
            dve.wait_ge(pe_row, PR.at(n, "o2"))
            nc.vector.tensor_tensor(X2a[:], pr2[:, P:P + D], row[:, 5, :], ALU.add).then_inc(dve_row, 1)
            dve.wait_ge(dve_row, seen("x2a"))
            nc.vector.scalar_tensor_tensor(out=X2[:], in0=X2a[:], scalar=rs["qm"][:, 0:1], in1=Q2[:],
                                           op0=ALU.mult, op1=ALU.add).then_inc(dve_row, 1)
            norm("b", X2[:], row[:, 6, :], row[:, 7, :], Y2, seen("x2"))
            dve.wait_ge(pe_row, PR.at(n, "z"))
            nc.vector.tensor_tensor(Z2a[:], pr2[:, P:P + D], row[:, 8, :], ALU.add).then_inc(dve_row, 1)
            dve.wait_ge(dve_row, seen("z2a"))
            nc.vector.tensor_tensor(Z2[:], Z2a[:], Y2[:], ALU.add).then_inc(dve_row, 1)
            dve.wait_ge(dve_row, seen("z2"))
            nc.vector.tensor_scalar(Z2m[:], Z2[:], last_now[:, 0:1], None, ALU.mult).then_inc(dve_row, 1)
            norm("c", Z2m[:], row[:, 9, :], row[:, 10, :], hfin, seen("z2m"))
            dve.wait_ge(pe_row, PR.at(n, "fT"))

            def seqs(tile):
                return tile[:, bass.ds(n * BATCH, BATCH)].rearrange("p (u t s) -> p u s t", u=LANES, s=2)
            src = pr2[:, 0:P].rearrange("p (u s t) -> p u s t", u=LANES, t=TILES)[:, :, 0:2, :]
            nc.vector.tensor_copy(seqs(hid_hi), src).then_inc(dve_row, 1)
            dve.wait_ge(dve_row, seen("hi"))
            nc.vector.tensor_tensor(seqs(hid_lo), src, seqs(hid_hi).bitcast(F32), ALU.subtract).then_inc(dve_row, 1)


        if True:
            with nc.Block() as block:
                @block.sync
                def _(sp):
                    def prefill(n):
                        for u in LN:
                            if n is not None:
                                sp.wait_ge(dve_lane, DL.at(n, "seq", u))
                            sp.dma_start(X[u][:], negpos[:]).then_inc(prefilled[u], 16)

                    def rows_load(n):
                        chunk = [n * LANES + u for u in LN]
                        if not isinstance(n, int):
                            chunk = [sp.snap(c) for c in chunk]
                        sp.wait_ge(dve_row, DR.start(n))
                        for u in LN:
                            sp.dma_start(idrow[32 * u + 16:32 * u + 18, :].rearrange("a (x p) -> a x p", p=P),
                                         ids_rows[bass.ds(chunk[u], 1)].rearrange("c a x p -> (c a) x p")).then_inc(rows_in, 16)

                    def last_load(n):
                        for u in LN:
                            sp.wait_ge(act_lane, AL.at(n, "s2N", u))
                            for s in range(2):
                                r = 32 * u + 8 * s
                                sp.dma_start(XL[r:r + 8, :], S2N[u][64 * s + 63:64 * s + 64, :, :]).then_inc(rows_in, 16)

                    prefill(None)
                    with sp.Fori(0, PASSES - 1) as n:
                        rows_load(n)
                        prefill(n)
                        last_load(n)
                    rows_load(PASSES - 1)
                    last_load(PASSES - 1)

                @block.gpsimd
                def _(pool):
                    def gather(n):
                        for u in LN:
                            tiles_of_u = n * (LANES * TILES) + u * TILES
                            if not isinstance(n, int):
                                pool.wait_ge(dve_lane, DL.at(n - 1, "seq", u))
                                tiles_of_u = pool.snap(tiles_of_u)
                            nc.gpsimd.tensor_copy(idx_now[u][:], idx_all[:, bass.ds(tiles_of_u, TILES)]).then_inc(idx_copied, 1)
                            pool.wait_ge(idx_copied, n * LANES + u + 1)
                            pool.wait_ge(prefilled[u], n * 16 + 16)
                            pool.reg_sub(last_item, table_rows, 1)
                            for t in range(TILES):
                                nc.gpsimd.indirect_dma_start(
                                    out=X[u][:, t, :], out_offset=None, in_=item_emb,
                                    in_offset=bass.IndirectOffsetOnAxis(ap=idx_now[u][:, t:t + 1], axis=0),
                                    bounds_check=last_item, oob_is_err=False).then_inc(gathered[u], 16)

                    table_rows = pool.to_reg(NI)
                    last_item = pool.alloc_register("last_item")
                    gather(0)
                    with pool.Fori(1, PASSES) as n:
                        gather(n)

                @block.scalar
                def _(act):
                    with act.Fori(0, PASSES) as n:
                        for u in LN:
                            act.wait_ge(pe_lane, PL.at(n, "keyT", u))
                            nc.scalar.activation(KT[u][:], pl[u][:], ACT.Copy).then_inc(act_lane, 1)
                        act.wait_ge(dve_lane, DL.at(n, "1var"))
                        nc.scalar.activation(st["ln"][:], st["var64"][:], ACT.Ln, scale=1.0 / 64, bias=eps[:, 0:1]).then_inc(act_lane, 1)
                        act.wait_ge(act_lane, AL.at(n, "1ln"))
                        nc.scalar.activation(st["r0"][:], st["ln"][:], ACT.Exp, scale=-0.5).then_inc(act_lane, 1)
                        act.wait_ge(pe_lane, PL.at(n, "kflagT"))
                        nc.scalar.activation(kflagT[:], pm[:, 0:P], ACT.Copy).then_inc(act_lane, 1)
                        for u in LN:
                            act.wait_ge(pe_lane, PL.at(n, "v", u))
                            nc.scalar.activation(V[u][:], pl[u][:], ACT.Copy).then_inc(act_lane, 1)
                        for u in LN:
                            act.wait_ge(pe_lane, PL.at(n, "hatT", u))
                            nc.scalar.activation(QT[u][:], pl[u][:], ACT.Identity, scale=col[:, 0:1], bias=col[:, 1:2]).then_inc(act_lane, 1)
                        for u in LN:
                            act.wait_ge(pe_lane, PL.at(n, "g", u))
                            for ab in range(2):
                                h = slice(64 * ab, 64 * ab + 64)
                                nc.scalar.activation(BLK[u][h, :, h], pl[u][h, :].rearrange("p (k i) -> p k i", i=S),
                                                     ACT.Identity, bias=cbias[h, 0:1]).then_inc(act_lane, 1)
                        for u in LN:
                            act.wait_ge(dve_lane, DL.at(n, "shift", u))
                            nc.scalar.activation(XN[u][:], XN[u][:], ACT.Exp).then_inc(act_lane, 1)
                        for u in LN:
                            act.wait_ge(pe_lane, PL.at(n, "pT", u))
                            for s in range(2):
                                h = slice(64 * s, 64 * s + 64)
                                nc.scalar.activation(BLK[u][h, :, h], pl[u][h, :].rearrange("p (k i) -> p k i", i=S),
                                                     ACT.Copy).then_inc(act_lane, 1)
                        act.wait_ge(dve_lane, DL.at(n, "2var"))
                        nc.scalar.activation(st["ln"][:], st["var64"][:], ACT.Ln, scale=1.0 / 64, bias=eps[:, 0:1]).then_inc(act_lane, 1)
                        act.wait_ge(act_lane, AL.at(n, "2ln"))
                        nc.scalar.activation(st["r0"][:], st["ln"][:], ACT.Exp, scale=-0.5).then_inc(act_lane, 1)
                        for u in LN:
                            act.wait_ge(pe_lane, PL.at(n, "yT", u))
                            nc.scalar.activation(QT[u][:], pl[u][:], ACT.Identity, scale=col[:, 2:3], bias=col[:, 3:4]).then_inc(act_lane, 1)
                        for u in LN:
                            act.wait_ge(pe_lane, PL.at(n, "h", u))
                            nc.scalar.activation(KT[u][:], pl[u][:], ACT.Relu, bias=col[:, 4:5]).then_inc(act_lane, 1)
                        for u in LN:
                            act.wait_ge(pe_lane, PL.at(n, "s2N", u))
                            nc.scalar.activation(S2N[u][:], pl[u][:], ACT.Copy).then_inc(act_lane, 1)
                        rows_act(act, n)

                @block.tensor
                def _(pe):
                    with pe.Fori(0, PASSES) as n:
                        for u in LN:
                            pe.wait_ge(act_lane, AL.start(n))
                            pe.wait_ge(dve_lane, DL.at(n, "seq", u))
                            for x in range(PAIRS):
                                m = nc.tensor.transpose(pl[u][:, x * P:(x + 1) * P],
                                                        SEQ[u][:, 2 * x:2 * x + 2, :].rearrange("p t f -> p (t f)"), ident[:])
                            m.then_inc(pe_lane, 1)
                        pe.wait_ge(dve_lane, DL.at(n, "kflag"))
                        nc.tensor.transpose(pm[:, 0:P], kflag[:].rearrange("p u t -> p (u t)"), ident[:]).then_inc(pe_lane, 1)
                        for u in LN:
                            pe.wait_ge(act_lane, AL.at(n, "keyT", u))
                            nc.tensor.matmul(pl[u][:], ones_b[:], bv3[:], start=True, stop=False, skip_group_check=True)
                            for x in range(PAIRS):
                                nc.tensor.matmul(pl[u][:, x * P:(x + 1) * P], KT[u][:, x * P:(x + 1) * P], bd["v"][:],
                                                 start=False, stop=(x == PAIRS - 1), skip_group_check=True)
                                m = nc.tensor.matmul(pg[:, u * TILES + 2 * x:u * TILES + 2 * x + 2],
                                                     KT[u][:, x * P:(x + 1) * P], gpair[:], start=True, stop=True, skip_group_check=True)
                            m.then_inc(pe_lane, 1)
                        for u in LN:
                            pe.wait_ge(act_lane, AL.at(n, "v", u))
                            pe.wait_ge(dve_lane, DL.at(n, "hat1", u))
                            for x in range(PAIRS):
                                m = nc.tensor.transpose(pl[u][:, x * P:(x + 1) * P],
                                                        XN[u][:, 2 * x:2 * x + 2, :].rearrange("p t f -> p (t f)"), ident[:])
                            m.then_inc(pe_lane, 1)
                        for u in LN:
                            pe.wait_ge(act_lane, AL.at(n, "qT", u))
                            nc.tensor.matmul(pl[u][:], bd["m"][:], QT[u][:], start=True, stop=True).then_inc(pe_lane, 1)
                        for u in LN:
                            pe.wait_ge(act_lane, AL.at(n, "gB", u))
                            nc.tensor.matmul(pl[u][:], maskid[:], later[:], start=True, stop=False, skip_group_check=True)
                            for x in range(PAIRS):
                                nc.tensor.matmul(pl[u][:, x * P:(x + 1) * P], ksel[32 * u:32 * u + TILES, x * P:(x + 1) * P],
                                                 kflagT[32 * u:32 * u + TILES, :], start=False, stop=False, skip_group_check=True)
                            for k in range(TILES):
                                m = nc.tensor.matmul(pl[u][:, k * S:(k + 1) * S], BLK[u][:, k, :], KT[u][:, k * S:(k + 1) * S],
                                                     start=False, stop=(k == TILES - 1), skip_group_check=True)
                            m.then_inc(pe_lane, 1)
                        for u in LN:
                            pe.wait_ge(dve_lane, DL.at(n, "prob", u))
                            for x in range(PAIRS):
                                m = nc.tensor.transpose(pl[u][:, x * P:(x + 1) * P],
                                                        XN[u][:, 2 * x:2 * x + 2, :].rearrange("p t f -> p (t f)"), ident[:])
                            m.then_inc(pe_lane, 1)
                        for u in LN:
                            pe.wait_ge(act_lane, AL.at(n, "pB", u))
                            for t in range(TILES):
                                ab, x = t % 2, t // 2
                                m = nc.tensor.matmul(pl[u][64 * ab:64 * ab + 64, x * P:(x + 1) * P], V[u][:, t, :], BLK[u][:, t, :],
                                                     start=True, stop=True, skip_group_check=True)
                            m.then_inc(pe_lane, 1)
                        for u in LN:
                            pe.wait_ge(dve_lane, DL.at(n, "res1", u))
                            for x in range(PAIRS):
                                m = nc.tensor.transpose(pl[u][:, x * P:(x + 1) * P],
                                                        SEQ[u][:].rearrange("p t f -> p (t f)")[:, x * P:(x + 1) * P], ident[:])
                            m.then_inc(pe_lane, 1)
                        for u in LN:
                            pe.wait_ge(dve_lane, DL.at(n, "hat2", u))
                            for x in range(PAIRS):
                                m = nc.tensor.transpose(pl[u][:, x * P:(x + 1) * P],
                                                        XN[u][:, 2 * x:2 * x + 2, :].rearrange("p t f -> p (t f)"), ident[:])
                            m.then_inc(pe_lane, 1)
                        for u in LN:
                            pe.wait_ge(act_lane, AL.at(n, "yT", u))
                            nc.tensor.matmul(pl[u][:], bd["w1"][:], QT[u][:], start=True, stop=True).then_inc(pe_lane, 1)
                        for u in LN:
                            pe.wait_ge(act_lane, AL.at(n, "hT", u))
                            nc.tensor.matmul(pl[u][:], bd["w2"][:], KT[u][:], start=True, stop=True).then_inc(pe_lane, 1)
                        for u in LN:
                            pe.wait_ge(dve_lane, DL.at(n, "seq2", u))
                            for x in range(PAIRS):
                                m = nc.tensor.transpose(pl[u][:, x * P:(x + 1) * P], S2T[u][:, x * P:(x + 1) * P], ident[:])
                            m.then_inc(pe_lane, 1)
                        rows_pe(pe, n)

                @block.vector
                def _(dve):
                    def var_steps(n, k):
                        e = lambda i: bn[:, :, :, i]
                        dve.wait_ge(dve_lane, DL.at(n, "bn" + k, LANES - 1))
                        nc.vector.tensor_tensor(st["sum"][:], e(1), e(4), ALU.add).then_inc(dve_lane, 1)
                        nc.vector.tensor_tensor(st["diff"][:], e(1), e(4), ALU.subtract).then_inc(dve_lane, 1)
                        nc.vector.tensor_tensor(st["m2"][:], e(2), e(5), ALU.add).then_inc(dve_lane, 1)
                        dve.wait_ge(dve_lane, DL.at(n, k + "diff"))
                        nc.vector.scalar_tensor_tensor(out=st["spread"][:], in0=st["diff"][:], scalar=16.0, in1=st["diff"][:],
                                                       op0=ALU.mult, op1=ALU.mult).then_inc(dve_lane, 1)
                        dve.wait_ge(dve_lane, DL.at(n, k + "spread"))
                        nc.vector.tensor_tensor(st["var64"][:], st["m2"][:], st["spread"][:], ALU.add).then_inc(dve_lane, 1)
                        dve.wait_ge(dve_lane, DL.at(n, k + "var64"))
                        nc.vector.tensor_scalar(st["var"][:], st["var64"][:], 1.0 / 64, EPS, ALU.mult, ALU.add).then_inc(dve_lane, 1)

                    def newton_steps(n, k):
                        dve.wait_ge(act_lane, AL.at(n, k + "r0"))
                        nc.vector.tensor_tensor(st["nsq"][:], st["r0"][:], st["r0"][:], ALU.mult).then_inc(dve_lane, 1)
                        dve.wait_ge(dve_lane, DL.at(n, k + "nsq"))
                        nc.vector.scalar_tensor_tensor(out=st["nhalf"][:], in0=st["nsq"][:], scalar=-0.5, in1=st["var"][:],
                                                       op0=ALU.mult, op1=ALU.mult).then_inc(dve_lane, 1)
                        dve.wait_ge(dve_lane, DL.at(n, k + "nhalf"))
                        nc.vector.scalar_tensor_tensor(out=st["rstd"][:], in0=st["nhalf"][:], scalar=1.5, in1=st["r0"][:],
                                                       op0=ALU.add, op1=ALU.mult).then_inc(dve_lane, 1)

                    with dve.Fori(0, PASSES) as n:
                        for u in LN:
                            dve.wait_ge(gathered[u], n * (16 * TILES) + 16 * TILES)
                            nc.vector.scalar_tensor_tensor(out=SEQ[u][:], in0=negpos[:], scalar=-1.0, in1=X[u][:],
                                                           op0=ALU.mult, op1=ALU.add).then_inc(dve_lane, 1)
                        for u in LN:
                            dve.wait_ge(dve_lane, DL.at(n, "seq", u))
                            for t in range(TILES):
                                m = nc.vector.bn_stats(bn[:, u, t, :], SEQ[u][:, t, :])
                            m.then_inc(dve_lane, 1)
                        var_steps(n, "1")
                        nc.vector.tensor_scalar(kflag[:, :, 0:TILES], st["sum"][:], 0.0, None, ALU.is_equal).then_inc(dve_lane, 1)
                        for u in LN:
                            nc.vector.scalar_tensor_tensor(out=XN[u][:], in0=bc(st["sum"][:, u, :]), scalar=-0.5, in1=SEQ[u][:],
                                                           op0=ALU.mult, op1=ALU.add).then_inc(dve_lane, 1)
                        newton_steps(n, "1")
                        for u in LN:
                            dve.wait_ge(dve_lane, DL.at(n, "1rstd"))
                            nc.vector.tensor_tensor(XN[u][:], XN[u][:], bc(st["rstd"][:, u, :]), ALU.mult).then_inc(dve_lane, 1)
                        dve.wait_ge(pe_lane, PL.at(n, "v", LANES - 1))
                        nc.vector.scalar_tensor_tensor(out=st["qs"][:], in0=st["sum"][:], scalar=gsum[:, 0:1],
                                                       in1=pg[:, 0:LANES * TILES].rearrange("p (u t) -> p u t", u=LANES),
                                                       op0=ALU.mult, op1=ALU.add).then_inc(dve_lane, 1)
                        dve.wait_ge(dve_lane, DL.at(n, "qs"))
                        nc.vector.tensor_tensor(st["qsr"][:], st["qs"][:], st["rstd"][:], ALU.mult).then_inc(dve_lane, 1)
                        dve.wait_ge(dve_lane, DL.at(n, "qsr"))
                        nc.vector.tensor_scalar(st["qtok"][:], st["qsr"][:], gsum[:, 1:2], 0.0, ALU.add, ALU.not_equal).then_inc(dve_lane, 1)
                        dve.wait_ge(dve_lane, DL.at(n, "qtok"))
                        for s in range(2):
                            for ab in range(2):
                                nc.vector.tensor_copy(st["qrow"][64 * ab:64 * ab + 64, :, s::2],
                                                      st["qtok"][64 * s:64 * s + 64, :, ab::2]).then_inc(dve_lane, 1)
                        for u in LN:
                            dve.wait_ge(pe_lane, PL.at(n, "s", u))
                            nc.vector.tensor_reduce(st["max"][:, u, :], pl[u][:].rearrange("p (k j) -> p k j", j=S), AX, ALU.max).then_inc(dve_lane, 1)
                        for u in LN:
                            dve.wait_ge(dve_lane, DL.at(n, "max", u))
                            nc.vector.scalar_tensor_tensor(out=XN[u][:], in0=pl[u][:].rearrange("p (k j) -> p k j", j=S), scalar=MASKED,
                                                           in1=bc(st["max"][:, u, :]), op0=ALU.max, op1=ALU.subtract).then_inc(dve_lane, 1)
                        for u in LN:
                            dve.wait_ge(act_lane, AL.at(n, "exp", u))
                            nc.vector.tensor_reduce(st["den"][:, u, :], XN[u][:], AX, ALU.add).then_inc(dve_lane, 1)
                        dve.wait_ge(dve_lane, DL.at(n, "den", LANES - 1))
                        nc.vector.reciprocal(st["rden"][:], st["den"][:]).then_inc(dve_lane, 1)
                        dve.wait_ge(dve_lane, DL.at(n, "rden"))
                        nc.vector.tensor_tensor(st["rq"][:], st["rden"][:], st["qrow"][:], ALU.mult).then_inc(dve_lane, 1)
                        for u in LN:
                            dve.wait_ge(dve_lane, DL.at(n, "rq"))
                            nc.vector.tensor_tensor(XN[u][:], XN[u][:], bc(st["rq"][:, u, :]), ALU.mult).then_inc(dve_lane, 1)
                        for u in LN:
                            dve.wait_ge(pe_lane, PL.at(n, "pv", u))
                            nc.vector.tensor_tensor(SEQ[u][:].rearrange("p t f -> p (t f)"), pl[u][:], QT[u][:], ALU.add).then_inc(dve_lane, 1)
                        for u in LN:
                            dve.wait_ge(pe_lane, PL.at(n, "xtok", u))
                            for t in range(TILES):
                                m = nc.vector.bn_stats(bn[:, u, t, :], pl[u][:, t * D:(t + 1) * D])
                            m.then_inc(dve_lane, 1)
                        var_steps(n, "2")
                        for u in LN:
                            nc.vector.scalar_tensor_tensor(out=XN[u][:], in0=bc(st["sum"][:, u, :]), scalar=-0.5,
                                                           in1=pl[u][:].rearrange("p (t f) -> p t f", f=D),
                                                           op0=ALU.mult, op1=ALU.add).then_inc(dve_lane, 1)
                        newton_steps(n, "2")
                        for u in LN:
                            dve.wait_ge(dve_lane, DL.at(n, "2rstd"))
                            nc.vector.tensor_tensor(XN[u][:], XN[u][:], bc(st["rstd"][:, u, :]), ALU.mult).then_inc(dve_lane, 1)
                        for u in LN:
                            dve.wait_ge(pe_lane, PL.at(n, "o", u))
                            nc.vector.scalar_tensor_tensor(out=S2T[u][:], in0=pl[u][:], scalar=col[:, 8:9], in1=QT[u][:],
                                                           op0=ALU.add, op1=ALU.add).then_inc(dve_lane, 1)
                        rows_dve(dve, n)


        ph1.close()
        with ExitStack() as ph2:
            def sb2(name, shape, dt=F32):
                return ph2.enter_context(nc.sbuf_tensor("s_" + name, shape, dt))

            embT = sb2("embT", [P, NO], F32R)
            ident2 = sb2("ident2", [P, P])
            raw = [sb2(f"raw{b}", [ER, EL, D]) for b in range(2)]
            split = [sb2(f"split{b}", [ER, EL, 2 * D]) for b in range(2)]
            hi_now = sb2("hi_now", [P, P], F32R)
            lo_now = sb2("lo_now", [P, P], F32R)
            outs = [sb2(f"outs{b}", [P, DSL * NSL]) for b in range(2)]
            ps = [ph2.enter_context(nc.psum_tensor(f"ps{b}", [P, 512], F32)) for b in range(DSL)]

            id_in = sem("id_in")
            raw_in = [sem(f"raw_in{b}") for b in range(2)]
            split_hi = sem("split_hi")
            split_lo = sem("split_lo")
            turned = sem("turned")
            emb_put = sem("emb_put")
            emb_rows = out_emb.rearrange("(n b a p) f -> n b p a f", b=2, a=EL, p=ER)
            NE = NO // (ER * EL * 2)
            with nc.Block() as block:
                @block.sync
                def _(sp):
                    sp.dma_start(ident2[:], const[:, 0:P]).then_inc(id_in, 16)
                    with sp.Fori(0, NE) as n:
                        for b in range(2):
                            sp.wait_ge(split_lo, n * 2)
                            sp.dma_start(raw[b][:], emb_rows[bass.ds(n, 1), b].rearrange("n p a f -> (n p) a f")).then_inc(raw_in[b], 16)

                @block.vector
                def _(dve):
                    with dve.Fori(0, NE) as n:
                        for b in range(2):
                            dve.wait_ge(raw_in[b], n * 16 + 16)
                            dve.wait_ge(turned, n * 2)
                            nc.vector.tensor_copy(split[b][:, :, 0:D].bitcast(F32R), raw[b][:]).then_inc(split_hi, 1)
                            dve.wait_ge(split_hi, n * 2 + b + 1)
                            nc.vector.tensor_tensor(split[b][:, :, D:2 * D], raw[b][:], split[b][:, :, 0:D], ALU.subtract).then_inc(split_lo, 1)

                @block.tensor
                def _(pe):
                    pe.wait_ge(id_in, 16)
                    with pe.Fori(0, NE) as n:
                        for b in range(2):
                            pe.wait_ge(split_lo, n * 2 + b + 1)
                            pe.wait_ge(emb_put, n * 2)
                            for a in range(EL):
                                m = nc.tensor.transpose(ps[b][:, a * ER:(a + 1) * ER], split[b][:, a, :], ident2[0:ER, 0:ER])
                            m.then_inc(turned, 1)

                @block.scalar
                def _(act):
                    with act.Fori(0, NE) as n:
                        for b in range(2):
                            act.wait_ge(turned, n * 2 + b + 1)
                            nc.scalar.activation(embT[:, bass.ds(n * (2 * EL * ER) + b * EL * ER, EL * ER)],
                                                 ps[b][:, 0:EL * ER], ACT.Copy).then_inc(emb_put, 1)

            ROUNDS = STORES // 2
            now_hi = sem("now_hi")
            now_lo = sem("now_lo")
            product = sem("product")
            left = [sem(f"left{b}") for b in range(DSL)]
            stored = [sem(f"stored{b}") for b in range(2)]
            on_act = [k for k in range(2 * DSL) if k % DSL % 2 == 0]
            on_dve = [k for k in range(2 * DSL) if k % DSL % 2 == 1]
            out_g = out.rearrange("(g p) c -> g p c", p=P)
            with nc.Block() as block:
                @block.tensor
                def _(pe):
                    with pe.Fori(0, GROUPS) as g:
                        with pe.Fori(0, ROUNDS) as r:
                            q = g * ROUNDS + r
                            for k in range(2 * DSL):
                                if k == 0:
                                    pe.wait_ge(now_lo, g + 1)
                                pe.wait_ge(left[k % DSL], q * 2 + k // DSL)
                                e = embT[:, bass.ds(r * (2 * DSL * NSL) + k * NSL, NSL)]
                                nc.tensor.matmul(ps[k % DSL][:, 0:NSL], hi_now[:], e, start=True, stop=False)
                                nc.tensor.matmul(ps[k % DSL][:, 0:NSL], lo_now[:], e, start=False, stop=True).then_inc(product, 1)

                @block.scalar
                def _(act):
                    with act.Fori(0, GROUPS) as g:
                        with act.Fori(0, ROUNDS) as r:
                            q = g * ROUNDS + r
                            for k in on_act:
                                if k in (0, DSL):
                                    act.wait_ge(stored[k // DSL], q * 16)
                                act.wait_ge(product, q * (2 * DSL) + k + 1)
                                nc.scalar.activation(outs[k // DSL][:, k % DSL * NSL:(k % DSL + 1) * NSL], ps[k % DSL][:, 0:NSL],
                                                     ACT.Copy).then_inc(left[k % DSL], 1)

                @block.vector
                def _(dve):
                    with dve.Fori(0, GROUPS) as g:
                        dve.wait_ge(product, g * (2 * DSL * ROUNDS))
                        nc.vector.tensor_copy(hi_now[:], hid_hi[:, bass.ds(g * P, P)].bitcast(F32)).then_inc(now_hi, 1)
                        nc.vector.tensor_copy(lo_now[:], hid_lo[:, bass.ds(g * P, P)].bitcast(F32)).then_inc(now_lo, 1)
                        with dve.Fori(0, ROUNDS) as r:
                            q = g * ROUNDS + r
                            for k in on_dve:
                                if k in (1, DSL + 1):
                                    dve.wait_ge(stored[k // DSL], q * 16)
                                dve.wait_ge(product, q * (2 * DSL) + k + 1)
                                nc.vector.tensor_copy(outs[k // DSL][:, k % DSL * NSL:(k % DSL + 1) * NSL],
                                                      ps[k % DSL][:, 0:NSL]).then_inc(left[k % DSL], 1)

                @block.sync
                def _(sp):
                    with sp.Fori(0, GROUPS) as g:
                        with sp.Fori(0, ROUNDS) as r:
                            q = g * ROUNDS + r
                            for b in range(2):
                                for k in range(DSL):
                                    sp.wait_ge(left[k], q * 2 + b + 1)
                                sp.dma_start(out_g[bass.ds(g, 1), :, bass.ds(r * (2 * DSL * NSL) + b * DSL * NSL, DSL * NSL)].rearrange("g p c -> (g p) c"),
                                             outs[b][:]).then_inc(stored[b], 16)
                    for b in range(2):
                        sp.wait_ge(stored[b], 16 * GROUPS * ROUNDS)


def _constants():
    import numpy as np

    p = np.arange(P)
    half, i = p // 64, p % 64
    ident = np.eye(P)
    key = np.arange(512)
    later = (key[None, :] % 64 > i[:, None])
    r = p % 32
    col_t = 2 * (key // P) + (key % P) // 64
    ksel = (r[:, None] == col_t[None, :]) & (r[:, None] < 8)
    lane, rs, rt = p // 32, (p % 32) // 8, p % 8
    used = (p % 32) < 16
    rsel = (lane[:, None] == lane[None, :]) & (r[:, None] == 16 + (rt % 2)[None, :]) & used[None, :]
    same = (rt[:, None] // 2 == key[None, :] // P) & (rs[:, None] == (key[None, :] % P) // 64)
    other = ~same & used[:, None]
    abrow = (half[:, None] == (rt % 2)[None, :]) & used[None, :]
    ab01 = (rt[:, None] % 2 == np.arange(2)[None, :])
    parts = [ident, MASKED * ident, later, MASKED * ksel, MASKED * rsel, other, abrow, ab01]
    return np.concatenate([np.asarray(x, np.float32) for x in parts], axis=1)


def kernel(**inputs):
    import numpy as np
    import concourse.bacc as bacc
    from concourse.bass_utils import run_bass_kernel_spmd

    x = {k.replace("L0_rec_", ""): np.asarray(v) for k, v in inputs.items()}
    two = lambda v: np.concatenate([v, v])
    cols = np.stack([two(v) for v in (x["ln1_g"][0], x["ln1_b"][0], x["ln2_g"][0], x["ln2_b"][0], x["b1"][0],
                                      x["bq"][0], x["bq"][1], x["b1"][1], x["b2"][0])], axis=1)
    rows = np.stack([x["ln1_g"][0], x["ln1_b"][0], x["bv"][0], x["ln1_g"][1], x["ln1_b"][1], x["bv"][1],
                     x["ln2_g"][1], x["ln2_b"][1], x["b2"][1], x["lnf_g"], x["lnf_b"]])
    arrays = {
        "ids": x["r_input_ids"], "item_emb": x["item_emb"], "pos_emb": x["pos_emb"],
        "wqT": x["Wq"].transpose(0, 2, 1), "wkT": x["Wk"].transpose(0, 2, 1), "wv": x["Wv"], "w1": x["W1"], "w2": x["W2"],
        "cols": cols, "rows": rows, "out_emb": x["out_item_emb"], "const": _constants(),
    }
    arrays = {k: np.ascontiguousarray(v) for k, v in arrays.items()}
    nc = bacc.Bacc("TRN2", target_bir_lowering=False, num_devices=1)
    aps = [nc.dram_tensor(f"in_{k}", v.shape, mybir.dt.from_np(v.dtype), kind="ExternalInput").ap() for k, v in arrays.items()]
    shape = (x["r_input_ids"].shape[0], x["out_item_emb"].shape[0])
    out = nc.dram_tensor("out_scores", shape, F32, kind="ExternalOutput").ap()
    recommender(nc, *aps, out)
    r = run_bass_kernel_spmd(nc, [{f"in_{k}": v for k, v in arrays.items()}], core_ids=[0])
    return r.results[0]["out_scores"]
```

```python
from contextlib import ExitStack

import concourse.bass as bass
from concourse import mybir

F32 = mybir.dt.float32
F32R = mybir.dt.float32r
BF16 = mybir.dt.bfloat16
I32 = mybir.dt.int32
ALU = mybir.AluOpType
ACT = mybir.ActivationFunctionType
AX = mybir.AxisListType.X

P = 128
LANES = 4
WIDE = 2
TILES = 8
PAIRS = TILES // 2
EPS = 1e-3
SEED = float(0x5F3759DF + 0xCB0000)
MASKED = -(2.0 ** 100)


class Steps:

    def __init__(self, sem, names):
        self.sem = sem
        self.per_pass = len(names)
        self.index = {name: i + 1 for i, name in enumerate(names)}
        assert len(self.index) == len(names)

    def at(self, n, *name):
        return n * self.per_pass + self.index[name]

    def start(self, n):
        return n * self.per_pass


def each(*names):
    return [(name, v) for name in names for v in range(WIDE)]


CHAIN = ("sum", "diff", "m2", "spread", "var64", "seed", "half", "times", "newton", "e1", "e2", "poly", "rstd")


def norm_steps(k):
    return [(name + "_" + k,) for name in CHAIN]


def recommender(nc, ids, item_emb, pos_emb, wqT, wkT, wv, w1, w2, cols, rows, out_emb, const, out):
    B, S = ids.shape
    NI, D = item_emb.shape
    NO = out_emb.shape[0]
    MASK_ID = NI - 1
    assert S == 64 and D == 64 and B % P == 0
    BATCH = 16 * LANES
    PASSES = B // BATCH
    T = B * S // P
    GROUPS = B // P
    TQ = T // P if T >= P else 1
    TR = min(T, P)
    NSL = 500
    DSL = 5
    STORES = NO // (NSL * DSL)
    ER = 125
    EL = 4
    ELOADS = NO // (ER * EL)
    assert NO % (NSL * DSL) == 0 and NO % (ER * EL) == 0

    ctx = ExitStack()
    with ctx:
        def sem(name):
            return ctx.enter_context(nc.semaphore(name))

        hid_hi = ctx.enter_context(nc.sbuf_tensor("s_hid_hi", [P, B], F32R))
        hid_lo = ctx.enter_context(nc.sbuf_tensor("s_hid_lo", [P, B], F32R))
        ph1 = ctx.enter_context(ExitStack())

        def sb(name, shape, dt=F32):
            return ph1.enter_context(nc.sbuf_tensor("s_" + name, shape, dt))

        ident = sb("ident", [P, P])
        maskid = sb("maskid", [P, P], BF16)
        ones_b = sb("ones_b", [P, P], BF16)
        later = sb("later", [P, 512], BF16)
        ksel = sb("ksel", [P, 512], BF16)
        rsel = sb("rsel", [P, P], BF16)
        other = sb("other", [P, 512], BF16)
        abrow = sb("abrow", [P, P])
        ab01 = sb("ab01", [P, 2])
        cstage = sb("cstage", [P, 512])
        bd = {k: sb("bd_" + k, [P, P]) for k in ("m", "v", "w1", "w2", "w1b", "w2b")}
        gpair = sb("gpair", [P, 2])
        col = sb("col", [P, cols.shape[1]])
        row = sb("row", [P, rows.shape[0], D])
        wq_s = sb("wq_s", [D, 2, D])
        wk_s = sb("wk_s", [D, 2, 2 * D])
        wq_d = sb("wq_d", [D, 2, 2 * D])
        m2dup = sb("m2dup", [D, P])
        cbias = sb("cbias", [P, 2])
        wv2 = sb("wv2", [D, D])
        bv3 = sb("bv3", [P, 512], BF16)
        bvt = sb("bvt", [P, 4, D])
        bvb = sb("bvb", [P, 3, D], BF16)
        gsum = sb("gsum", [P, 2])

        idx_all = sb("idx_all", [P, T], I32)
        kept_all = sb("kept_all", [P, T])
        last_i = sb("last_i", [P, PASSES], I32)
        last_all = sb("last_all", [P, PASSES])

        LN = range(LANES)
        GR = range(LANES // WIDE)
        X = [sb(f"XIN{u}", [P, TILES, D]) for u in LN]
        SEQ = [sb(f"SEQ{u}", [P, TILES, D]) for u in LN]
        RES = [sb(f"RES{u}", [P, TILES, D]) for u in LN]
        XN = [sb(f"XN{u}", [P, TILES, D]) for u in LN]
        KT = [sb(f"KT{u}", [P, 512]) for u in LN]
        QT = [sb(f"QT{u}", [P, 512]) for u in LN]
        BLK = [sb(f"BLK{u}", [P, TILES, P]) for u in LN]
        V = [sb(f"V{u}", [P, TILES, D]) for u in LN]
        S2T = [sb(f"S2T{u}", [P, 512]) for u in LN]
        S2N = [sb(f"S2N{u}", [P, TILES, D]) for u in LN]
        idx_now = [sb(f"idx_now{u}", [P, TILES], I32) for u in LN]
        bn = sb("bn", [P, LANES, TILES, 6])
        st = {k: sb("st_" + k, [P, LANES, TILES]) for k in
              ("sum", "diff", "m2", "spread", "var64", "rho", "tmp", "poly", "rstd", "max", "den", "rden", "rq", "qs", "qsr", "qtok", "qrow")}
        bnz = sb("bnz", [P, LANES, TILES, 6])
        sz = {k: sb("sz_" + k, [P, LANES, TILES]) for k in
              ("sum", "diff", "m2", "spread", "var64", "rho", "tmp", "poly", "rstd")}
        kflag = [sb(f"kflag{g}", [P, LANES, 32]) for g in GR]
        kflagT = [sb(f"kflagT{g}", [P, P], BF16) for g in GR]

        XL = sb("XL", [P, D])
        XLM = sb("XLM", [P, D])
        last_now = sb("last_now", [P, 1])
        kept_now = sb("kept_now", [P, LANES * TILES])
        rbn = sb("rbn", [P, 6])
        rs = {k: sb("rs_" + k, [P, 1]) for k in
              ("sum", "diff", "m2", "spread", "var64", "rho", "tmp", "poly", "rstd", "mean",
               "qsum", "qm", "max", "negmax", "den", "rden", "ra", "rb")}
        rhat = sb("rhat", [P, D])
        rgain = sb("rgain", [P, D])
        Q2w = sb("Q2w", [P, P])
        Q2 = Q2w[:, 0:D]
        rT = sb("rT", [D, P])
        G2B = sb("G2B", [P, LANES, 32])
        idrow = sb("idrow", [P, 512], I32)
        idflag = sb("idflag", [P, 512])
        flag2 = sb("flag2", [P, 512], BF16)
        P2 = sb("P2", [P, 512])
        P2T = sb("P2T", [P, PAIRS, P])
        A2w = sb("A2w", [P, P])
        A2 = A2w[:, 0:D]
        X2a = sb("X2a", [P, D])
        X2 = ph1.enter_context(nc.sbuf_tensor("s_X2", [P, PASSES, D], F32))

        pl = [ph1.enter_context(nc.psum_tensor(f"pl{u}", [P, 512], F32)) for u in LN]
        pr = ph1.enter_context(nc.psum_tensor("pr", [P, 512], F32))
        pr2 = ph1.enter_context(nc.psum_tensor("pr2", [P, 512], F32))
        pg = [ph1.enter_context(nc.psum_tensor(f"pg{g}", [P, 512], F32)) for g in GR]

        loaded = sem("loaded")
        stage_in = sem("stage_in")
        set_dve = sem("set_dve")
        set_pe = sem("set_pe")
        set_act = sem("set_act")
        prefilled = [sem(f"prefilled{u}") for u in LN]
        cleared = sem("cleared")
        idx_copied = sem("idx_copied")
        gathered = [sem(f"gathered{u}") for u in LN]
        tokens_in = sem("tokens_in")
        ids_in_rows = sem("ids_in_rows")
        seq_made = sem("seq_made")
        dve_z = [sem(f"dve_z{g}") for g in GR]
        dve_g = [sem(f"dve_g{g}") for g in GR]
        act_g = [sem(f"act_g{g}") for g in GR]
        pe_g = [sem(f"pe_g{g}") for g in GR]
        dve_row = sem("dve_row")
        act_row = sem("act_row")
        pe_row = sem("pe_row")

        dve_steps = (each("cen1", "hat1") + [("qs",), ("qsr",), ("qtok",)] + [("qrow", k) for k in range(4)]
                     + [(name, v) for v in range(WIDE) for name in ("max", "shift")]
                     + [(name, v) for v in range(WIDE) for name in ("den", "rden", "rq", "prob")]
                     + each("res1", "bn2") + norm_steps("2") + each("cen2", "hat2", "seq2"))
        act_steps = (each("keyT") + [("kflagT",)] + each("qT") + [(h, v) for v in range(WIDE) for h in ("gA", "gB")]
                     + each("v", "exp") + [(h, v) for v in range(WIDE) for h in ("pA", "pB")] + each("yT", "hT", "s2N"))
        pe_steps = each("keyT") + [("kflagT",)] + each("hatT", "g", "v", "s", "pT", "pv", "xtok", "yT", "h", "o", "s2N")
        DZ = [Steps(dve_z[g], each("bn1") + norm_steps("1") + [("kflag",)]) for g in GR]
        DL = [Steps(dve_g[g], dve_steps) for g in GR]
        AL = [Steps(act_g[g], act_steps) for g in GR]
        PL = [Steps(pe_g[g], pe_steps) for g in GR]
        DR = Steps(dve_row, [("now",), ("kept",), ("idflag",), ("xlm",), ("abn",)] + norm_steps("a")
                   + [("mean",), ("hat",), ("gain",), ("q",), ("qsum",), ("qm",), ("g2",), ("flag2",),
                      ("max",), ("negmax",), ("rden",), ("ra",), ("rb",)] + [("p2T", k) for k in range(PAIRS)]
                   + [("a2a",), ("a2",), ("x2a",), ("x2",)])
        AR = Steps(act_row, [("qT",), ("exp",), ("a2T",)])
        PR = Steps(pe_row, [("qT",), ("g2",), ("s2",), ("flag",), ("p2T",), ("a2",), ("a2T",), ("o2",)])

        ids_tiles = ids.rearrange("b s -> (b s)").rearrange("(q r p) -> r q p", r=TR, p=P)
        ids_rows = ids.rearrange("b s -> (b s)").rearrange("(c x a p) -> c a x p", x=PAIRS, a=2, p=P)
        ids_last = ids.rearrange("(n u t s) j -> u s t n j", u=LANES, t=TILES, s=2)

        def bc(ap, w=D):
            return ap.unsqueeze(2).broadcast_to([ap.shape[0], ap.shape[1], w])

        negpos = sb("negpos", [P, TILES, D])
        with ExitStack() as setup:
            ids_in = setup.enter_context(nc.sbuf_tensor("s_ids_in", [P, TQ, P], I32))
            idf = setup.enter_context(nc.sbuf_tensor("s_idf", [P, TQ, P], F32))
            idn = setup.enter_context(nc.sbuf_tensor("s_idn", [P, TQ, P], F32))
            LOADS = 22
            CW = [("ident", P), ("maskid", P), ("later", 512), ("ksel", 512), ("rsel", P), ("other", 512), ("abrow", P), ("ab01", 2)]
            with nc.Block() as block:
                @block.sync
                def _(sp):
                    off = 0
                    for k, (name, w) in enumerate(CW):
                        if k:
                            sp.wait_ge(set_act, k)
                        sp.dma_start(cstage[:, 0:w], const[:, off:off + w]).then_inc(stage_in, 16)
                        off += w

                @block.scalar
                def _(act):
                    tiles = {"ident": ident, "maskid": maskid, "later": later, "ksel": ksel, "rsel": rsel,
                             "other": other, "abrow": abrow, "ab01": ab01}
                    for k, (name, w) in enumerate(CW):
                        act.wait_ge(stage_in, 16 * (k + 1))
                        nc.scalar.activation(tiles[name][:], cstage[:, 0:w], ACT.Copy).then_inc(set_act, 1)
                    N0 = len(CW)
                    act.wait_ge(set_pe, 4)
                    nc.scalar.activation(bd["m"][0:D, 0:D], pr[0:D, 0:D], ACT.Copy, scale=0.125).then_inc(set_act, 1)
                    nc.scalar.activation(bd["m"][D:P, D:P], pr[D:P, 0:D], ACT.Copy, scale=0.125).then_inc(set_act, 1)
                    nc.scalar.activation(m2dup[:, 0:D], pr[0:D, 64:128], ACT.Copy, scale=0.125).then_inc(set_act, 1)
                    nc.scalar.activation(m2dup[:, D:P], pr[0:D, 64:128], ACT.Copy, scale=0.125).then_inc(set_act, 1)
                    nc.scalar.activation(cbias[:, :], pr[:, 128:130], ACT.Copy, scale=0.125).then_inc(set_act, 1)
                    act.wait_ge(set_act, N0 + 5)

                @block.gpsimd
                def _(pool):
                    zeros = (bd["m"], bd["v"], bd["w1"], bd["w2"], gpair, G2B, idrow, bv3, last_i, P2T, kflag[0], kflag[1], XL, Q2w, A2w, X2, bd["w1b"], bd["w2b"])
                    for t in zeros:
                        nc.gpsimd.memset(t[:], 0).then_inc(cleared, 1)
                    nc.gpsimd.memset(ones_b[:], 1.0).then_inc(cleared, 1)
                    CLEAR = len(zeros) + 1
                    for u in LN:
                        nc.gpsimd.memset(BLK[u][:], 0).then_inc(cleared, 1)
                    pool.wait_ge(cleared, CLEAR + LANES)
                    for ab in range(2):
                        for u in LN:
                            nc.gpsimd.memset(G2B[ab * D:ab * D + D, u, 16 + ab:17 + ab], 1.0).then_inc(cleared, 1)
                    pool.wait_ge(cleared, CLEAR + 3 * LANES)
                    h = slice
                    dma = [(bd["v"][0:D, 0:D], wv[0]), (bd["v"][D:P, D:P], wv[0]),
                           (bd["w1"][0:D, 0:D], w1[0]), (bd["w1"][D:P, D:P], w1[0]),
                           (bd["w2"][0:D, 0:D], w2[0]), (bd["w2"][D:P, D:P], w2[0]),
                           (bd["w1b"][0:D, 0:D], w1[1]), (bd["w1b"][D:P, D:P], w1[1]),
                           (bd["w2b"][0:D, 0:D], w2[1]), (bd["w2b"][D:P, D:P], w2[1]), (wv2[:], wv[1]),
                           (col[:], cols), (gpair[0:D, 0:1], cols[0:D, 0:1]), (gpair[D:P, 1:2], cols[D:P, 0:1]),
                           (wq_d[:, :, 0:D], wqT.rearrange("l d f -> d l f")), (wq_d[:, :, D:P], wqT.rearrange("l d f -> d l f")),
                           (wk_s[:, :, 0:D], wkT.rearrange("l d f -> d l f")), (wk_s[:, :, D:P], wkT.rearrange("l d f -> d l f")),
                           (row[:], rows.unsqueeze(0).broadcast_to([P, rows.shape[0], D])),
                           (SEQ[0][0:S, 0, :], pos_emb), (SEQ[0][S:P, 0, :], pos_emb),
                           (ids_in[0:TR], ids_tiles)]
                    assert len(dma) == LOADS
                    for dst, src in dma:
                        pool.dma_start(dst, src, allow_slow_non_contiguous=True).then_inc(loaded, 16)
                    for u in LN:
                        for s in range(2):
                            pool.dma_start(last_i[32 * u + 8 * s:32 * u + 8 * s + 8, :].unsqueeze(2), ids_last[u, s][:, :, S - 1:S],
                                           allow_slow_non_contiguous=True).then_inc(loaded, 16)
                    pool.wait_ge(loaded, 16 * (len(dma) + 2 * LANES))

                @block.tensor
                def _(pe):
                    pe.wait_ge(loaded, 16 * (LOADS + 2 * LANES))
                    nc.tensor.matmul(pr[:, 0:D], wq_d[:, 0, :], wk_s[:, 0, 0:D], start=True, stop=True).then_inc(set_pe, 1)
                    nc.tensor.matmul(pr[0:D, D:P], wq_d[:, 1, 0:D], wk_s[:, 1, 0:D], start=True, stop=True).then_inc(set_pe, 1)
                    for l in range(2):
                        nc.tensor.matmul(pr[:, P + l:P + l + 1], wk_s[:, l, :], col[0:D, 5 + l:6 + l], start=True, stop=True).then_inc(set_pe, 1)
                    pe.wait_ge(set_dve, 12)
                    pe.wait_ge(set_act, 1)
                    for q in range(TQ):
                        if q:
                            pe.wait_ge(set_dve, 12 + 2 * q)
                        nc.tensor.transpose(pl[0][:, 0:TR], idf[0:TR, q, :], ident[0:TR, 0:TR]).then_inc(set_pe, 1)
                        nc.tensor.transpose(pl[1][:, 0:TR], idn[0:TR, q, :], ident[0:TR, 0:TR]).then_inc(set_pe, 1)

                @block.vector
                def _(dve):
                    dve.wait_ge(loaded, 16 * (LOADS + 2 * LANES))
                    k = [0]

                    def done(ins):
                        ins.then_inc(set_dve, 1)
                        k[0] += 1
                        dve.wait_ge(set_dve, k[0])

                    done(nc.vector.tensor_copy(idf[0:TR], ids_in[0:TR]))
                    done(nc.vector.tensor_scalar(idn[0:TR], idf[0:TR], 0.0, float(NI), ALU.is_lt, ALU.mult))
                    done(nc.vector.tensor_tensor(idn[0:TR], idn[0:TR], idf[0:TR], ALU.add))
                    done(nc.vector.tensor_scalar(idn[0:TR], idn[0:TR], 0.0, float(NI - 1), ALU.max, ALU.min))
                    done(nc.vector.scalar_tensor_tensor(out=idf[0:TR], in0=idf[0:TR], scalar=float(MASK_ID), in1=idn[0:TR],
                                                        op0=ALU.is_equal, op1=ALU.add))
                    done(nc.vector.tensor_copy(idn[0:TR], ids_in[0:TR]))
                    done(nc.vector.tensor_scalar(idn[0:TR], idn[0:TR], float(MASK_ID), None, ALU.not_equal))
                    done(nc.vector.tensor_copy(last_all[:], last_i[:]))
                    done(nc.vector.tensor_scalar(last_all[:], last_all[:], float(MASK_ID), None, ALU.not_equal))
                    done(nc.vector.tensor_scalar(negpos[:, :, :], SEQ[0][:, 0, :].unsqueeze(1).broadcast_to([P, TILES, D]),
                                                 -1.0, None, ALU.mult))
                    done(nc.vector.tensor_reduce(gsum[:, 0:1], row[:, 0, :], AX, ALU.add))
                    done(nc.vector.tensor_reduce(gsum[:, 1:2], row[:, 1, :], AX, ALU.add))
                    assert k[0] == 12
                    for q in range(TQ):
                        dve.wait_ge(set_pe, 4 + 2 * q + 2)
                        done(nc.vector.tensor_copy(idx_all[:, q * TR:q * TR + TR], pl[0][:, 0:TR]))
                        done(nc.vector.tensor_copy(kept_all[:, q * TR:q * TR + TR], pl[1][:, 0:TR]))
                    done(nc.vector.tensor_scalar(gsum[:, 0:1], gsum[:, 0:1], -0.5, None, ALU.mult))
                    bv = row[:, 2, :]
                    done(nc.vector.tensor_copy(bvb[:, 0, :], bv))
                    done(nc.vector.tensor_copy(bvt[:, 0, :], bvb[:, 0, :]))
                    done(nc.vector.tensor_tensor(bvt[:, 1, :], bv, bvt[:, 0, :], ALU.subtract))
                    done(nc.vector.tensor_copy(bvb[:, 1, :], bvt[:, 1, :]))
                    done(nc.vector.tensor_copy(bvt[:, 2, :], bvb[:, 1, :]))
                    done(nc.vector.tensor_tensor(bvt[:, 3, :], bvt[:, 1, :], bvt[:, 2, :], ALU.subtract))
                    done(nc.vector.tensor_copy(bvb[:, 2, :], bvt[:, 3, :]))
                    for r in range(3):
                        done(nc.vector.tensor_copy(bv3[32 * r:32 * r + 1, :].rearrange("p (t f) -> p t f", f=D),
                                                   bvb[32 * r:32 * r + 1, r, :].unsqueeze(1).broadcast_to([1, TILES, D])))


        def flat(tile, lo=0, hi=512):
            return tile[:].rearrange("p t f -> p (t f)")[:, lo:hi]

        def turn(bank, tile):
            for x in range(PAIRS):
                m = nc.tensor.transpose(bank[:, x * P:(x + 1) * P], flat(tile, x * P, (x + 1) * P), ident[:])
            return m

        def half_pe(pe, first=None, second=None, zero=None, rows=None):
            if first is not None:
                g, n = first
                lanes = [(v, g * WIDE + v) for v in range(WIDE)]
                for v, u in lanes:
                    if not (isinstance(n, int) and n == 0):
                        pe.wait_ge(act_g[g], AL[g].start(n))
                    pe.wait_ge(seq_made, n * LANES + u + 1)
                    turn(pl[u], SEQ[u]).then_inc(pe_g[g], 1)
                pe.wait_ge(dve_z[g], DZ[g].at(n, "kflag"))
                nc.tensor.transpose(pg[g][:, 0:P], kflag[g][:].rearrange("p u t -> p (u t)"), ident[:]).then_inc(pe_g[g], 1)
            if second is not None:
                g2, n2 = second
                lanes2 = [(v, g2 * WIDE + v) for v in range(WIDE)]
                for v, u in lanes2:
                    pe.wait_ge(dve_g[g2], DL[g2].at(n2, "prob", v))
                    turn(pl[u], XN[u]).then_inc(pe_g[g2], 1)
            if first is not None:
                for v, u in lanes:
                    pe.wait_ge(act_g[g], AL[g].at(n, "keyT", v))
                    pe.wait_ge(dve_g[g], DL[g].at(n, "hat1", v))
                    turn(pl[u], XN[u]).then_inc(pe_g[g], 1)
            if second is not None:
                for v, u in lanes2:
                    pe.wait_ge(act_g[g2], AL[g2].at(n2, "pB", v))
                    for t in range(TILES):
                        ab, x = t % 2, t // 2
                        m = nc.tensor.matmul(pl[u][64 * ab:64 * ab + 64, x * P:(x + 1) * P], V[u][:, t, :], BLK[u][:, t, :],
                                             start=True, stop=True, skip_group_check=True)
                    m.then_inc(pe_g[g2], 1)
            if first is not None:
                for v, u in lanes:
                    pe.wait_ge(act_g[g], AL[g].at(n, "qT", v))
                    nc.tensor.matmul(pl[u][:], bd["m"][:], QT[u][:], start=True, stop=True).then_inc(pe_g[g], 1)
            if second is not None:
                for v, u in lanes2:
                    pe.wait_ge(dve_g[g2], DL[g2].at(n2, "res1", v))
                    turn(pl[u], RES[u]).then_inc(pe_g[g2], 1)

            def values(v, u):
                pe.wait_ge(act_g[g], AL[g].at(n, "gB", v))
                nc.tensor.matmul(pl[u][:], ones_b[:], bv3[:], start=True, stop=False, skip_group_check=True)
                for x in range(PAIRS):
                    c = P + v * TILES + 2 * x
                    nc.tensor.matmul(pl[u][:, x * P:(x + 1) * P], KT[u][:, x * P:(x + 1) * P], bd["v"][:],
                                     start=False, stop=(x == PAIRS - 1), skip_group_check=True)
                    m = nc.tensor.matmul(pg[g][:, c:c + 2], KT[u][:, x * P:(x + 1) * P], gpair[:],
                                         start=True, stop=True, skip_group_check=True)
                m.then_inc(pe_g[g], 1)

            def scores(v, u):
                pe.wait_ge(act_g[g], AL[g].at(n, "v", v))
                nc.tensor.matmul(pl[u][:], maskid[:], later[:], start=True, stop=False, skip_group_check=True)
                for x in range(PAIRS):
                    nc.tensor.matmul(pl[u][:, x * P:(x + 1) * P], ksel[32 * v:32 * v + TILES, x * P:(x + 1) * P],
                                     kflagT[g][32 * v:32 * v + TILES, :], start=False, stop=False, skip_group_check=True)
                for k in range(TILES):
                    m = nc.tensor.matmul(pl[u][:, k * S:(k + 1) * S], BLK[u][:, k, :], KT[u][:, k * S:(k + 1) * S],
                                         start=False, stop=(k == TILES - 1), skip_group_check=True)
                m.then_inc(pe_g[g], 1)

            if rows is not None:
                pe.wait_ge(dve_row, DR.at(rows, "q"))
                nc.tensor.transpose(pr2[:, 0:P], Q2w[:], ident[:]).then_inc(pe_row, 1)
            if first is not None:
                values(*lanes[0])
            if rows is not None:
                pe.wait_ge(act_row, AR.at(rows, "qT"))
                nc.tensor.matmul(pr2[:, P:2 * P], m2dup[:], rT[:], start=True, stop=True).then_inc(pe_row, 1)
            if first is not None:
                values(*lanes[1])
                scores(*lanes[0])
            if rows is not None:
                pe.wait_ge(dve_row, DR.at(rows, "g2"))
                for u in LN:
                    m = nc.tensor.matmul(pr[32 * u:32 * u + 32, :], G2B[:, u, :], S2T[u][:], start=True, stop=False, skip_group_check=True)
                m.then_inc(pe_row, 1)
            if first is not None:
                scores(*lanes[1])
            if rows is not None:
                pe.wait_ge(dve_row, DR.at(rows, "flag2"))
                nc.tensor.matmul(pr[:], rsel[:], flag2[:], start=False, stop=False, skip_group_check=True)
                nc.tensor.matmul(pr[:], maskid[:], other[:], start=False, stop=True, skip_group_check=True).then_inc(pe_row, 1)
            if second is not None:
                for v, u in lanes2:
                    pe.wait_ge(dve_g[g2], DL[g2].at(n2, "hat2", v))
                    turn(pl[u], XN[u]).then_inc(pe_g[g2], 1)
                for v, u in lanes2:
                    pe.wait_ge(act_g[g2], AL[g2].at(n2, "yT", v))
                    nc.tensor.matmul(pl[u][:], bd["w1"][:], QT[u][:], start=True, stop=True).then_inc(pe_g[g2], 1)
            if rows is not None:
                pe.wait_ge(act_row, AR.at(rows, "exp"))
                for x in range(PAIRS):
                    m = nc.tensor.transpose(pr[:, x * P:(x + 1) * P], P2[:, x * P:(x + 1) * P], ident[:])
                m.then_inc(pe_row, 1)
            if second is not None:
                for v, u in lanes2:
                    pe.wait_ge(act_g[g2], AL[g2].at(n2, "hT", v))
                    nc.tensor.matmul(pl[u][:], bd["w2"][:], KT[u][:], start=True, stop=True).then_inc(pe_g[g2], 1)
            if rows is not None:
                pe.wait_ge(dve_row, DR.at(rows, "p2T", PAIRS - 1))
                for u in LN:
                    for x in range(PAIRS):
                        m = nc.tensor.matmul(pr2[32 * u:32 * u + 32, 0:P], P2T[:, x, 32 * u:32 * u + 32],
                                             S2N[u][:, 2 * x:2 * x + 2, :].rearrange("p t f -> p (t f)"),
                                             start=(x == 0), stop=(x == PAIRS - 1), skip_group_check=True)
                m.then_inc(pe_row, 1)
                pe.wait_ge(dve_row, DR.at(rows, "a2"))
                nc.tensor.transpose(pr2[:, 0:P], A2w[:], ident[:]).then_inc(pe_row, 1)
            if second is not None:
                for v, u in lanes2:
                    pe.wait_ge(dve_g[g2], DL[g2].at(n2, "seq2", v))
                    for x in range(PAIRS):
                        m = nc.tensor.transpose(pl[u][:, x * P:(x + 1) * P], S2T[u][:, x * P:(x + 1) * P], ident[:])
                    m.then_inc(pe_g[g2], 1)
            if rows is not None:
                pe.wait_ge(act_row, AR.at(rows, "a2T"))
                nc.tensor.matmul(pr2[:, P:P + D], rT[:], wv2[:], start=True, stop=True).then_inc(pe_row, 1)

        def load_ids(act, n):
            for u in LN:
                act.dma_start(idrow[32 * u + 16:32 * u + 18, :].rearrange("a (x p) -> a x p", p=P),
                              ids_rows[bass.ds(n * LANES + u, 1)].rearrange("c a x p -> (c a) x p")).then_inc(ids_in_rows, 16)

        def half_act(act, first=None, second=None, zero=None, rows=None):
            if first is not None:
                g, n = first
                lanes = [(v, g * WIDE + v) for v in range(WIDE)]
                for v, u in lanes:
                    act.wait_ge(pe_g[g], PL[g].at(n, "keyT", v))
                    nc.scalar.activation(KT[u][:], pl[u][:], ACT.Copy).then_inc(act_g[g], 1)
                act.wait_ge(pe_g[g], PL[g].at(n, "kflagT"))
                nc.scalar.activation(kflagT[g][:], pg[g][:, 0:P], ACT.Copy).then_inc(act_g[g], 1)
            if second is not None:
                g2, n2 = second
                lanes2 = [(v, g2 * WIDE + v) for v in range(WIDE)]
                for v, u in lanes2:
                    act.wait_ge(pe_g[g2], PL[g2].at(n2, "pT", v))
                    for s in range(2):
                        h = slice(64 * s, 64 * s + 64)
                        nc.scalar.activation(BLK[u][h, :, h], pl[u][h, :].rearrange("p (k i) -> p k i", i=S),
                                             ACT.Copy).then_inc(act_g[g2], 1)
            if first is not None:
                for v, u in lanes:
                    act.wait_ge(pe_g[g], PL[g].at(n, "hatT", v))
                    nc.scalar.activation(QT[u][:], pl[u][:], ACT.Identity, scale=col[:, 0:1], bias=col[:, 1:2]).then_inc(act_g[g], 1)
                for v, u in lanes:
                    act.wait_ge(pe_g[g], PL[g].at(n, "g", v))
                    for ab in range(2):
                        h = slice(64 * ab, 64 * ab + 64)
                        nc.scalar.activation(BLK[u][h, :, h], pl[u][h, :].rearrange("p (k i) -> p k i", i=S),
                                             ACT.Identity, bias=cbias[h, 0:1]).then_inc(act_g[g], 1)
            if rows is not None:
                act.wait_ge(pe_row, PR.at(rows, "qT"))
                nc.scalar.activation(rT[:], pr2[0:D, 0:P], ACT.Copy).then_inc(act_row, 1)
            if first is not None:
                for v, u in lanes:
                    act.wait_ge(pe_g[g], PL[g].at(n, "v", v))
                    nc.scalar.activation(V[u][:], pl[u][:], ACT.Copy).then_inc(act_g[g], 1)
            if second is not None:
                for v, u in lanes2:
                    act.wait_ge(pe_g[g2], PL[g2].at(n2, "yT", v))
                    nc.scalar.activation(QT[u][:], pl[u][:], ACT.Identity, scale=col[:, 2:3], bias=col[:, 3:4]).then_inc(act_g[g2], 1)
            if rows is not None:
                act.wait_ge(dve_row, DR.at(rows, "negmax"))
                nc.scalar.activation(P2[:], pr[:], ACT.Exp, bias=rs["negmax"][:, 0:1], accum_out=rs["den"][:, 0:1]).then_inc(act_row, 1)
                if not (isinstance(rows, int) and rows == LAST):
                    load_ids(act, rows + 1)
            if second is not None:
                for v, u in lanes2:
                    act.wait_ge(pe_g[g2], PL[g2].at(n2, "h", v))
                    nc.scalar.activation(KT[u][:], pl[u][:], ACT.Relu, bias=col[:, 4:5]).then_inc(act_g[g2], 1)
            if first is not None:
                for v, u in lanes:
                    act.wait_ge(dve_g[g], DL[g].at(n, "shift", v))
                    nc.scalar.activation(XN[u][:], XN[u][:], ACT.Exp).then_inc(act_g[g], 1)
            if rows is not None:
                act.wait_ge(pe_row, PR.at(rows, "a2T"))
                nc.scalar.activation(rT[:], pr2[0:D, 0:P], ACT.Copy).then_inc(act_row, 1)
            if second is not None:
                for v, u in lanes2:
                    act.wait_ge(pe_g[g2], PL[g2].at(n2, "s2N", v))
                    nc.scalar.activation(S2N[u][:], pl[u][:], ACT.Copy).then_inc(act_g[g2], 1)
                for v, u in lanes2:
                    act.wait_ge(act_g[g2], AL[g2].at(n2, "s2N", v))
                    for s in range(2):
                        r = 32 * u + 8 * s
                        act.dma_start(XL[r:r + 8, :], S2N[u][64 * s + 63:64 * s + 64, :, :]).then_inc(tokens_in, 16)

        def norm_step(dve, name, b, e, sem, at):
            if name == "sum":
                m = nc.vector.tensor_tensor(b["sum"], e(1), e(4), ALU.add)
            elif name == "diff":
                m = nc.vector.tensor_tensor(b["diff"], e(1), e(4), ALU.subtract)
            elif name == "m2":
                m = nc.vector.tensor_tensor(b["m2"], e(2), e(5), ALU.add)
            elif name == "spread":
                dve.wait_ge(sem, at("diff"))
                m = nc.vector.scalar_tensor_tensor(out=b["spread"], in0=b["diff"], scalar=16.0, in1=b["diff"], op0=ALU.mult, op1=ALU.mult)
            elif name == "var64":
                dve.wait_ge(sem, at("spread"))
                m = nc.vector.scalar_tensor_tensor(out=b["var64"], in0=b["m2"], scalar=64 * EPS, in1=b["spread"], op0=ALU.add, op1=ALU.add)
            elif name == "seed":
                dve.wait_ge(sem, at("var64"))
                m = nc.vector.tensor_scalar(b["rho"].bitcast(I32), b["var64"].bitcast(I32), -0.5, SEED, ALU.mult, ALU.add)
            elif name == "half":
                dve.wait_ge(sem, at("seed"))
                m = nc.vector.scalar_tensor_tensor(out=b["tmp"], in0=b["rho"], scalar=-1.0 / 18, in1=b["rho"], op0=ALU.mult, op1=ALU.mult)
            elif name == "times":
                dve.wait_ge(sem, at("half"))
                m = nc.vector.tensor_tensor(b["tmp"], b["tmp"], b["var64"], ALU.mult)
            elif name == "newton":
                dve.wait_ge(sem, at("times"))
                m = nc.vector.scalar_tensor_tensor(out=b["rho"], in0=b["tmp"], scalar=1.5, in1=b["rho"], op0=ALU.add, op1=ALU.mult)
            elif name == "e1":
                dve.wait_ge(sem, at("newton"))
                m = nc.vector.scalar_tensor_tensor(out=b["tmp"], in0=b["rho"], scalar=1.0 / 9, in1=b["var64"], op0=ALU.mult, op1=ALU.mult)
            elif name == "e2":
                dve.wait_ge(sem, at("e1"))
                m = nc.vector.tensor_tensor(b["tmp"], b["tmp"], b["rho"], ALU.mult)
            elif name == "poly":
                dve.wait_ge(sem, at("e2"))
                m = nc.vector.scalar_tensor_tensor(out=b["poly"], in0=b["tmp"], scalar=-10.0 / 3, in1=b["tmp"], op0=ALU.add, op1=ALU.mult)
            else:
                dve.wait_ge(sem, at("poly"))
                m = nc.vector.scalar_tensor_tensor(out=b["rstd"], in0=b["poly"], scalar=5.0, in1=b["rho"], op0=ALU.add, op1=ALU.mult)
            m.then_inc(sem, 1)

        def half_dve(dve, first=None, second=None, zero=None, rows=None):
            if first is not None:
                g, n = first
                lanes = [(v, g * WIDE + v) for v in range(WIDE)]
                mine = slice(g * WIDE, (g + 1) * WIDE)
                for v, u in lanes:
                    dve.wait_ge(dve_z[g], DZ[g].at(n, "rstd_1"))
                    nc.vector.scalar_tensor_tensor(out=XN[u][:], in0=bc(sz["sum"][:, u, :]), scalar=-0.5, in1=SEQ[u][:],
                                                   op0=ALU.mult, op1=ALU.add).then_inc(dve_g[g], 1)
                for v, u in lanes:
                    dve.wait_ge(dve_g[g], DL[g].at(n, "cen1", v))
                    nc.vector.tensor_tensor(XN[u][:], XN[u][:], bc(sz["rstd"][:, u, :]), ALU.mult).then_inc(dve_g[g], 1)
            if second is not None:
                g2, n2 = second
                lanes2 = [(v, g2 * WIDE + v) for v in range(WIDE)]
                mine2 = slice(g2 * WIDE, (g2 + 1) * WIDE)
            if zero is not None:
                g0, n0 = zero
                lanes0 = [(v, g0 * WIDE + v) for v in range(WIDE)]
                mine0 = slice(g0 * WIDE, (g0 + 1) * WIDE)

            def token_stats(v, u):
                dve.wait_ge(seq_made, n0 * LANES + u + 1)
                for t in range(TILES):
                    m = nc.vector.bn_stats(bnz[:, u, t, :], SEQ[u][:, t, :])
                m.then_inc(dve_z[g0], 1)

            def residual(v, u):
                dve.wait_ge(pe_g[g2], PL[g2].at(n2, "pv", v))
                nc.vector.tensor_tensor(flat(RES[u]), pl[u][:], QT[u][:], ALU.add).then_inc(dve_g[g2], 1)

            def center(v, u):
                nc.vector.scalar_tensor_tensor(out=XN[u][:], in0=bc(st["sum"][:, u, :]), scalar=-0.5,
                                               in1=pl[u][:].rearrange("p (t f) -> p t f", f=D),
                                               op0=ALU.mult, op1=ALU.add).then_inc(dve_g[g2], 1)

            def scale(v, u):
                dve.wait_ge(dve_g[g2], DL[g2].at(n2, "cen2", v))
                nc.vector.tensor_tensor(XN[u][:], XN[u][:], bc(st["rstd"][:, u, :]), ALU.mult).then_inc(dve_g[g2], 1)

            def next_sequence(v, u):
                dve.wait_ge(pe_g[g2], PL[g2].at(n2, "o", v))
                nc.vector.scalar_tensor_tensor(out=S2T[u][:], in0=pl[u][:], scalar=col[:, 8:9], in1=QT[u][:],
                                               op0=ALU.add, op1=ALU.add).then_inc(dve_g[g2], 1)

            def shifted_scores(v, u):
                dve.wait_ge(pe_g[g], PL[g].at(n, "s", v))
                nc.vector.tensor_reduce(st["max"][:, u, :], pl[u][:].rearrange("p (k j) -> p k j", j=S), AX, ALU.max).then_inc(dve_g[g], 1)
                dve.wait_ge(dve_g[g], DL[g].at(n, "max", v))
                nc.vector.scalar_tensor_tensor(out=XN[u][:], in0=pl[u][:].rearrange("p (k j) -> p k j", j=S), scalar=MASKED,
                                               in1=bc(st["max"][:, u, :]), op0=ALU.max, op1=ALU.subtract).then_inc(dve_g[g], 1)

            def softmax_weights(v, u):
                dve.wait_ge(act_g[g], AL[g].at(n, "exp", v))
                nc.vector.tensor_reduce(st["den"][:, u, :], XN[u][:], AX, ALU.add).then_inc(dve_g[g], 1)
                dve.wait_ge(dve_g[g], DL[g].at(n, "den", v))
                nc.vector.reciprocal(st["rden"][:, u, :], st["den"][:, u, :]).then_inc(dve_g[g], 1)
                dve.wait_ge(dve_g[g], DL[g].at(n, "rden", v))
                nc.vector.tensor_tensor(st["rq"][:, u, :], st["rden"][:, u, :], st["qrow"][:, u, :], ALU.mult).then_inc(dve_g[g], 1)
                dve.wait_ge(dve_g[g], DL[g].at(n, "rq", v))
                nc.vector.tensor_tensor(XN[u][:], XN[u][:], bc(st["rq"][:, u, :]), ALU.mult).then_inc(dve_g[g], 1)

            if zero is not None:
                token_stats(*lanes0[0])
            if rows is not None:
                nc.vector.tensor_copy(last_now[:], last_all[:, bass.ds(rows, 1)]).then_inc(dve_row, 1)
                nc.vector.tensor_copy(kept_now[:], kept_all[:, bass.ds(rows * (LANES * TILES), LANES * TILES)]).then_inc(dve_row, 1)
                dve.wait_ge(ids_in_rows, rows * (16 * LANES) + 16 * LANES)
                nc.vector.tensor_scalar(idflag[:], idrow[:], float(MASK_ID), None, ALU.is_equal).then_inc(dve_row, 1)
                dve.wait_ge(tokens_in, rows * (32 * LANES) + 32 * LANES)
                dve.wait_ge(dve_row, DR.at(rows, "now"))
                nc.vector.tensor_scalar(XLM[:], XL[:], last_now[:, 0:1], None, ALU.mult).then_inc(dve_row, 1)
                dve.wait_ge(dve_row, DR.at(rows, "xlm"))
                nc.vector.bn_stats(rbn[:], XLM[:]).then_inc(dve_row, 1)
                dve.wait_ge(dve_row, DR.at(rows, "abn"))
                for name in CHAIN:
                    norm_step(dve, name, {q: rs[q][:] for q in rs}, lambda i: rbn[:, i:i + 1], dve_row,
                              lambda step: DR.at(rows, step + "_a"))
                nc.vector.tensor_scalar(rs["mean"][:], rs["sum"][:], 0.5, None, ALU.mult).then_inc(dve_row, 1)
            if zero is not None:
                token_stats(*lanes0[1])
            if rows is not None:
                dve.wait_ge(dve_row, DR.at(rows, "mean"))
                nc.vector.tensor_scalar(rhat[:], XLM[:], rs["mean"][:, 0:1], rs["rstd"][:, 0:1], ALU.subtract, ALU.mult).then_inc(dve_row, 1)
            if second is not None:
                residual(*lanes2[0])
            if rows is not None:
                dve.wait_ge(dve_row, DR.at(rows, "hat"))
                nc.vector.tensor_tensor(rgain[:], rhat[:], row[:, 3, :], ALU.mult).then_inc(dve_row, 1)
            if second is not None:
                residual(*lanes2[1])
            if rows is not None:
                dve.wait_ge(dve_row, DR.at(rows, "gain"))
                nc.vector.tensor_tensor(Q2[:], rgain[:], row[:, 4, :], ALU.add).then_inc(dve_row, 1)
            if second is not None:
                for v, u in lanes2:
                    dve.wait_ge(pe_g[g2], PL[g2].at(n2, "xtok", v))
                    for t in range(TILES):
                        m = nc.vector.bn_stats(bn[:, u, t, :], pl[u][:, t * D:(t + 1) * D])
                    m.then_inc(dve_g[g2], 1)
            if rows is not None:
                dve.wait_ge(dve_row, DR.at(rows, "q"))
                nc.vector.tensor_reduce(rs["qsum"][:], Q2[:], AX, ALU.add).then_inc(dve_row, 1)
                dve.wait_ge(dve_row, DR.at(rows, "qsum"))
                nc.vector.tensor_scalar(rs["qm"][:], rs["qsum"][:], 0.0, None, ALU.not_equal).then_inc(dve_row, 1)
            if second is not None:
                dve.wait_ge(dve_g[g2], DL[g2].at(n2, "bn2", WIDE - 1))
            if zero is not None:
                dve.wait_ge(dve_z[g0], DZ[g0].at(n0, "bn1", WIDE - 1))
            for name in CHAIN:
                if second is not None:
                    norm_step(dve, name, {q: st[q][:, mine2, :] for q in sz}, lambda i: bn[:, mine2, :, i],
                              dve_g[g2], lambda step: DL[g2].at(n2, step + "_2"))
                if zero is not None:
                    norm_step(dve, name, {q: sz[q][:, mine0, :] for q in sz}, lambda i: bnz[:, mine0, :, i],
                              dve_z[g0], lambda step: DZ[g0].at(n0, step + "_1"))
                if rows is not None and name == "var64":
                    dve.wait_ge(pe_row, PR.at(rows, "g2"))
                    nc.vector.scalar_tensor_tensor(out=G2B[:, :, 0:16], in0=pr2[:, P:2 * P].rearrange("p (u r) -> p u r", r=32)[:, :, 0:16],
                                                   scalar=cbias[:, 1:2], in1=abrow[:].rearrange("p (u r) -> p u r", r=32)[:, :, 0:16],
                                                   op0=ALU.add, op1=ALU.mult).then_inc(dve_row, 1)
            if zero is not None:
                nc.vector.tensor_scalar(kflag[g0][:, 0:WIDE, 0:TILES], sz["sum"][:, mine0, :], 0.0, None, ALU.is_equal).then_inc(dve_z[g0], 1)
            if second is not None:
                center(*lanes2[0])
                center(*lanes2[1])
                scale(*lanes2[0])
                scale(*lanes2[1])
            if rows is not None:
                dve.wait_ge(dve_row, DR.at(rows, "idflag"))
                dve.wait_ge(pe_row, PR.at(rows, "s2"))
                nc.vector.scalar_tensor_tensor(out=flag2[:], in0=pr[:], scalar=0.0, in1=idflag[:],
                                               op0=ALU.is_equal, op1=ALU.max).then_inc(dve_row, 1)
            if first is not None:
                dve.wait_ge(pe_g[g], PL[g].at(n, "v", WIDE - 1))
                nc.vector.scalar_tensor_tensor(out=st["qs"][:, mine, :], in0=sz["sum"][:, mine, :], scalar=gsum[:, 0:1],
                                               in1=pg[g][:, P:P + WIDE * TILES].rearrange("p (u t) -> p u t", u=WIDE),
                                               op0=ALU.mult, op1=ALU.add).then_inc(dve_g[g], 1)
                dve.wait_ge(dve_g[g], DL[g].at(n, "qs"))
                nc.vector.tensor_tensor(st["qsr"][:, mine, :], st["qs"][:, mine, :], sz["rstd"][:, mine, :], ALU.mult).then_inc(dve_g[g], 1)
                dve.wait_ge(dve_g[g], DL[g].at(n, "qsr"))
                nc.vector.tensor_scalar(st["qtok"][:, mine, :], st["qsr"][:, mine, :], gsum[:, 1:2], 0.0, ALU.add, ALU.not_equal).then_inc(dve_g[g], 1)
                dve.wait_ge(dve_g[g], DL[g].at(n, "qtok"))
                for s in range(2):
                    for ab in range(2):
                        nc.vector.tensor_copy(st["qrow"][64 * ab:64 * ab + 64, mine, s::2],
                                              st["qtok"][64 * s:64 * s + 64, mine, ab::2]).then_inc(dve_g[g], 1)
                shifted_scores(*lanes[0])
            if rows is not None:
                dve.wait_ge(pe_row, PR.at(rows, "flag"))
                nc.vector.tensor_reduce(rs["max"][:], pr[:], AX, ALU.max).then_inc(dve_row, 1)
                dve.wait_ge(dve_row, DR.at(rows, "max"))
                nc.vector.tensor_scalar(rs["negmax"][:], rs["max"][:], -1.0, None, ALU.mult).then_inc(dve_row, 1)
            if first is not None:
                shifted_scores(*lanes[1])
                softmax_weights(*lanes[0])
            if rows is not None:
                dve.wait_ge(act_row, AR.at(rows, "exp"))
                nc.vector.reciprocal(rs["rden"][:], rs["den"][:]).then_inc(dve_row, 1)
                dve.wait_ge(dve_row, DR.at(rows, "rden"))
                nc.vector.tensor_tensor(rs["ra"][:], rs["rden"][:], ab01[:, 0:1], ALU.mult).then_inc(dve_row, 1)
                nc.vector.tensor_tensor(rs["rb"][:], rs["rden"][:], ab01[:, 1:2], ALU.mult).then_inc(dve_row, 1)
                dve.wait_ge(pe_row, PR.at(rows, "p2T"))
                kn = kept_now[:].rearrange("p (u t) -> p u t", u=LANES).unsqueeze(2).broadcast_to([P, LANES, 2, TILES])
                for x in range(PAIRS):
                    nc.vector.tensor_tensor(P2T[:, x, :].rearrange("p (u s t) -> p u s t", u=LANES, t=TILES)[:, :, 0:2, :],
                                            pr[:, x * P:(x + 1) * P].rearrange("p (u s t) -> p u s t", u=LANES, t=TILES)[:, :, 0:2, :],
                                            kn, ALU.mult).then_inc(dve_row, 1)
            if second is not None:
                next_sequence(*lanes2[0])
            if first is not None:
                softmax_weights(*lanes[1])
            if rows is not None:
                dve.wait_ge(pe_row, PR.at(rows, "a2"))
                dve.wait_ge(dve_row, DR.at(rows, "rb"))
                nc.vector.tensor_scalar(A2[:], pr2[:, 0:D], rs["ra"][:, 0:1], None, ALU.mult).then_inc(dve_row, 1)
                dve.wait_ge(dve_row, DR.at(rows, "a2a"))
                nc.vector.scalar_tensor_tensor(out=A2[:], in0=pr2[:, D:P], scalar=rs["rb"][:, 0:1], in1=A2[:],
                                               op0=ALU.mult, op1=ALU.add).then_inc(dve_row, 1)
            if second is not None:
                next_sequence(*lanes2[1])
            if rows is not None:
                dve.wait_ge(pe_row, PR.at(rows, "o2"))
                nc.vector.tensor_tensor(X2a[:], pr2[:, P:P + D], row[:, 5, :], ALU.add).then_inc(dve_row, 1)
                dve.wait_ge(dve_row, DR.at(rows, "x2a"))
                nc.vector.scalar_tensor_tensor(out=X2[:, bass.ds(rows, 1), :].rearrange("p n f -> p (n f)"), in0=X2a[:],
                                               scalar=rs["qm"][:, 0:1], in1=Q2[:], op0=ALU.mult, op1=ALU.add).then_inc(dve_row, 1)

        LAST = PASSES - 1

        def all_halves(half, engine):
            half(engine, zero=(0, 0))
            half(engine, first=(0, 0), zero=(1, 0))
            half(engine, first=(1, 0), second=(0, 0), zero=(0, 1))
            half(engine, first=(0, 1), second=(1, 0), zero=(1, 1))
            half(engine, first=(1, 1), second=(0, 1), zero=(0, 2), rows=0)
            with engine.Fori(1, LAST - 1) as n:
                half(engine, first=(0, n + 1), second=(1, n), zero=(1, n + 1))
                half(engine, first=(1, n + 1), second=(0, n + 1), zero=(0, n + 2), rows=n)
            half(engine, first=(0, LAST), second=(1, LAST - 1), zero=(1, LAST))
            half(engine, first=(1, LAST), second=(0, LAST), rows=LAST - 1)
            half(engine, second=(1, LAST))
            half(engine, rows=LAST)

        with nc.Block() as block:
            @block.sync
            def _(sp):
                def prefill(u, n=None):
                    if n is not None:
                        sp.wait_ge(seq_made, n * LANES + u + 1)
                    sp.dma_start(X[u][:], negpos[:]).then_inc(prefilled[u], 16)

                def one_pass(n):
                    for u in LN:
                        prefill(u, n)

                for u in LN:
                    prefill(u)
                one_pass(0)
                with sp.Fori(1, LAST) as n:
                    one_pass(n)

            @block.gpsimd
            def _(pool):
                table_rows = pool.to_reg(NI)
                last_item = pool.alloc_register("last_item")

                def gather(n, u):
                    nc.gpsimd.tensor_copy(idx_now[u][:], idx_all[:, bass.ds(n * (LANES * TILES) + u * TILES, TILES)]).then_inc(idx_copied, 1)
                    pool.wait_ge(idx_copied, n * LANES + u + 1)
                    pool.wait_ge(prefilled[u], n * 16 + 16)
                    pool.reg_sub(last_item, table_rows, 1)
                    for t in range(TILES):
                        nc.gpsimd.indirect_dma_start(
                            out=X[u][:, t, :], out_offset=None, in_=item_emb,
                            in_offset=bass.IndirectOffsetOnAxis(ap=idx_now[u][:, t:t + 1], axis=0),
                            bounds_check=last_item, oob_is_err=False).then_inc(gathered[u], 16)

                def sequence(n, u):
                    g, v = u // WIDE, u % WIDE
                    pool.wait_ge(gathered[u], n * (16 * TILES) + 16 * TILES)
                    if not (isinstance(n, int) and n == 0):
                        pool.wait_ge(pe_g[g], PL[g].at(n - 1, "keyT", v))
                        pool.wait_ge(dve_g[g], DL[g].at(n - 1, "cen1", v))
                    nc.gpsimd.tensor_tensor(SEQ[u][:], X[u][:], negpos[:], ALU.subtract).then_inc(seq_made, 1)

                def one_pass(n, last=False):
                    for u in LN:
                        if u + 1 < LANES:
                            gather(n, u + 1)
                        elif not last:
                            gather(n + 1, 0)
                        sequence(n, u)

                gather(0, 0)
                one_pass(0)
                with pool.Fori(1, LAST) as n:
                    one_pass(n)
                one_pass(LAST, last=True)

            @block.scalar
            def _(act):
                load_ids(act, 0)
                all_halves(half_act, act)

            @block.tensor
            def _(pe):
                all_halves(half_pe, pe)

            @block.vector
            def _(dve):
                all_halves(half_dve, dve)


        CHUNKS = PASSES // TILES
        assert PASSES % TILES == 0 and CHUNKS <= LANES
        CH = range(CHUNKS)
        dve_end = sem("dve_end")
        act_end = sem("act_end")
        pe_end = sem("pe_end")

        def chunks(*names):
            return [(name, c) for name in names for c in CH]

        DE = Steps(dve_end, chunks("bnb") + norm_steps("b") + chunks("cenb", "hatb", "z", "zm", "bnc")
                   + norm_steps("c") + chunks("cenc", "hatc") + [(q, k) for k in range(2 * CHUNKS) for q in ("hi", "lo")])
        AE = Steps(act_end, chunks("yT", "hT") + [("fin", k) for k in range(2 * CHUNKS)])
        PE = Steps(pe_end, chunks("yT", "h", "o", "z") + [("fin", k) for k in range(2 * CHUNKS)])
        with nc.Block() as block:
            @block.vector
            def _(dve):
                def rows_norm(k, src):
                    for c in CH:
                        if k == "c":
                            dve.wait_ge(dve_end, DE.at(0, "zm", c))
                        for t in range(TILES):
                            m = nc.vector.bn_stats(bn[:, c, t, :], src[c][:, t, :])
                        m.then_inc(dve_end, 1)
                    dve.wait_ge(dve_end, DE.at(0, "bn" + k, CHUNKS - 1))
                    for name in CHAIN:
                        norm_step(dve, name, {q: st[q][:, 0:CHUNKS, :] for q in sz}, lambda i: bn[:, 0:CHUNKS, :, i],
                                  dve_end, lambda step: DE.at(0, step + "_" + k))
                    for c in CH:
                        nc.vector.scalar_tensor_tensor(out=XN[c][:], in0=bc(st["sum"][:, c, :]), scalar=-0.5, in1=src[c][:],
                                                       op0=ALU.mult, op1=ALU.add).then_inc(dve_end, 1)
                    dve.wait_ge(dve_end, DE.at(0, "rstd_" + k))
                    for c in CH:
                        dve.wait_ge(dve_end, DE.at(0, "cen" + k, c))
                        if k == "b":
                            nc.vector.tensor_tensor(XN[c][:], XN[c][:], bc(st["rstd"][:, c, :]), ALU.mult).then_inc(dve_end, 1)
                        else:
                            nc.vector.tensor_tensor(BLK[c][:].rearrange("p t (k f) -> p t k f", f=D),
                                                    XN[c][:].unsqueeze(2).broadcast_to([P, TILES, 2, D]),
                                                    bc(st["rstd"][:, c, :]).unsqueeze(2).broadcast_to([P, TILES, 2, D]),
                                                    ALU.mult).then_inc(dve_end, 1)

                rows_norm("b", [X2[:, c * TILES:(c + 1) * TILES, :] for c in CH])
                for c in CH:
                    dve.wait_ge(pe_end, PE.at(0, "o", c))
                    nc.vector.scalar_tensor_tensor(out=S2T[c][:], in0=pl[c][:], scalar=col[:, 11:12], in1=QT[c][:],
                                                   op0=ALU.add, op1=ALU.add).then_inc(dve_end, 1)
                for c in CH:
                    dve.wait_ge(pe_end, PE.at(0, "z", c))
                    nc.vector.tensor_tensor(SEQ[c][:], pl[c][:].rearrange("p (t f) -> p t f", f=D),
                                            bc(last_all[:, c * TILES:(c + 1) * TILES]), ALU.mult).then_inc(dve_end, 1)
                rows_norm("c", [SEQ[c] for c in CH])
                for k in range(2 * CHUNKS):
                    c, half = k % CHUNKS, k // CHUNKS
                    dve.wait_ge(act_end, AE.at(0, "fin", k))
                    final = (QT if half == 0 else KT)[c]
                    for part, tile in (("hi", hid_hi), ("lo", hid_lo)):
                        for i in range(4):
                            n = c * TILES + half * 4 + i
                            dst = tile[:, n * BATCH:(n + 1) * BATCH].rearrange("p (u t s) -> p u s t", u=LANES, s=2)
                            src = final[:, i * P:(i + 1) * P].rearrange("p (u s t) -> p u s t", u=LANES, t=TILES)[:, :, 0:2, :]
                            if part == "hi":
                                m = nc.vector.tensor_copy(dst, src)
                            else:
                                high = hid_hi[:, n * BATCH:(n + 1) * BATCH].rearrange("p (u t s) -> p u s t", u=LANES, s=2).bitcast(F32)
                                m = nc.vector.tensor_tensor(dst, src, high, ALU.subtract)
                        m.then_inc(dve_end, 1)
                        if part == "hi":
                            dve.wait_ge(dve_end, DE.at(0, "hi", k))

            @block.tensor
            def _(pe):
                for c in CH:
                    pe.wait_ge(dve_end, DE.at(0, "hatb", c))
                    turn(pl[c], XN[c]).then_inc(pe_end, 1)
                for c in CH:
                    pe.wait_ge(act_end, AE.at(0, "yT", c))
                    nc.tensor.matmul(pl[c][:], bd["w1b"][:], QT[c][:], start=True, stop=True).then_inc(pe_end, 1)
                for c in CH:
                    pe.wait_ge(act_end, AE.at(0, "hT", c))
                    nc.tensor.matmul(pl[c][:], bd["w2b"][:], KT[c][:], start=True, stop=True).then_inc(pe_end, 1)
                for c in CH:
                    pe.wait_ge(dve_end, DE.at(0, "z", c))
                    for x in range(PAIRS):
                        m = nc.tensor.transpose(pl[c][:, x * P:(x + 1) * P], S2T[c][:, x * P:(x + 1) * P], ident[:])
                    m.then_inc(pe_end, 1)
                for k in range(2 * CHUNKS):
                    c, half = k % CHUNKS, k // CHUNKS
                    pe.wait_ge(dve_end, DE.at(0, "hatc", c))
                    if half:
                        pe.wait_ge(act_end, AE.at(0, "fin", c))
                    for i in range(4):
                        m = nc.tensor.transpose(pl[c][:, i * P:(i + 1) * P], BLK[c][:, 4 * half + i, :], ident[:])
                    m.then_inc(pe_end, 1)

            @block.scalar
            def _(act):
                for c in CH:
                    act.wait_ge(pe_end, PE.at(0, "yT", c))
                    nc.scalar.activation(QT[c][:], pl[c][:], ACT.Identity, scale=col[:, 9:10], bias=col[:, 10:11]).then_inc(act_end, 1)
                for c in CH:
                    act.wait_ge(pe_end, PE.at(0, "h", c))
                    nc.scalar.activation(KT[c][:], pl[c][:], ACT.Relu, bias=col[:, 7:8]).then_inc(act_end, 1)
                for k in range(2 * CHUNKS):
                    c, half = k % CHUNKS, k // CHUNKS
                    act.wait_ge(pe_end, PE.at(0, "fin", k))
                    nc.scalar.activation((QT if half == 0 else KT)[c][:], pl[c][:], ACT.Identity,
                                         scale=col[:, 12:13], bias=col[:, 13:14]).then_inc(act_end, 1)

        ph1.close()
        with ExitStack() as ph2:
            def sb2(name, shape, dt=F32):
                return ph2.enter_context(nc.sbuf_tensor("s_" + name, shape, dt))

            embT = sb2("embT", [P, NO], F32R)
            ident2 = sb2("ident2", [P, P])
            raw = [sb2(f"raw{b}", [ER, EL, D]) for b in range(2)]
            split = [sb2(f"split{b}", [ER, EL, 2 * D]) for b in range(2)]
            hi_now = sb2("hi_now", [P, P], F32R)
            lo_now = sb2("lo_now", [P, P], F32R)
            outs = [sb2(f"outs{b}", [P, DSL * NSL]) for b in range(2)]
            ps = [ph2.enter_context(nc.psum_tensor(f"ps{b}", [P, 512], F32)) for b in range(DSL)]

            id_in = sem("id_in")
            raw_in = [sem(f"raw_in{b}") for b in range(2)]
            split_hi = sem("split_hi")
            split_lo = sem("split_lo")
            turned = sem("turned")
            emb_put = sem("emb_put")
            emb_rows = out_emb.rearrange("(n b a p) f -> n b p a f", b=2, a=EL, p=ER)
            NE = NO // (ER * EL * 2)
            with nc.Block() as block:
                @block.sync
                def _(sp):
                    sp.dma_start(ident2[:], const[:, 0:P]).then_inc(id_in, 16)
                    with sp.Fori(0, NE) as n:
                        for b in range(2):
                            sp.wait_ge(split_lo, n * 2)
                            sp.dma_start(raw[b][:], emb_rows[bass.ds(n, 1), b].rearrange("n p a f -> (n p) a f")).then_inc(raw_in[b], 16)

                @block.vector
                def _(dve):
                    with dve.Fori(0, NE) as n:
                        for b in range(2):
                            dve.wait_ge(raw_in[b], n * 16 + 16)
                            dve.wait_ge(turned, n * 2)
                            nc.vector.tensor_copy(split[b][:, :, 0:D].bitcast(F32R), raw[b][:]).then_inc(split_hi, 1)
                            dve.wait_ge(split_hi, n * 2 + b + 1)
                            nc.vector.tensor_tensor(split[b][:, :, D:2 * D], raw[b][:], split[b][:, :, 0:D], ALU.subtract).then_inc(split_lo, 1)

                @block.tensor
                def _(pe):
                    pe.wait_ge(id_in, 16)
                    with pe.Fori(0, NE) as n:
                        for b in range(2):
                            pe.wait_ge(split_lo, n * 2 + b + 1)
                            pe.wait_ge(emb_put, n * 2)
                            for a in range(EL):
                                m = nc.tensor.transpose(ps[b][:, a * ER:(a + 1) * ER], split[b][:, a, :], ident2[0:ER, 0:ER])
                            m.then_inc(turned, 1)

                @block.scalar
                def _(act):
                    with act.Fori(0, NE) as n:
                        for b in range(2):
                            act.wait_ge(turned, n * 2 + b + 1)
                            nc.scalar.activation(embT[:, bass.ds(n * (2 * EL * ER) + b * EL * ER, EL * ER)],
                                                 ps[b][:, 0:EL * ER], ACT.Copy).then_inc(emb_put, 1)

            ROUNDS = STORES // 2
            now_hi = sem("now_hi")
            now_lo = sem("now_lo")
            product = sem("product")
            left = [sem(f"left{b}") for b in range(DSL)]
            stored = [sem(f"stored{b}") for b in range(2)]
            on_act = [k for k in range(2 * DSL) if k % DSL % 2 == 0]
            on_dve = [k for k in range(2 * DSL) if k % DSL % 2 == 1]
            out_g = out.rearrange("(g p) c -> g p c", p=P)
            with nc.Block() as block:
                @block.tensor
                def _(pe):
                    with pe.Fori(0, GROUPS) as g:
                        with pe.Fori(0, ROUNDS) as r:
                            q = g * ROUNDS + r
                            for k in range(2 * DSL):
                                if k == 0:
                                    pe.wait_ge(now_lo, g + 1)
                                pe.wait_ge(left[k % DSL], q * 2 + k // DSL)
                                e = embT[:, bass.ds(r * (2 * DSL * NSL) + k * NSL, NSL)]
                                nc.tensor.matmul(ps[k % DSL][:, 0:NSL], hi_now[:], e, start=True, stop=False)
                                nc.tensor.matmul(ps[k % DSL][:, 0:NSL], lo_now[:], e, start=False, stop=True).then_inc(product, 1)

                @block.scalar
                def _(act):
                    with act.Fori(0, GROUPS) as g:
                        with act.Fori(0, ROUNDS) as r:
                            q = g * ROUNDS + r
                            for k in on_act:
                                if k in (0, DSL):
                                    act.wait_ge(stored[k // DSL], q * 16)
                                act.wait_ge(product, q * (2 * DSL) + k + 1)
                                nc.scalar.activation(outs[k // DSL][:, k % DSL * NSL:(k % DSL + 1) * NSL], ps[k % DSL][:, 0:NSL],
                                                     ACT.Copy).then_inc(left[k % DSL], 1)

                @block.vector
                def _(dve):
                    with dve.Fori(0, GROUPS) as g:
                        dve.wait_ge(product, g * (2 * DSL * ROUNDS))
                        nc.vector.tensor_copy(hi_now[:], hid_hi[:, bass.ds(g * P, P)].bitcast(F32)).then_inc(now_hi, 1)
                        nc.vector.tensor_copy(lo_now[:], hid_lo[:, bass.ds(g * P, P)].bitcast(F32)).then_inc(now_lo, 1)
                        with dve.Fori(0, ROUNDS) as r:
                            q = g * ROUNDS + r
                            for k in on_dve:
                                if k in (1, DSL + 1):
                                    dve.wait_ge(stored[k // DSL], q * 16)
                                dve.wait_ge(product, q * (2 * DSL) + k + 1)
                                nc.vector.tensor_copy(outs[k // DSL][:, k % DSL * NSL:(k % DSL + 1) * NSL],
                                                      ps[k % DSL][:, 0:NSL]).then_inc(left[k % DSL], 1)

                @block.sync
                def _(sp):
                    with sp.Fori(0, GROUPS) as g:
                        with sp.Fori(0, ROUNDS) as r:
                            q = g * ROUNDS + r
                            for b in range(2):
                                for k in range(DSL):
                                    sp.wait_ge(left[k], q * 2 + b + 1)
                                sp.dma_start(out_g[bass.ds(g, 1), :, bass.ds(r * (2 * DSL * NSL) + b * DSL * NSL, DSL * NSL)].rearrange("g p c -> (g p) c"),
                                             outs[b][:]).then_inc(stored[b], 16)
                    for b in range(2):
                        sp.wait_ge(stored[b], 16 * GROUPS * ROUNDS)


def _constants():
    import numpy as np

    p = np.arange(P)
    half, i = p // 64, p % 64
    ident = np.eye(P)
    key = np.arange(512)
    later = (key[None, :] % 64 > i[:, None])
    r = p % 32
    col_t = 2 * (key // P) + (key % P) // 64
    ksel = (r[:, None] == col_t[None, :]) & (r[:, None] < 8)
    lane, rs, rt = p // 32, (p % 32) // 8, p % 8
    used = (p % 32) < 16
    rsel = (lane[:, None] == lane[None, :]) & (r[:, None] == 16 + (rt % 2)[None, :]) & used[None, :]
    same = (rt[:, None] // 2 == key[None, :] // P) & (rs[:, None] == (key[None, :] % P) // 64)
    other = ~same & used[:, None]
    abrow = (half[:, None] == (rt % 2)[None, :]) & used[None, :]
    ab01 = (rt[:, None] % 2 == np.arange(2)[None, :])
    parts = [ident, MASKED * ident, later, MASKED * ksel, MASKED * rsel, other, abrow, ab01]
    return np.concatenate([np.asarray(x, np.float32) for x in parts], axis=1)


def kernel(**inputs):
    import numpy as np
    import concourse.bacc as bacc
    from concourse.bass_utils import run_bass_kernel_spmd

    x = {k.replace("L0_rec_", ""): np.asarray(v) for k, v in inputs.items()}
    two = lambda v: np.concatenate([v, v])
    cols = np.stack([two(v) for v in (x["ln1_g"][0], x["ln1_b"][0], x["ln2_g"][0], x["ln2_b"][0], x["b1"][0],
                                      x["bq"][0], x["bq"][1], x["b1"][1], x["b2"][0], x["ln2_g"][1], x["ln2_b"][1],
                                      x["b2"][1], x["lnf_g"], x["lnf_b"])], axis=1)
    rows = np.stack([x["ln1_g"][0], x["ln1_b"][0], x["bv"][0], x["ln1_g"][1], x["ln1_b"][1], x["bv"][1]])
    arrays = {
        "ids": x["r_input_ids"], "item_emb": x["item_emb"], "pos_emb": x["pos_emb"],
        "wqT": x["Wq"].transpose(0, 2, 1), "wkT": x["Wk"].transpose(0, 2, 1), "wv": x["Wv"], "w1": x["W1"], "w2": x["W2"],
        "cols": cols, "rows": rows, "out_emb": x["out_item_emb"], "const": _constants(),
    }
    arrays = {k: np.ascontiguousarray(v) for k, v in arrays.items()}
    nc = bacc.Bacc("TRN2", target_bir_lowering=False, num_devices=1)
    aps = [nc.dram_tensor(f"in_{k}", v.shape, mybir.dt.from_np(v.dtype), kind="ExternalInput").ap() for k, v in arrays.items()]
    shape = (x["r_input_ids"].shape[0], x["out_item_emb"].shape[0])
    out = nc.dram_tensor("out_scores", shape, F32, kind="ExternalOutput").ap()
    recommender(nc, *aps, out)
    r = run_bass_kernel_spmd(nc, [{f"in_{k}": v for k, v in arrays.items()}], core_ids=[0])
    return r.results[0]["out_scores"]
```

```python
from contextlib import ExitStack

import concourse.bass as bass
from concourse import mybir

F32 = mybir.dt.float32
F32R = mybir.dt.float32r
BF16 = mybir.dt.bfloat16
I32 = mybir.dt.int32
ALU = mybir.AluOpType
ACT = mybir.ActivationFunctionType
AX = mybir.AxisListType.X

P = 128
LANES = 4
WIDE = 2
TILES = 8
PAIRS = TILES // 2
EPS = 1e-3
SEED = float(0x5F3759DF + 0xCB0000)
MASKED = -(2.0 ** 100)


class Steps:

    def __init__(self, sem, names):
        self.sem = sem
        self.per_pass = len(names)
        self.index = {name: i + 1 for i, name in enumerate(names)}
        assert len(self.index) == len(names)

    def at(self, n, *name):
        return n * self.per_pass + self.index[name]

    def start(self, n):
        return n * self.per_pass


def each(*names):
    return [(name, v) for name in names for v in range(WIDE)]


CHAIN = ("sum", "diff", "m2", "spread", "var64", "seed", "half", "times", "newton", "e1", "e2", "poly", "rstd")


def norm_steps(k):
    return [(name + k,) for name in CHAIN]


def recommender(nc, ids, item_emb, pos_emb, wqT, wkT, wv, w1, w2, cols, rows, out_emb, const, out):
    B, S = ids.shape
    NI, D = item_emb.shape
    NO = out_emb.shape[0]
    MASK_ID = NI - 1
    assert S == 64 and D == 64 and B % P == 0
    BATCH = 16 * LANES
    PASSES = B // BATCH
    T = B * S // P
    GROUPS = B // P
    TQ = T // P if T >= P else 1
    TR = min(T, P)
    NSL = 500
    DSL = 5
    STORES = NO // (NSL * DSL)
    SBUFS = 5 if STORES % 5 == 0 else 2
    ER = 125
    EL = 4
    EBUFS = 5
    assert NO % (NSL * DSL) == 0 and NO % (ER * EL) == 0

    ctx = ExitStack()
    with ctx:
        def sem(name):
            return ctx.enter_context(nc.semaphore(name))

        hid_hi = ctx.enter_context(nc.sbuf_tensor("s_hid_hi", [P, B], F32R))
        hid_lo = ctx.enter_context(nc.sbuf_tensor("s_hid_lo", [P, B], F32R))
        ph1 = ctx.enter_context(ExitStack())

        def sb(name, shape, dt=F32):
            return ph1.enter_context(nc.sbuf_tensor("s_" + name, shape, dt))

        ident = sb("ident", [P, P])
        maskid = sb("maskid", [P, P], BF16)
        ones_b = sb("ones_b", [P, P], BF16)
        later = sb("later", [P, 512], BF16)
        ksel = sb("ksel", [P, 512], BF16)
        rsel = sb("rsel", [P, P], BF16)
        other = sb("other", [P, 512], BF16)
        abrow = sb("abrow", [P, P])
        ab01 = sb("ab01", [P, 2])
        cstage = [sb(f"cstage{b}", [P, 512]) for b in range(2)]
        bd = {k: sb("bd_" + k, [P, P]) for k in ("m", "v", "w1", "w2", "w1b", "w2b")}
        gpair = sb("gpair", [P, 2])
        col = sb("col", [P, cols.shape[1]])
        row = sb("row", [P, rows.shape[0], D])
        wq_s = sb("wq_s", [D, 2, D])
        wk_s = sb("wk_s", [D, 2, 2 * D])
        wq_d = sb("wq_d", [D, 2, 2 * D])
        m2dup = sb("m2dup", [D, P])
        cbias = sb("cbias", [P, 2])
        wv2 = sb("wv2", [D, D])
        bv3 = sb("bv3", [P, 512], BF16)
        bvt = sb("bvt", [P, 4, D])
        bvb = sb("bvb", [P, 3, D], BF16)
        gsum = sb("gsum", [P, 2])

        idx_all = sb("idx_all", [P, T], I32)
        kept_all = sb("kept_all", [P, T])
        last_i = sb("last_i", [P, PASSES], I32)
        last_all = sb("last_all", [P, PASSES])

        LN = range(LANES)
        GR = range(LANES // WIDE)
        X = [sb(f"XIN{u}", [P, TILES, D]) for u in LN]
        SEQ = [sb(f"SEQ{u}", [P, TILES, D]) for u in LN]
        RES = [sb(f"RES{u}", [P, TILES, D]) for u in LN]
        XN = [sb(f"XN{u}", [P, TILES, D]) for u in LN]
        KT = [sb(f"KT{u}", [P, 512]) for u in LN]
        QT = [sb(f"QT{u}", [P, 512]) for u in LN]
        BLK = [sb(f"BLK{u}", [P, TILES, P]) for u in LN]
        V = [sb(f"V{u}", [P, TILES, D]) for u in LN]
        S2T = [sb(f"S2T{u}", [P, 512]) for u in LN]
        S2N = [sb(f"S2N{u}", [P, TILES, D]) for u in LN]
        idx_now = [sb(f"idx_now{u}", [P, TILES], I32) for u in LN]
        bn = sb("bn", [P, LANES, 2, TILES, 6])
        sz = {k: sb("sz_" + k, [P, LANES, 2, TILES]) for k in
              ("sum", "diff", "m2", "spread", "var64", "rho", "tmp", "poly", "rstd")}
        st = {k: sb("st_" + k, [P, LANES, TILES]) for k in
              ("max", "den", "rden", "rq", "qs", "qsr", "qtok", "qrow")}
        kflag = [sb(f"kflag{g}", [P, LANES, 32]) for g in GR]
        kflagT = [sb(f"kflagT{g}", [P, P], BF16) for g in GR]

        XL = sb("XL", [P, D])
        XLM = sb("XLM", [P, D])
        last_now = sb("last_now", [P, 1])
        kept_now = sb("kept_now", [P, LANES * TILES])
        rbn = sb("rbn", [P, 6])
        rs = {k: sb("rs_" + k, [P, 1]) for k in
              ("sum", "diff", "m2", "spread", "var64", "rho", "tmp", "poly", "rstd", "mean",
               "qsum", "qm", "max", "negmax", "den", "rden", "ra", "rb")}
        rhat = sb("rhat", [P, D])
        rgain = sb("rgain", [P, D])
        Q2w = sb("Q2w", [P, P])
        Q2 = Q2w[:, 0:D]
        rT = sb("rT", [D, P])
        G2B = sb("G2B", [P, LANES, 32])
        idrow = sb("idrow", [P, 512], I32)
        idflag = sb("idflag", [P, 512])
        flag2 = sb("flag2", [P, 512], BF16)
        P2 = sb("P2", [P, 512])
        P2T = sb("P2T", [P, PAIRS, P])
        A2w = sb("A2w", [P, P])
        A2 = A2w[:, 0:D]
        X2a = sb("X2a", [P, D])
        X2 = ph1.enter_context(nc.sbuf_tensor("s_X2", [P, PASSES, D], F32))

        pl = [ph1.enter_context(nc.psum_tensor(f"pl{u}", [P, 512], F32)) for u in LN]
        pr = ph1.enter_context(nc.psum_tensor("pr", [P, 512], F32))
        pr2 = ph1.enter_context(nc.psum_tensor("pr2", [P, 512], F32))
        pg = [ph1.enter_context(nc.psum_tensor(f"pg{g}", [P, 512], F32)) for g in GR]

        loaded = sem("loaded")
        stage_in = [sem(f"stage_in{b}") for b in range(2)]
        ids_loaded = sem("ids_loaded")
        set_dve = sem("set_dve")
        set_pe = sem("set_pe")
        set_act = sem("set_act")
        prefilled = [sem(f"prefilled{u}") for u in LN]
        cleared = sem("cleared")
        idx_copied = sem("idx_copied")
        gathered = [sem(f"gathered{u}") for u in LN]
        tokens_in = sem("tokens_in")
        ids_in_rows = sem("ids_in_rows")
        seq_made = sem("seq_made")
        dve_b = [sem(f"dve_b{g}") for g in GR]
        dve_z = [sem(f"dve_z{g}") for g in GR]
        dve_g = [sem(f"dve_g{g}") for g in GR]
        act_g = [sem(f"act_g{g}") for g in GR]
        pe_g = [sem(f"pe_g{g}") for g in GR]
        dve_row = sem("dve_row")
        act_row = sem("act_row")
        pe_row = sem("pe_row")

        dve_steps = (each("cen1", "hat1") + [("qs",), ("qsr",), ("qtok",)] + [("qrow", k) for k in range(4)]
                     + [(name, v) for v in range(WIDE) for name in ("max", "shift")]
                     + [(name, v) for v in range(WIDE) for name in ("den", "rden", "rq", "prob")]
                     + each("res1", "bn2") + each("cen2", "hat2"))
        act_steps = (each("keyT") + [("kflagT",)] + each("qT") + [(h, v) for v in range(WIDE) for h in ("gA", "gB")]
                     + each("v", "exp") + [(h, v) for v in range(WIDE) for h in ("pA", "pB")] + each("yT", "hT", "seq2", "s2N"))
        pe_steps = each("keyT") + [("kflagT",)] + each("hatT", "g", "v", "s", "pT", "pv", "xtok", "yT", "h", "o", "s2N")
        DZ = [Steps(dve_z[g], norm_steps("") + [("kflag",)]) for g in GR]
        DL = [Steps(dve_g[g], dve_steps) for g in GR]
        AL = [Steps(act_g[g], act_steps) for g in GR]
        PL = [Steps(pe_g[g], pe_steps) for g in GR]
        DR = Steps(dve_row, [("now",), ("kept",), ("idflag",), ("xlm",), ("abn",)] + norm_steps("_a")
                   + [("mean",), ("hat",), ("gain",), ("q",), ("qsum",), ("qm",), ("g2",), ("flag2",),
                      ("max",), ("negmax",), ("rden",), ("ra",), ("rb",)] + [("p2T", k) for k in range(PAIRS)]
                   + [("a2a",), ("a2",), ("x2a",), ("x2",)])
        AR = Steps(act_row, [("qT",), ("exp",), ("a2T",)])
        PR = Steps(pe_row, [("qT",), ("g2",), ("s2",), ("flag",), ("p2T",), ("a2",), ("a2T",), ("o2",)])

        ids_tiles = ids.rearrange("b s -> (b s)").rearrange("(q r p) -> r q p", r=TR, p=P)
        ids_rows = ids.rearrange("b s -> (b s)").rearrange("(c x a p) -> c a x p", x=PAIRS, a=2, p=P)
        ids_last = ids.rearrange("(n u t s) j -> u s t n j", u=LANES, t=TILES, s=2)

        def bc(ap, w=D):
            return ap.unsqueeze(2).broadcast_to([ap.shape[0], ap.shape[1], w])

        negpos = sb("negpos", [P, TILES, D])
        with ExitStack() as setup:
            ids_in = setup.enter_context(nc.sbuf_tensor("s_ids_in", [P, TQ, P], I32))
            idf = setup.enter_context(nc.sbuf_tensor("s_idf", [P, TQ, P], F32))
            idn = setup.enter_context(nc.sbuf_tensor("s_idn", [P, TQ, P], F32))
            zeros = [bd["m"], bd["v"], bd["w1"], bd["w2"], bd["w1b"], bd["w2b"], gpair, last_i, G2B, idrow, bv3, P2T,
                     kflag[0], kflag[1], XL, Q2w, A2w, X2] + BLK
            CLEARED = len(zeros) + 1
            LOADS = 21
            CW = [("ident", P), ("maskid", P), ("later", 512), ("ksel", 512), ("rsel", P), ("other", 512), ("abrow", P), ("ab01", 2)]
            with nc.Block() as block:
                @block.sync
                def _(sp):
                    sp.dma_start(ids_in[0:TR], ids_tiles, allow_slow_non_contiguous=True).then_inc(ids_loaded, 16)
                    plain = [(SEQ[0][0:S, 0, :], pos_emb), (SEQ[0][S:P, 0, :], pos_emb), (col[:], cols),
                             (row[:], rows.unsqueeze(0).broadcast_to([P, rows.shape[0], D])), (wv2[:], wv[1]),
                             (wq_d[:, :, 0:D], wqT.rearrange("l d f -> d l f")), (wq_d[:, :, D:P], wqT.rearrange("l d f -> d l f")),
                             (wk_s[:, :, 0:D], wkT.rearrange("l d f -> d l f")), (wk_s[:, :, D:P], wkT.rearrange("l d f -> d l f"))]
                    into = [(bd[k][h * D:(h + 1) * D, h * D:(h + 1) * D], w) for k, w in
                            (("v", wv[0]), ("w1", w1[0]), ("w2", w2[0]), ("w1b", w1[1]), ("w2b", w2[1])) for h in range(2)]
                    into += [(gpair[0:D, 0:1], cols[0:D, 0:1]), (gpair[D:P, 1:2], cols[D:P, 0:1])]
                    assert len(plain) + len(into) == LOADS
                    for dst, src in plain:
                        sp.dma_start(dst, src, allow_slow_non_contiguous=True).then_inc(loaded, 16)
                    sp.wait_ge(cleared, CLEARED)
                    for dst, src in into:
                        sp.dma_start(dst, src, allow_slow_non_contiguous=True).then_inc(loaded, 16)
                    for u in LN:
                        for s in range(2):
                            sp.dma_start(last_i[32 * u + 8 * s:32 * u + 8 * s + 8, :].unsqueeze(2), ids_last[u, s][:, :, S - 1:S],
                                         allow_slow_non_contiguous=True).then_inc(loaded, 16)

                @block.scalar
                def _(act):
                    tiles = {"ident": ident, "maskid": maskid, "later": later, "ksel": ksel, "rsel": rsel,
                             "other": other, "abrow": abrow, "ab01": ab01}
                    offs = [sum(w for _, w in CW[:k]) for k in range(len(CW) + 1)]

                    def stage(k):
                        act.dma_start(cstage[k % 2][:, 0:CW[k][1]], const[:, offs[k]:offs[k + 1]]).then_inc(stage_in[k % 2], 16)

                    stage(0)
                    for k, (name, w) in enumerate(CW):
                        if k:
                            act.wait_ge(set_act, k)
                        if k + 1 < len(CW):
                            stage(k + 1)
                        act.wait_ge(stage_in[k % 2], 16 * (k // 2 + 1))
                        nc.scalar.activation(tiles[name][:], cstage[k % 2][:, 0:w], ACT.Copy).then_inc(set_act, 1)
                    N0 = len(CW)
                    act.wait_ge(set_pe, 2 * TQ + 4)
                    nc.scalar.activation(bd["m"][0:D, 0:D], pr[0:D, 0:D], ACT.Copy, scale=0.125).then_inc(set_act, 1)
                    nc.scalar.activation(bd["m"][D:P, D:P], pr[D:P, 0:D], ACT.Copy, scale=0.125).then_inc(set_act, 1)
                    nc.scalar.activation(m2dup[:, 0:D], pr[0:D, 64:128], ACT.Copy, scale=0.125).then_inc(set_act, 1)
                    nc.scalar.activation(m2dup[:, D:P], pr[0:D, 64:128], ACT.Copy, scale=0.125).then_inc(set_act, 1)
                    nc.scalar.activation(cbias[:, :], pr[:, 128:130], ACT.Copy, scale=0.125).then_inc(set_act, 1)
                    act.wait_ge(set_act, N0 + 5)

                @block.gpsimd
                def _(pool):
                    for t in zeros:
                        nc.gpsimd.memset(t[:], 0).then_inc(cleared, 1)
                    nc.gpsimd.memset(ones_b[:], 1.0).then_inc(cleared, 1)
                    pool.wait_ge(cleared, CLEARED)
                    for ab in range(2):
                        for u in LN:
                            nc.gpsimd.memset(G2B[ab * D:ab * D + D, u, 16 + ab:17 + ab], 1.0).then_inc(cleared, 1)
                    pool.wait_ge(cleared, CLEARED + 2 * LANES)

                @block.tensor
                def _(pe):
                    pe.wait_ge(set_dve, 7)
                    pe.wait_ge(set_act, 1)
                    for q in range(TQ):
                        if q:
                            pe.wait_ge(set_dve, 7 + 2 * q)
                        nc.tensor.transpose(pl[0][:, 0:TR], idf[0:TR, q, :], ident[0:TR, 0:TR]).then_inc(set_pe, 1)
                        nc.tensor.transpose(pl[1][:, 0:TR], idn[0:TR, q, :], ident[0:TR, 0:TR]).then_inc(set_pe, 1)
                    pe.wait_ge(loaded, 16 * (LOADS + 2 * LANES))
                    nc.tensor.matmul(pr[:, 0:D], wq_d[:, 0, :], wk_s[:, 0, 0:D], start=True, stop=True).then_inc(set_pe, 1)
                    nc.tensor.matmul(pr[0:D, D:P], wq_d[:, 1, 0:D], wk_s[:, 1, 0:D], start=True, stop=True).then_inc(set_pe, 1)
                    for l in range(2):
                        nc.tensor.matmul(pr[:, P + l:P + l + 1], wk_s[:, l, :], col[0:D, 5 + l:6 + l], start=True, stop=True).then_inc(set_pe, 1)

                @block.vector
                def _(dve):
                    dve.wait_ge(ids_loaded, 16)
                    k = [0]

                    def done(ins):
                        ins.then_inc(set_dve, 1)
                        k[0] += 1
                        dve.wait_ge(set_dve, k[0])

                    done(nc.vector.tensor_copy(idf[0:TR], ids_in[0:TR]))
                    done(nc.vector.tensor_scalar(idn[0:TR], idf[0:TR], 0.0, float(NI), ALU.is_lt, ALU.mult))
                    done(nc.vector.tensor_tensor(idn[0:TR], idn[0:TR], idf[0:TR], ALU.add))
                    done(nc.vector.tensor_scalar(idn[0:TR], idn[0:TR], 0.0, float(NI - 1), ALU.max, ALU.min))
                    done(nc.vector.scalar_tensor_tensor(out=idf[0:TR], in0=idf[0:TR], scalar=float(MASK_ID), in1=idn[0:TR],
                                                        op0=ALU.is_equal, op1=ALU.add))
                    done(nc.vector.tensor_copy(idn[0:TR], ids_in[0:TR]))
                    done(nc.vector.tensor_scalar(idn[0:TR], idn[0:TR], float(MASK_ID), None, ALU.not_equal))
                    assert k[0] == 7
                    for q in range(TQ):
                        dve.wait_ge(set_pe, 2 * q + 2)
                        done(nc.vector.tensor_copy(idx_all[:, q * TR:q * TR + TR], pl[0][:, 0:TR]))
                        done(nc.vector.tensor_copy(kept_all[:, q * TR:q * TR + TR], pl[1][:, 0:TR]))
                    dve.wait_ge(loaded, 16 * (LOADS + 2 * LANES))
                    done(nc.vector.tensor_copy(last_all[:], last_i[:]))
                    done(nc.vector.tensor_scalar(last_all[:], last_all[:], float(MASK_ID), None, ALU.not_equal))
                    done(nc.vector.tensor_scalar(negpos[:, :, :], SEQ[0][:, 0, :].unsqueeze(1).broadcast_to([P, TILES, D]),
                                                 -1.0, None, ALU.mult))
                    done(nc.vector.tensor_reduce(gsum[:, 0:1], row[:, 0, :], AX, ALU.add))
                    done(nc.vector.tensor_reduce(gsum[:, 1:2], row[:, 1, :], AX, ALU.add))
                    done(nc.vector.tensor_scalar(gsum[:, 0:1], gsum[:, 0:1], -0.5, None, ALU.mult))
                    bv = row[:, 2, :]
                    done(nc.vector.tensor_copy(bvb[:, 0, :], bv))
                    done(nc.vector.tensor_copy(bvt[:, 0, :], bvb[:, 0, :]))
                    done(nc.vector.tensor_tensor(bvt[:, 1, :], bv, bvt[:, 0, :], ALU.subtract))
                    done(nc.vector.tensor_copy(bvb[:, 1, :], bvt[:, 1, :]))
                    done(nc.vector.tensor_copy(bvt[:, 2, :], bvb[:, 1, :]))
                    done(nc.vector.tensor_tensor(bvt[:, 3, :], bvt[:, 1, :], bvt[:, 2, :], ALU.subtract))
                    done(nc.vector.tensor_copy(bvb[:, 2, :], bvt[:, 3, :]))
                    for r in range(3):
                        done(nc.vector.tensor_copy(bv3[32 * r:32 * r + 1, :].rearrange("p (t f) -> p t f", f=D),
                                                   bvb[32 * r:32 * r + 1, r, :].unsqueeze(1).broadcast_to([1, TILES, D])))


        def flat(tile, lo=0, hi=512):
            return tile[:].rearrange("p t f -> p (t f)")[:, lo:hi]

        def turn(bank, tile):
            for x in range(PAIRS):
                m = nc.tensor.transpose(bank[:, x * P:(x + 1) * P], flat(tile, x * P, (x + 1) * P), ident[:])
            return m

        def half_pe(pe, first=None, second=None, zero=None, rows=None, done=None):
            if first is not None:
                g, n = first
                lanes = [(v, g * WIDE + v) for v in range(WIDE)]
            if second is not None:
                g2, n2 = second
                lanes2 = [(v, g2 * WIDE + v) for v in range(WIDE)]
            if first is not None:
                for v, u in lanes:
                    if not (isinstance(n, int) and n == 0):
                        pe.wait_ge(act_g[g], AL[g].start(n))
                    pe.wait_ge(seq_made, n * LANES + u + 1)
                    turn(pl[u], SEQ[u]).then_inc(pe_g[g], 1)
                pe.wait_ge(dve_z[g], DZ[g].at(n, "kflag"))
                nc.tensor.transpose(pg[g][:, 0:P], kflag[g][:].rearrange("p u t -> p (u t)"), ident[:]).then_inc(pe_g[g], 1)
            if second is not None:
                for v, u in lanes2:
                    pe.wait_ge(dve_g[g2], DL[g2].at(n2, "prob", v))
                    turn(pl[u], XN[u]).then_inc(pe_g[g2], 1)
            if done is not None:
                pe.wait_ge(dve_row, DR.at(done, "a2"))
                nc.tensor.transpose(pr2[:, 0:P], A2w[:], ident[:]).then_inc(pe_row, 1)
            if first is not None:
                for v, u in lanes:
                    pe.wait_ge(act_g[g], AL[g].at(n, "keyT", v))
                    pe.wait_ge(dve_g[g], DL[g].at(n, "hat1", v))
                    turn(pl[u], XN[u]).then_inc(pe_g[g], 1)
            if done is not None:
                pe.wait_ge(act_row, AR.at(done, "a2T"))
                nc.tensor.matmul(pr2[:, P:P + D], rT[:], wv2[:], start=True, stop=True).then_inc(pe_row, 1)
            if second is not None:
                for v, u in lanes2:
                    pe.wait_ge(act_g[g2], AL[g2].at(n2, "pB", v))
                    for t in range(TILES):
                        ab, x = t % 2, t // 2
                        m = nc.tensor.matmul(pl[u][64 * ab:64 * ab + 64, x * P:(x + 1) * P], V[u][:, t, :], BLK[u][:, t, :],
                                             start=True, stop=True, skip_group_check=True)
                    m.then_inc(pe_g[g2], 1)
            if first is not None:
                for v, u in lanes:
                    pe.wait_ge(act_g[g], AL[g].at(n, "qT", v))
                    nc.tensor.matmul(pl[u][:], bd["m"][:], QT[u][:], start=True, stop=True).then_inc(pe_g[g], 1)
            if second is not None:
                for v, u in lanes2:
                    pe.wait_ge(dve_g[g2], DL[g2].at(n2, "res1", v))
                    turn(pl[u], RES[u]).then_inc(pe_g[g2], 1)

            def values(v, u):
                pe.wait_ge(act_g[g], AL[g].at(n, "gB", v))
                nc.tensor.matmul(pl[u][:], ones_b[:], bv3[:], start=True, stop=False, skip_group_check=True)
                for x in range(PAIRS):
                    c = P + v * TILES + 2 * x
                    nc.tensor.matmul(pl[u][:, x * P:(x + 1) * P], KT[u][:, x * P:(x + 1) * P], bd["v"][:],
                                     start=False, stop=(x == PAIRS - 1), skip_group_check=True)
                    m = nc.tensor.matmul(pg[g][:, c:c + 2], KT[u][:, x * P:(x + 1) * P], gpair[:],
                                         start=True, stop=True, skip_group_check=True)
                m.then_inc(pe_g[g], 1)

            def scores(v, u):
                pe.wait_ge(act_g[g], AL[g].at(n, "v", v))
                nc.tensor.matmul(pl[u][:], maskid[:], later[:], start=True, stop=False, skip_group_check=True)
                for x in range(PAIRS):
                    nc.tensor.matmul(pl[u][:, x * P:(x + 1) * P], ksel[32 * v:32 * v + TILES, x * P:(x + 1) * P],
                                     kflagT[g][32 * v:32 * v + TILES, :], start=False, stop=False, skip_group_check=True)
                for k in range(TILES):
                    m = nc.tensor.matmul(pl[u][:, k * S:(k + 1) * S], BLK[u][:, k, :], KT[u][:, k * S:(k + 1) * S],
                                         start=False, stop=(k == TILES - 1), skip_group_check=True)
                m.then_inc(pe_g[g], 1)

            if first is not None:
                values(*lanes[0])
                values(*lanes[1])
                scores(*lanes[0])
            if rows is not None:
                pe.wait_ge(dve_row, DR.at(rows, "q"))
                nc.tensor.transpose(pr2[:, 0:P], Q2w[:], ident[:]).then_inc(pe_row, 1)
            if first is not None:
                scores(*lanes[1])
            if rows is not None:
                pe.wait_ge(act_row, AR.at(rows, "qT"))
                nc.tensor.matmul(pr2[:, P:2 * P], m2dup[:], rT[:], start=True, stop=True).then_inc(pe_row, 1)
                pe.wait_ge(dve_row, DR.at(rows, "g2"))
                for u in LN:
                    m = nc.tensor.matmul(pr[32 * u:32 * u + 32, :], G2B[:, u, :], S2T[u][:], start=True, stop=False, skip_group_check=True)
                m.then_inc(pe_row, 1)
            if second is not None:
                for v, u in lanes2:
                    pe.wait_ge(dve_g[g2], DL[g2].at(n2, "hat2", v))
                    turn(pl[u], XN[u]).then_inc(pe_g[g2], 1)
            if rows is not None:
                pe.wait_ge(dve_row, DR.at(rows, "flag2"))
                nc.tensor.matmul(pr[:], rsel[:], flag2[:], start=False, stop=False, skip_group_check=True)
                nc.tensor.matmul(pr[:], maskid[:], other[:], start=False, stop=True, skip_group_check=True).then_inc(pe_row, 1)
            if second is not None:
                for v, u in lanes2:
                    pe.wait_ge(act_g[g2], AL[g2].at(n2, "yT", v))
                    nc.tensor.matmul(pl[u][:], bd["w1"][:], QT[u][:], start=True, stop=True).then_inc(pe_g[g2], 1)
                for v, u in lanes2:
                    pe.wait_ge(act_g[g2], AL[g2].at(n2, "hT", v))
                    nc.tensor.matmul(pl[u][:], bd["w2"][:], KT[u][:], start=True, stop=False)
                    nc.tensor.matmul(pl[u][:], ident[:], QT[u][:], start=False, stop=True).then_inc(pe_g[g2], 1)
            if rows is not None:
                pe.wait_ge(act_row, AR.at(rows, "exp"))
                for x in range(PAIRS):
                    m = nc.tensor.transpose(pr[:, x * P:(x + 1) * P], P2[:, x * P:(x + 1) * P], ident[:])
                m.then_inc(pe_row, 1)
                pe.wait_ge(dve_row, DR.at(rows, "p2T", PAIRS - 1))
                for u in LN:
                    for x in range(PAIRS):
                        m = nc.tensor.matmul(pr2[32 * u:32 * u + 32, 0:P], P2T[:, x, 32 * u:32 * u + 32],
                                             S2N[u][:, 2 * x:2 * x + 2, :].rearrange("p t f -> p (t f)"),
                                             start=(x == 0), stop=(x == PAIRS - 1), skip_group_check=True)
                m.then_inc(pe_row, 1)
            if second is not None:
                for v, u in lanes2:
                    pe.wait_ge(act_g[g2], AL[g2].at(n2, "seq2", v))
                    for x in range(PAIRS):
                        m = nc.tensor.transpose(pl[u][:, x * P:(x + 1) * P], S2T[u][:, x * P:(x + 1) * P], ident[:])
                    m.then_inc(pe_g[g2], 1)

        def load_ids(act, n):
            for u in LN:
                act.dma_start(idrow[32 * u + 16:32 * u + 18, :].rearrange("a (x p) -> a x p", p=P),
                              ids_rows[bass.ds(n * LANES + u, 1)].rearrange("c a x p -> (c a) x p")).then_inc(ids_in_rows, 16)

        def half_act(act, first=None, second=None, zero=None, rows=None, done=None):
            if first is not None:
                g, n = first
                lanes = [(v, g * WIDE + v) for v in range(WIDE)]
                for v, u in lanes:
                    act.wait_ge(pe_g[g], PL[g].at(n, "keyT", v))
                    nc.scalar.activation(KT[u][:], pl[u][:], ACT.Copy).then_inc(act_g[g], 1)
                act.wait_ge(pe_g[g], PL[g].at(n, "kflagT"))
                nc.scalar.activation(kflagT[g][:], pg[g][:, 0:P], ACT.Copy).then_inc(act_g[g], 1)
            if done is not None:
                act.wait_ge(pe_row, PR.at(done, "a2T"))
                nc.scalar.activation(rT[:], pr2[0:D, 0:P], ACT.Copy).then_inc(act_row, 1)
            if second is not None:
                g2, n2 = second
                lanes2 = [(v, g2 * WIDE + v) for v in range(WIDE)]
                for v, u in lanes2:
                    act.wait_ge(pe_g[g2], PL[g2].at(n2, "pT", v))
                    for s in range(2):
                        h = slice(64 * s, 64 * s + 64)
                        nc.scalar.activation(BLK[u][h, :, h], pl[u][h, :].rearrange("p (k i) -> p k i", i=S),
                                             ACT.Copy).then_inc(act_g[g2], 1)
            if first is not None:
                for v, u in lanes:
                    act.wait_ge(pe_g[g], PL[g].at(n, "hatT", v))
                    nc.scalar.activation(QT[u][:], pl[u][:], ACT.Identity, scale=col[:, 0:1], bias=col[:, 1:2]).then_inc(act_g[g], 1)
                for v, u in lanes:
                    act.wait_ge(pe_g[g], PL[g].at(n, "g", v))
                    for ab in range(2):
                        h = slice(64 * ab, 64 * ab + 64)
                        nc.scalar.activation(BLK[u][h, :, h], pl[u][h, :].rearrange("p (k i) -> p k i", i=S),
                                             ACT.Identity, bias=cbias[h, 0:1]).then_inc(act_g[g], 1)
            if first is not None:
                for v, u in lanes:
                    act.wait_ge(pe_g[g], PL[g].at(n, "v", v))
                    nc.scalar.activation(V[u][:], pl[u][:], ACT.Copy).then_inc(act_g[g], 1)
            if rows is not None:
                act.wait_ge(pe_row, PR.at(rows, "qT"))
                nc.scalar.activation(rT[:], pr2[0:D, 0:P], ACT.Copy).then_inc(act_row, 1)
            if second is not None:
                for v, u in lanes2:
                    act.wait_ge(pe_g[g2], PL[g2].at(n2, "yT", v))
                    nc.scalar.activation(QT[u][:], pl[u][:], ACT.Identity, scale=col[:, 2:3], bias=col[:, 3:4]).then_inc(act_g[g2], 1)
                for v, u in lanes2:
                    act.wait_ge(pe_g[g2], PL[g2].at(n2, "h", v))
                    nc.scalar.activation(KT[u][:], pl[u][:], ACT.Relu, bias=col[:, 4:5]).then_inc(act_g[g2], 1)

            def weights_exp(v, u):
                act.wait_ge(dve_g[g], DL[g].at(n, "shift", v))
                nc.scalar.activation(XN[u][:], XN[u][:], ACT.Exp).then_inc(act_g[g], 1)

            if first is not None:
                weights_exp(*lanes[0])
            if rows is not None:
                act.wait_ge(dve_row, DR.at(rows, "negmax"))
                nc.scalar.activation(P2[:], pr[:], ACT.Exp, bias=rs["negmax"][:, 0:1], accum_out=rs["den"][:, 0:1]).then_inc(act_row, 1)
                if not (isinstance(rows, int) and rows == LAST):
                    load_ids(act, rows + 1)
            if first is not None:
                weights_exp(*lanes[1])
            if second is not None:
                for v, u in lanes2:
                    act.wait_ge(pe_g[g2], PL[g2].at(n2, "o", v))
                    nc.scalar.activation(S2T[u][:], pl[u][:], ACT.Identity, bias=col[:, 8:9]).then_inc(act_g[g2], 1)
                for v, u in lanes2:
                    act.wait_ge(pe_g[g2], PL[g2].at(n2, "s2N", v))
                    nc.scalar.activation(S2N[u][:], pl[u][:], ACT.Copy).then_inc(act_g[g2], 1)
                for v, u in lanes2:
                    act.wait_ge(act_g[g2], AL[g2].at(n2, "s2N", v))
                    for s in range(2):
                        r = 32 * u + 8 * s
                        act.dma_start(XL[r:r + 8, :], S2N[u][64 * s + 63:64 * s + 64, :, :]).then_inc(tokens_in, 16)

        def norm_step(dve, name, b, e, sem, at):
            if name == "sum":
                m = nc.vector.tensor_tensor(b["sum"], e(1), e(4), ALU.add)
            elif name == "diff":
                m = nc.vector.tensor_tensor(b["diff"], e(1), e(4), ALU.subtract)
            elif name == "m2":
                m = nc.vector.tensor_tensor(b["m2"], e(2), e(5), ALU.add)
            elif name == "spread":
                dve.wait_ge(sem, at("diff"))
                m = nc.vector.scalar_tensor_tensor(out=b["spread"], in0=b["diff"], scalar=16.0, in1=b["diff"], op0=ALU.mult, op1=ALU.mult)
            elif name == "var64":
                dve.wait_ge(sem, at("spread"))
                m = nc.vector.scalar_tensor_tensor(out=b["var64"], in0=b["m2"], scalar=64 * EPS, in1=b["spread"], op0=ALU.add, op1=ALU.add)
            elif name == "seed":
                dve.wait_ge(sem, at("var64"))
                m = nc.vector.tensor_scalar(b["rho"].bitcast(I32), b["var64"].bitcast(I32), -0.5, SEED, ALU.mult, ALU.add)
            elif name == "half":
                dve.wait_ge(sem, at("seed"))
                m = nc.vector.scalar_tensor_tensor(out=b["tmp"], in0=b["rho"], scalar=-1.0 / 18, in1=b["rho"], op0=ALU.mult, op1=ALU.mult)
            elif name == "times":
                dve.wait_ge(sem, at("half"))
                m = nc.vector.tensor_tensor(b["tmp"], b["tmp"], b["var64"], ALU.mult)
            elif name == "newton":
                dve.wait_ge(sem, at("times"))
                m = nc.vector.scalar_tensor_tensor(out=b["rho"], in0=b["tmp"], scalar=1.5, in1=b["rho"], op0=ALU.add, op1=ALU.mult)
            elif name == "e1":
                dve.wait_ge(sem, at("newton"))
                m = nc.vector.scalar_tensor_tensor(out=b["tmp"], in0=b["rho"], scalar=1.0 / 9, in1=b["var64"], op0=ALU.mult, op1=ALU.mult)
            elif name == "e2":
                dve.wait_ge(sem, at("e1"))
                m = nc.vector.tensor_tensor(b["tmp"], b["tmp"], b["rho"], ALU.mult)
            elif name == "poly":
                dve.wait_ge(sem, at("e2"))
                m = nc.vector.scalar_tensor_tensor(out=b["poly"], in0=b["tmp"], scalar=-10.0 / 3, in1=b["tmp"], op0=ALU.add, op1=ALU.mult)
            else:
                dve.wait_ge(sem, at("poly"))
                m = nc.vector.scalar_tensor_tensor(out=b["rstd"], in0=b["poly"], scalar=5.0, in1=b["rho"], op0=ALU.add, op1=ALU.mult)
            m.then_inc(sem, 1)

        def half_dve(dve, first=None, second=None, zero=None, rows=None, done=None):
            if first is not None:
                g, n = first
                lanes = [(v, g * WIDE + v) for v in range(WIDE)]
                mine = slice(g * WIDE, (g + 1) * WIDE)
                for v, u in lanes:
                    dve.wait_ge(dve_z[g], DZ[g].at(n, "rstd"))
                    nc.vector.scalar_tensor_tensor(out=XN[u][:], in0=bc(sz["sum"][:, u, 1, :]), scalar=-0.5, in1=SEQ[u][:],
                                                   op0=ALU.mult, op1=ALU.add).then_inc(dve_g[g], 1)
                for v, u in lanes:
                    dve.wait_ge(dve_g[g], DL[g].at(n, "cen1", v))
                    nc.vector.tensor_tensor(XN[u][:], XN[u][:], bc(sz["rstd"][:, u, 1, :]), ALU.mult).then_inc(dve_g[g], 1)
            if second is not None:
                g2, n2 = second
                lanes2 = [(v, g2 * WIDE + v) for v in range(WIDE)]
                mine2 = slice(g2 * WIDE, (g2 + 1) * WIDE)
            if zero is not None:
                g0, n0 = zero
                lanes0 = [(v, g0 * WIDE + v) for v in range(WIDE)]
                mine0 = slice(g0 * WIDE, (g0 + 1) * WIDE)

            def row_chain(i):
                if rows is not None and i < len(CHAIN):
                    norm_step(dve, CHAIN[i], {q: rs[q][:] for q in rs}, lambda k: rbn[:, k:k + 1], dve_row,
                              lambda step: DR.at(rows, step + "_a"))

            def token_stats(v, u):
                dve.wait_ge(seq_made, n0 * LANES + u + 1)
                for t in range(TILES):
                    m = nc.vector.bn_stats(bn[:, u, 1, t, :], SEQ[u][:, t, :])
                m.then_inc(dve_b[g0], 1)

            def attention_stats(v, u, chain):
                dve.wait_ge(pe_g[g2], PL[g2].at(n2, "xtok", v))
                for t in range(TILES):
                    m = nc.vector.bn_stats(bn[:, u, 0, t, :], pl[u][:, t * D:(t + 1) * D])
                    if t == TILES - 1:
                        m.then_inc(dve_g[g2], 1)
                    if t % 2:
                        row_chain(chain + t // 2)

            def residual(v, u):
                dve.wait_ge(pe_g[g2], PL[g2].at(n2, "pv", v))
                nc.vector.tensor_tensor(flat(RES[u]), pl[u][:], QT[u][:], ALU.add).then_inc(dve_g[g2], 1)

            def center(v, u):
                nc.vector.scalar_tensor_tensor(out=XN[u][:], in0=bc(sz["sum"][:, u, 0, :]), scalar=-0.5,
                                               in1=pl[u][:].rearrange("p (t f) -> p t f", f=D),
                                               op0=ALU.mult, op1=ALU.add).then_inc(dve_g[g2], 1)

            def scale(v, u):
                dve.wait_ge(dve_g[g2], DL[g2].at(n2, "cen2", v))
                nc.vector.tensor_tensor(XN[u][:], XN[u][:], bc(sz["rstd"][:, u, 0, :]), ALU.mult).then_inc(dve_g[g2], 1)

            def shifted_scores(v, u):
                dve.wait_ge(pe_g[g], PL[g].at(n, "s", v))
                nc.vector.tensor_reduce(st["max"][:, u, :], pl[u][:].rearrange("p (k j) -> p k j", j=S), AX, ALU.max).then_inc(dve_g[g], 1)
                dve.wait_ge(dve_g[g], DL[g].at(n, "max", v))
                nc.vector.scalar_tensor_tensor(out=XN[u][:], in0=pl[u][:].rearrange("p (k j) -> p k j", j=S), scalar=MASKED,
                                               in1=bc(st["max"][:, u, :]), op0=ALU.max, op1=ALU.subtract).then_inc(dve_g[g], 1)

            def query_mask(step):
                if step == "half":
                    dve.wait_ge(pe_g[g], PL[g].at(n, "v", WIDE - 1))
                    nc.vector.scalar_tensor_tensor(out=st["qs"][:, mine, :], in0=sz["sum"][:, mine, 1, :], scalar=gsum[:, 0:1],
                                                   in1=pg[g][:, P:P + WIDE * TILES].rearrange("p (u t) -> p u t", u=WIDE),
                                                   op0=ALU.mult, op1=ALU.add).then_inc(dve_g[g], 1)
                elif step == "times":
                    dve.wait_ge(dve_g[g], DL[g].at(n, "qs"))
                    nc.vector.tensor_tensor(st["qsr"][:, mine, :], st["qs"][:, mine, :], sz["rstd"][:, mine, 1, :], ALU.mult).then_inc(dve_g[g], 1)
                elif step == "newton":
                    dve.wait_ge(dve_g[g], DL[g].at(n, "qsr"))
                    nc.vector.tensor_scalar(st["qtok"][:, mine, :], st["qsr"][:, mine, :], gsum[:, 1:2], 0.0, ALU.add, ALU.not_equal).then_inc(dve_g[g], 1)
                elif step in ("e1", "e2"):
                    s = 0 if step == "e1" else 1
                    dve.wait_ge(dve_g[g], DL[g].at(n, "qtok"))
                    for ab in range(2):
                        nc.vector.tensor_copy(st["qrow"][64 * ab:64 * ab + 64, mine, s::2],
                                              st["qtok"][64 * s:64 * s + 64, mine, ab::2]).then_inc(dve_g[g], 1)

            def softmax_weights(v, u):
                dve.wait_ge(act_g[g], AL[g].at(n, "exp", v))
                nc.vector.tensor_reduce(st["den"][:, u, :], XN[u][:], AX, ALU.add).then_inc(dve_g[g], 1)
                dve.wait_ge(dve_g[g], DL[g].at(n, "den", v))
                nc.vector.reciprocal(st["rden"][:, u, :], st["den"][:, u, :]).then_inc(dve_g[g], 1)
                dve.wait_ge(dve_g[g], DL[g].at(n, "rden", v))
                nc.vector.tensor_tensor(st["rq"][:, u, :], st["rden"][:, u, :], st["qrow"][:, u, :], ALU.mult).then_inc(dve_g[g], 1)
                dve.wait_ge(dve_g[g], DL[g].at(n, "rq", v))
                nc.vector.tensor_tensor(XN[u][:], XN[u][:], bc(st["rq"][:, u, :]), ALU.mult).then_inc(dve_g[g], 1)

            if zero is not None:
                token_stats(*lanes0[0])
            if zero is not None:
                token_stats(*lanes0[1])
            if done is not None:
                dve.wait_ge(pe_row, PR.at(done, "o2"))
                nc.vector.tensor_tensor(X2a[:], pr2[:, P:P + D], row[:, 5, :], ALU.add).then_inc(dve_row, 1)
                dve.wait_ge(dve_row, DR.at(done, "x2a"))
                nc.vector.scalar_tensor_tensor(out=X2[:, bass.ds(done, 1), :].rearrange("p n f -> p (n f)"), in0=X2a[:],
                                               scalar=rs["qm"][:, 0:1], in1=Q2[:], op0=ALU.mult, op1=ALU.add).then_inc(dve_row, 1)
            if rows is not None:
                nc.vector.tensor_copy(last_now[:], last_all[:, bass.ds(rows, 1)]).then_inc(dve_row, 1)
                nc.vector.tensor_copy(kept_now[:], kept_all[:, bass.ds(rows * (LANES * TILES), LANES * TILES)]).then_inc(dve_row, 1)
                dve.wait_ge(ids_in_rows, rows * (16 * LANES) + 16 * LANES)
                nc.vector.tensor_scalar(idflag[:], idrow[:], float(MASK_ID), None, ALU.is_equal).then_inc(dve_row, 1)
                dve.wait_ge(tokens_in, rows * (32 * LANES) + 32 * LANES)
                dve.wait_ge(dve_row, DR.at(rows, "now"))
                nc.vector.tensor_scalar(XLM[:], XL[:], last_now[:, 0:1], None, ALU.mult).then_inc(dve_row, 1)
                dve.wait_ge(dve_row, DR.at(rows, "xlm"))
                nc.vector.bn_stats(rbn[:], XLM[:]).then_inc(dve_row, 1)
                dve.wait_ge(dve_row, DR.at(rows, "abn"))
                row_chain(0)
                row_chain(1)
                row_chain(2)
            if second is not None:
                residual(*lanes2[0])
                row_chain(3)
                residual(*lanes2[1])
                row_chain(4)
                attention_stats(*lanes2[0], chain=5)
                attention_stats(*lanes2[1], chain=9)
            elif rows is not None:
                for i in range(3, len(CHAIN)):
                    row_chain(i)
            if rows is not None:
                nc.vector.tensor_scalar(rs["mean"][:], rs["sum"][:], 0.5, None, ALU.mult).then_inc(dve_row, 1)
            if second is not None:
                dve.wait_ge(dve_g[g2], DL[g2].at(n2, "bn2", WIDE - 1))
            if zero is not None:
                dve.wait_ge(dve_b[g0], n0 * WIDE + WIDE)
            if zero is not None or second is not None:
                gc, m = (g0, n0) if zero is not None else (g2, n2 + 1)
                of_group = slice(gc * WIDE, (gc + 1) * WIDE)
                kinds = slice(0 if second is not None else 1, 2 if zero is not None else 1)
            for name in CHAIN:
                if zero is not None or second is not None:
                    norm_step(dve, name, {q: sz[q][:, of_group, kinds, :] for q in sz}, lambda i: bn[:, of_group, kinds, :, i],
                              dve_z[gc], lambda step: DZ[gc].at(m, step))
                if first is not None:
                    query_mask(name)
                if rows is None:
                    continue
                if name == "spread":
                    dve.wait_ge(dve_row, DR.at(rows, "mean"))
                    nc.vector.tensor_scalar(rhat[:], XLM[:], rs["mean"][:, 0:1], rs["rstd"][:, 0:1], ALU.subtract, ALU.mult).then_inc(dve_row, 1)
                elif name == "seed":
                    dve.wait_ge(dve_row, DR.at(rows, "hat"))
                    nc.vector.tensor_tensor(rgain[:], rhat[:], row[:, 3, :], ALU.mult).then_inc(dve_row, 1)
                elif name == "times":
                    dve.wait_ge(dve_row, DR.at(rows, "gain"))
                    nc.vector.tensor_tensor(Q2[:], rgain[:], row[:, 4, :], ALU.add).then_inc(dve_row, 1)
                elif name == "e1":
                    dve.wait_ge(dve_row, DR.at(rows, "q"))
                    nc.vector.tensor_reduce(rs["qsum"][:], Q2[:], AX, ALU.add).then_inc(dve_row, 1)
                elif name == "poly":
                    dve.wait_ge(dve_row, DR.at(rows, "qsum"))
                    nc.vector.tensor_scalar(rs["qm"][:], rs["qsum"][:], 0.0, None, ALU.not_equal).then_inc(dve_row, 1)
            if zero is not None:
                nc.vector.tensor_scalar(kflag[g0][:, 0:WIDE, 0:TILES], sz["sum"][:, of_group, 1, :], 0.0, None, ALU.is_equal).then_inc(dve_z[g0], 1)
            if second is not None:
                center(*lanes2[0])
                center(*lanes2[1])
            if rows is not None:
                dve.wait_ge(pe_row, PR.at(rows, "g2"))
                nc.vector.scalar_tensor_tensor(out=G2B[:, :, 0:16], in0=pr2[:, P:2 * P].rearrange("p (u r) -> p u r", r=32)[:, :, 0:16],
                                               scalar=cbias[:, 1:2], in1=abrow[:].rearrange("p (u r) -> p u r", r=32)[:, :, 0:16],
                                               op0=ALU.add, op1=ALU.mult).then_inc(dve_row, 1)
            if second is not None:
                scale(*lanes2[0])
                scale(*lanes2[1])
            if rows is not None:
                dve.wait_ge(dve_row, DR.at(rows, "idflag"))
                dve.wait_ge(pe_row, PR.at(rows, "s2"))
                nc.vector.scalar_tensor_tensor(out=flag2[:], in0=pr[:], scalar=0.0, in1=idflag[:],
                                               op0=ALU.is_equal, op1=ALU.max).then_inc(dve_row, 1)
            if first is not None:
                shifted_scores(*lanes[0])
            if rows is not None:
                dve.wait_ge(pe_row, PR.at(rows, "flag"))
                nc.vector.tensor_reduce(rs["max"][:], pr[:], AX, ALU.max).then_inc(dve_row, 1)
                dve.wait_ge(dve_row, DR.at(rows, "max"))
                nc.vector.tensor_scalar(rs["negmax"][:], rs["max"][:], -1.0, None, ALU.mult).then_inc(dve_row, 1)
            if first is not None:
                shifted_scores(*lanes[1])
                softmax_weights(*lanes[0])
            if rows is not None:
                dve.wait_ge(act_row, AR.at(rows, "exp"))
                nc.vector.reciprocal(rs["rden"][:], rs["den"][:]).then_inc(dve_row, 1)
                dve.wait_ge(dve_row, DR.at(rows, "rden"))
                nc.vector.tensor_tensor(rs["ra"][:], rs["rden"][:], ab01[:, 0:1], ALU.mult).then_inc(dve_row, 1)
                nc.vector.tensor_tensor(rs["rb"][:], rs["rden"][:], ab01[:, 1:2], ALU.mult).then_inc(dve_row, 1)
                dve.wait_ge(pe_row, PR.at(rows, "p2T"))
                kn = kept_now[:].rearrange("p (u t) -> p u t", u=LANES).unsqueeze(2).broadcast_to([P, LANES, 2, TILES])
                for x in range(PAIRS):
                    nc.vector.tensor_tensor(P2T[:, x, :].rearrange("p (u s t) -> p u s t", u=LANES, t=TILES)[:, :, 0:2, :],
                                            pr[:, x * P:(x + 1) * P].rearrange("p (u s t) -> p u s t", u=LANES, t=TILES)[:, :, 0:2, :],
                                            kn, ALU.mult).then_inc(dve_row, 1)
            if first is not None:
                softmax_weights(*lanes[1])
            if rows is not None:
                dve.wait_ge(pe_row, PR.at(rows, "a2"))
                dve.wait_ge(dve_row, DR.at(rows, "rb"))
                nc.vector.tensor_scalar(A2[:], pr2[:, 0:D], rs["ra"][:, 0:1], None, ALU.mult).then_inc(dve_row, 1)
                dve.wait_ge(dve_row, DR.at(rows, "a2a"))
                nc.vector.scalar_tensor_tensor(out=A2[:], in0=pr2[:, D:P], scalar=rs["rb"][:, 0:1], in1=A2[:],
                                               op0=ALU.mult, op1=ALU.add).then_inc(dve_row, 1)
        LAST = PASSES - 1

        def all_halves(half, engine):
            half(engine, zero=(0, 0))
            half(engine, first=(0, 0), zero=(1, 0))
            half(engine, first=(1, 0), second=(0, 0), zero=(0, 1))
            half(engine, first=(0, 1), second=(1, 0), zero=(1, 1))
            half(engine, first=(1, 1), second=(0, 1), zero=(0, 2), rows=0)
            with engine.Fori(1, LAST - 1) as n:
                half(engine, first=(0, n + 1), second=(1, n), zero=(1, n + 1), done=n - 1)
                half(engine, first=(1, n + 1), second=(0, n + 1), zero=(0, n + 2), rows=n)
            half(engine, first=(0, LAST), second=(1, LAST - 1), zero=(1, LAST), done=LAST - 2)
            half(engine, first=(1, LAST), second=(0, LAST), rows=LAST - 1)
            half(engine, second=(1, LAST), done=LAST - 1)
            half(engine, rows=LAST)
            half(engine, done=LAST)

        with nc.Block() as block:
            @block.sync
            def _(sp):
                def prefill(u, n=None):
                    if n is not None:
                        sp.wait_ge(seq_made, n * LANES + u + 1)
                    sp.dma_start(X[u][:], negpos[:]).then_inc(prefilled[u], 16)

                def one_pass(n):
                    for u in LN:
                        prefill(u, n)

                for u in LN:
                    prefill(u)
                one_pass(0)
                with sp.Fori(1, LAST) as n:
                    one_pass(n)

            @block.gpsimd
            def _(pool):
                table_rows = pool.to_reg(NI)
                last_item = pool.alloc_register("last_item")

                def gather(n, u):
                    nc.gpsimd.tensor_copy(idx_now[u][:], idx_all[:, bass.ds(n * (LANES * TILES) + u * TILES, TILES)]).then_inc(idx_copied, 1)
                    pool.wait_ge(idx_copied, n * LANES + u + 1)
                    pool.wait_ge(prefilled[u], n * 16 + 16)
                    pool.reg_sub(last_item, table_rows, 1)
                    for t in range(TILES):
                        nc.gpsimd.indirect_dma_start(
                            out=X[u][:, t, :], out_offset=None, in_=item_emb,
                            in_offset=bass.IndirectOffsetOnAxis(ap=idx_now[u][:, t:t + 1], axis=0),
                            bounds_check=last_item, oob_is_err=False).then_inc(gathered[u], 16)

                def sequence(n, u):
                    g, v = u // WIDE, u % WIDE
                    pool.wait_ge(gathered[u], n * (16 * TILES) + 16 * TILES)
                    if not (isinstance(n, int) and n == 0):
                        pool.wait_ge(pe_g[g], PL[g].at(n - 1, "keyT", v))
                        pool.wait_ge(dve_g[g], DL[g].at(n - 1, "cen1", v))
                    nc.gpsimd.tensor_tensor(SEQ[u][:], X[u][:], negpos[:], ALU.subtract).then_inc(seq_made, 1)

                def one_pass(n, last=False):
                    for u in LN:
                        if u + 1 < LANES:
                            gather(n, u + 1)
                        elif not last:
                            gather(n + 1, 0)
                        sequence(n, u)

                gather(0, 0)
                one_pass(0)
                with pool.Fori(1, LAST) as n:
                    one_pass(n)
                one_pass(LAST, last=True)

            @block.scalar
            def _(act):
                load_ids(act, 0)
                all_halves(half_act, act)

            @block.tensor
            def _(pe):
                all_halves(half_pe, pe)

            @block.vector
            def _(dve):
                all_halves(half_dve, dve)


        CHUNKS = PASSES // TILES
        assert PASSES % TILES == 0 and CHUNKS <= LANES
        CH = range(CHUNKS)
        dve_end = sem("dve_end")
        act_end = sem("act_end")
        pe_end = sem("pe_end")

        def chunks(*names):
            return [(name, c) for name in names for c in CH]

        DE = Steps(dve_end, chunks("bnb") + norm_steps("_b") + chunks("cenb", "hatb", "z", "zm", "bnc")
                   + norm_steps("_c") + chunks("cenc", "hatc") + [(q, k) for k in range(2 * CHUNKS) for q in ("hi", "lo")])
        AE = Steps(act_end, chunks("yT", "hT") + [("fin", k) for k in range(2 * CHUNKS)])
        PE = Steps(pe_end, chunks("yT", "h", "o", "z") + [("fin", k) for k in range(2 * CHUNKS)])
        with nc.Block() as block:
            @block.vector
            def _(dve):
                def rows_norm(k, src):
                    for c in CH:
                        if k == "c":
                            dve.wait_ge(dve_end, DE.at(0, "zm", c))
                        for t in range(TILES):
                            m = nc.vector.bn_stats(bn[:, c, 0, t, :], src[c][:, t, :])
                        m.then_inc(dve_end, 1)
                    dve.wait_ge(dve_end, DE.at(0, "bn" + k, CHUNKS - 1))
                    for name in CHAIN:
                        norm_step(dve, name, {q: sz[q][:, 0:CHUNKS, 0, :] for q in sz}, lambda i: bn[:, 0:CHUNKS, 0, :, i],
                                  dve_end, lambda step: DE.at(0, step + "_" + k))
                    for c in CH:
                        nc.vector.scalar_tensor_tensor(out=XN[c][:], in0=bc(sz["sum"][:, c, 0, :]), scalar=-0.5, in1=src[c][:],
                                                       op0=ALU.mult, op1=ALU.add).then_inc(dve_end, 1)
                    dve.wait_ge(dve_end, DE.at(0, "rstd_" + k))
                    for c in CH:
                        dve.wait_ge(dve_end, DE.at(0, "cen" + k, c))
                        if k == "b":
                            nc.vector.tensor_tensor(XN[c][:], XN[c][:], bc(sz["rstd"][:, c, 0, :]), ALU.mult).then_inc(dve_end, 1)
                        else:
                            nc.vector.tensor_tensor(BLK[c][:].rearrange("p t (k f) -> p t k f", f=D),
                                                    XN[c][:].unsqueeze(2).broadcast_to([P, TILES, 2, D]),
                                                    bc(sz["rstd"][:, c, 0, :]).unsqueeze(2).broadcast_to([P, TILES, 2, D]),
                                                    ALU.mult).then_inc(dve_end, 1)

                rows_norm("b", [X2[:, c * TILES:(c + 1) * TILES, :] for c in CH])
                for c in CH:
                    dve.wait_ge(pe_end, PE.at(0, "o", c))
                    nc.vector.scalar_tensor_tensor(out=S2T[c][:], in0=pl[c][:], scalar=col[:, 11:12], in1=QT[c][:],
                                                   op0=ALU.add, op1=ALU.add).then_inc(dve_end, 1)
                for c in CH:
                    dve.wait_ge(pe_end, PE.at(0, "z", c))
                    nc.vector.tensor_tensor(SEQ[c][:], pl[c][:].rearrange("p (t f) -> p t f", f=D),
                                            bc(last_all[:, c * TILES:(c + 1) * TILES]), ALU.mult).then_inc(dve_end, 1)
                rows_norm("c", [SEQ[c] for c in CH])
                for k in range(2 * CHUNKS):
                    c, half = k % CHUNKS, k // CHUNKS
                    dve.wait_ge(act_end, AE.at(0, "fin", k))
                    final = (QT if half == 0 else KT)[c]
                    for part, tile in (("hi", hid_hi), ("lo", hid_lo)):
                        for i in range(4):
                            n = c * TILES + half * 4 + i
                            dst = tile[:, n * BATCH:(n + 1) * BATCH].rearrange("p (u t s) -> p u s t", u=LANES, s=2)
                            src = final[:, i * P:(i + 1) * P].rearrange("p (u s t) -> p u s t", u=LANES, t=TILES)[:, :, 0:2, :]
                            if part == "hi":
                                m = nc.vector.tensor_copy(dst, src)
                            else:
                                high = hid_hi[:, n * BATCH:(n + 1) * BATCH].rearrange("p (u t s) -> p u s t", u=LANES, s=2).bitcast(F32)
                                m = nc.vector.tensor_tensor(dst, src, high, ALU.subtract)
                        m.then_inc(dve_end, 1)
                        if part == "hi":
                            dve.wait_ge(dve_end, DE.at(0, "hi", k))

            @block.tensor
            def _(pe):
                for c in CH:
                    pe.wait_ge(dve_end, DE.at(0, "hatb", c))
                    turn(pl[c], XN[c]).then_inc(pe_end, 1)
                for c in CH:
                    pe.wait_ge(act_end, AE.at(0, "yT", c))
                    nc.tensor.matmul(pl[c][:], bd["w1b"][:], QT[c][:], start=True, stop=True).then_inc(pe_end, 1)
                for c in CH:
                    pe.wait_ge(act_end, AE.at(0, "hT", c))
                    nc.tensor.matmul(pl[c][:], bd["w2b"][:], KT[c][:], start=True, stop=True).then_inc(pe_end, 1)
                for c in CH:
                    pe.wait_ge(dve_end, DE.at(0, "z", c))
                    for x in range(PAIRS):
                        m = nc.tensor.transpose(pl[c][:, x * P:(x + 1) * P], S2T[c][:, x * P:(x + 1) * P], ident[:])
                    m.then_inc(pe_end, 1)
                for k in range(2 * CHUNKS):
                    c, half = k % CHUNKS, k // CHUNKS
                    pe.wait_ge(dve_end, DE.at(0, "hatc", c))
                    if half:
                        pe.wait_ge(act_end, AE.at(0, "fin", c))
                    for i in range(4):
                        m = nc.tensor.transpose(pl[c][:, i * P:(i + 1) * P], BLK[c][:, 4 * half + i, :], ident[:])
                    m.then_inc(pe_end, 1)

            @block.scalar
            def _(act):
                for c in CH:
                    act.wait_ge(pe_end, PE.at(0, "yT", c))
                    nc.scalar.activation(QT[c][:], pl[c][:], ACT.Identity, scale=col[:, 9:10], bias=col[:, 10:11]).then_inc(act_end, 1)
                for c in CH:
                    act.wait_ge(pe_end, PE.at(0, "h", c))
                    nc.scalar.activation(KT[c][:], pl[c][:], ACT.Relu, bias=col[:, 7:8]).then_inc(act_end, 1)
                for k in range(2 * CHUNKS):
                    c, half = k % CHUNKS, k // CHUNKS
                    act.wait_ge(pe_end, PE.at(0, "fin", k))
                    nc.scalar.activation((QT if half == 0 else KT)[c][:], pl[c][:], ACT.Identity,
                                         scale=col[:, 12:13], bias=col[:, 13:14]).then_inc(act_end, 1)

        ph1.close()
        with ExitStack() as ph2:
            def sb2(name, shape, dt=F32):
                return ph2.enter_context(nc.sbuf_tensor("s_" + name, shape, dt))

            embT = sb2("embT", [P, NO], F32R)
            ident2 = sb2("ident2", [P, P])
            raw = [sb2(f"raw{b}", [ER, EL, D]) for b in range(EBUFS)]
            split = [sb2(f"split{b}", [ER, EL, 2 * D]) for b in range(EBUFS)]
            hi_now = sb2("hi_now", [P, P], F32R)
            lo_now = sb2("lo_now", [P, P], F32R)
            outs = [sb2(f"outs{b}", [P, DSL * NSL]) for b in range(SBUFS)]
            ps = [ph2.enter_context(nc.psum_tensor(f"ps{b}", [P, 512], F32)) for b in range(DSL)]

            id_in = sem("id_in")
            raw_in = [sem(f"raw_in{b}") for b in range(EBUFS)]
            split_hi = sem("split_hi")
            split_lo = [sem(f"split_lo{b}") for b in range(EBUFS)]
            turned = [sem(f"turned{b}") for b in range(EBUFS)]
            emb_put = [sem(f"emb_put{b}") for b in range(EBUFS)]
            emb_rows = out_emb.rearrange("(n b a p) f -> n b p a f", b=EBUFS, a=EL, p=ER)
            NE = NO // (ER * EL * EBUFS)
            assert NO % (ER * EL * EBUFS) == 0
            with nc.Block() as block:
                @block.sync
                def _(sp):
                    sp.dma_start(ident2[:], const[:, 0:P]).then_inc(id_in, 16)
                    with sp.Fori(0, NE) as n:
                        for b in range(EBUFS):
                            sp.wait_ge(split_lo[b], n)
                            sp.dma_start(raw[b][:], emb_rows[bass.ds(n, 1), b].rearrange("n p a f -> (n p) a f")).then_inc(raw_in[b], 16)

                @block.vector
                def _(dve):
                    with dve.Fori(0, NE) as n:
                        for b in range(EBUFS):
                            dve.wait_ge(raw_in[b], n * 16 + 16)
                            dve.wait_ge(turned[b], n)
                            nc.vector.tensor_copy(split[b][:, :, 0:D].bitcast(F32R), raw[b][:]).then_inc(split_hi, 1)
                            dve.wait_ge(split_hi, n * EBUFS + b + 1)
                            nc.vector.tensor_tensor(split[b][:, :, D:2 * D], raw[b][:], split[b][:, :, 0:D], ALU.subtract).then_inc(split_lo[b], 1)

                @block.tensor
                def _(pe):
                    pe.wait_ge(id_in, 16)
                    with pe.Fori(0, NE) as n:
                        for b in range(EBUFS):
                            pe.wait_ge(split_lo[b], n + 1)
                            pe.wait_ge(emb_put[b], n)
                            for a in range(EL):
                                m = nc.tensor.transpose(ps[b][:, a * ER:(a + 1) * ER], split[b][:, a, :], ident2[0:ER, 0:ER])
                            m.then_inc(turned[b], 1)

                @block.scalar
                def _(act):
                    with act.Fori(0, NE) as n:
                        for b in range(EBUFS):
                            act.wait_ge(turned[b], n + 1)
                            nc.scalar.activation(embT[:, bass.ds(n * (EBUFS * EL * ER) + b * EL * ER, EL * ER)],
                                                 ps[b][:, 0:EL * ER], ACT.Copy).then_inc(emb_put[b], 1)

            ROUNDS = STORES // SBUFS
            now_hi = sem("now_hi")
            now_lo = sem("now_lo")
            product = sem("product")
            left = [sem(f"left{b}") for b in range(DSL)]
            stored = [sem(f"stored{b}") for b in range(SBUFS)]
            on_act = [k for k in range(SBUFS * DSL) if k % DSL % 2 == 0]
            on_dve = [k for k in range(SBUFS * DSL) if k % DSL % 2 == 1]
            out_g = out.rearrange("(g p) c -> g p c", p=P)
            with nc.Block() as block:
                @block.tensor
                def _(pe):
                    with pe.Fori(0, GROUPS) as g:
                        with pe.Fori(0, ROUNDS) as r:
                            q = g * ROUNDS + r
                            for k in range(SBUFS * DSL):
                                if k == 0:
                                    pe.wait_ge(now_lo, g + 1)
                                pe.wait_ge(left[k % DSL], q * SBUFS + k // DSL)
                                e = embT[:, bass.ds(r * (SBUFS * DSL * NSL) + k * NSL, NSL)]
                                nc.tensor.matmul(ps[k % DSL][:, 0:NSL], hi_now[:], e, start=True, stop=False)
                                nc.tensor.matmul(ps[k % DSL][:, 0:NSL], lo_now[:], e, start=False, stop=True).then_inc(product, 1)

                @block.scalar
                def _(act):
                    with act.Fori(0, GROUPS) as g:
                        with act.Fori(0, ROUNDS) as r:
                            q = g * ROUNDS + r
                            for k in on_act:
                                if k % DSL == 0:
                                    act.wait_ge(stored[k // DSL], q * 16)
                                act.wait_ge(product, q * (SBUFS * DSL) + k + 1)
                                nc.scalar.activation(outs[k // DSL][:, k % DSL * NSL:(k % DSL + 1) * NSL], ps[k % DSL][:, 0:NSL],
                                                     ACT.Copy).then_inc(left[k % DSL], 1)

                @block.vector
                def _(dve):
                    with dve.Fori(0, GROUPS) as g:
                        dve.wait_ge(product, g * (SBUFS * DSL * ROUNDS))
                        nc.vector.tensor_copy(hi_now[:], hid_hi[:, bass.ds(g * P, P)].bitcast(F32)).then_inc(now_hi, 1)
                        nc.vector.tensor_copy(lo_now[:], hid_lo[:, bass.ds(g * P, P)].bitcast(F32)).then_inc(now_lo, 1)
                        with dve.Fori(0, ROUNDS) as r:
                            q = g * ROUNDS + r
                            for k in on_dve:
                                if k % DSL == 1:
                                    dve.wait_ge(stored[k // DSL], q * 16)
                                dve.wait_ge(product, q * (SBUFS * DSL) + k + 1)
                                nc.vector.tensor_copy(outs[k // DSL][:, k % DSL * NSL:(k % DSL + 1) * NSL],
                                                      ps[k % DSL][:, 0:NSL]).then_inc(left[k % DSL], 1)

                @block.sync
                def _(sp):
                    with sp.Fori(0, GROUPS) as g:
                        with sp.Fori(0, ROUNDS) as r:
                            q = g * ROUNDS + r
                            for b in range(SBUFS):
                                for k in range(DSL):
                                    sp.wait_ge(left[k], q * SBUFS + b + 1)
                                sp.dma_start(out_g[bass.ds(g, 1), :, bass.ds(r * (SBUFS * DSL * NSL) + b * DSL * NSL, DSL * NSL)].rearrange("g p c -> (g p) c"),
                                             outs[b][:]).then_inc(stored[b], 16)
                    for b in range(SBUFS):
                        sp.wait_ge(stored[b], 16 * GROUPS * ROUNDS)


def _constants():
    import numpy as np

    p = np.arange(P)
    half, i = p // 64, p % 64
    ident = np.eye(P)
    key = np.arange(512)
    later = (key[None, :] % 64 > i[:, None])
    r = p % 32
    col_t = 2 * (key // P) + (key % P) // 64
    ksel = (r[:, None] == col_t[None, :]) & (r[:, None] < 8)
    lane, rs, rt = p // 32, (p % 32) // 8, p % 8
    used = (p % 32) < 16
    rsel = (lane[:, None] == lane[None, :]) & (r[:, None] == 16 + (rt % 2)[None, :]) & used[None, :]
    same = (rt[:, None] // 2 == key[None, :] // P) & (rs[:, None] == (key[None, :] % P) // 64)
    other = ~same & used[:, None]
    abrow = (half[:, None] == (rt % 2)[None, :]) & used[None, :]
    ab01 = (rt[:, None] % 2 == np.arange(2)[None, :])
    parts = [ident, MASKED * ident, later, MASKED * ksel, MASKED * rsel, other, abrow, ab01]
    return np.concatenate([np.asarray(x, np.float32) for x in parts], axis=1)


def kernel(**inputs):
    import numpy as np
    import concourse.bacc as bacc
    from concourse.bass_utils import run_bass_kernel_spmd

    x = {k.replace("L0_rec_", ""): np.asarray(v) for k, v in inputs.items()}
    two = lambda v: np.concatenate([v, v])
    cols = np.stack([two(v) for v in (x["ln1_g"][0], x["ln1_b"][0], x["ln2_g"][0], x["ln2_b"][0], x["b1"][0],
                                      x["bq"][0], x["bq"][1], x["b1"][1], x["b2"][0], x["ln2_g"][1], x["ln2_b"][1],
                                      x["b2"][1], x["lnf_g"], x["lnf_b"])], axis=1)
    rows = np.stack([x["ln1_g"][0], x["ln1_b"][0], x["bv"][0], x["ln1_g"][1], x["ln1_b"][1], x["bv"][1]])
    arrays = {
        "ids": x["r_input_ids"], "item_emb": x["item_emb"], "pos_emb": x["pos_emb"],
        "wqT": x["Wq"].transpose(0, 2, 1), "wkT": x["Wk"].transpose(0, 2, 1), "wv": x["Wv"], "w1": x["W1"], "w2": x["W2"],
        "cols": cols, "rows": rows, "out_emb": x["out_item_emb"], "const": _constants(),
    }
    arrays = {k: np.ascontiguousarray(v) for k, v in arrays.items()}
    nc = bacc.Bacc("TRN2", target_bir_lowering=False, num_devices=1)
    aps = [nc.dram_tensor(f"in_{k}", v.shape, mybir.dt.from_np(v.dtype), kind="ExternalInput").ap() for k, v in arrays.items()]
    shape = (x["r_input_ids"].shape[0], x["out_item_emb"].shape[0])
    out = nc.dram_tensor("out_scores", shape, F32, kind="ExternalOutput").ap()
    recommender(nc, *aps, out)
    r = run_bass_kernel_spmd(nc, [{f"in_{k}": v for k, v in arrays.items()}], core_ids=[0])
    return r.results[0]["out_scores"]
```
